# Optimizing a Trainium2 kernel written in Bass

```python
import numpy as np
import jax
import jax.numpy as jnp

def _softmax(x, axis=-1):
    return jax.nn.softmax(x, axis=axis)

def _gelu(x):
    return jax.nn.gelu(x, approximate=True)

def _silu(x):
    return jax.nn.silu(x)

def _sigmoid(x):
    return jax.nn.sigmoid(x)

def _layernorm(x, axis=-1, eps=1e-05):
    m = jnp.mean(x, axis=axis, keepdims=True)
    v = jnp.var(x, axis=axis, keepdims=True)
    return (x - m) / jnp.sqrt(v + eps)

def _scatter_add(tgt, idx, src, axis=0):
    return tgt.at[idx].add(src)

def _segment_sum(src, seg, n):
    return jax.ops.segment_sum(src, seg, n)
kernel_name = 'mk_lm_tower_d2_tok_ids512_r4_d45d56'

def setup_inputs(seed: int=0):
    np.random.seed(seed)
    _w = jnp.asarray

    def _rec_inputs():
        import jax
        import jax.numpy as jnp
        _rk = jax.random.key(seed)
        x = jax.random.randint(jax.random.fold_in(_rk, 1), (16, 128), 0, 30521, jnp.int32)
        return x
    x = _rec_inputs()

    def _L0_tok_setup():
        import jax, jax.numpy as jnp
        import numpy as np
        import math
        V, D, H, N, DFF = (30522, 128, 8, 4, 512)
        DH = D // H

        def sinusoidal_pe(L, d):
            pos = jnp.arange(L, dtype=jnp.float32)[:, None]
            div = jnp.exp(jnp.arange(0, d, 2, dtype=jnp.float32) * (-math.log(10000.0) / d))
            pe = jnp.zeros((L, d), dtype=jnp.float32)
            pe = pe.at[:, 0::2].set(jnp.sin(pos * div))
            pe = pe.at[:, 1::2].set(jnp.cos(pos * div))
            return pe

        def layer_norm(x, g, b, eps=1e-05):
            mu = jnp.mean(x, axis=-1, keepdims=True)
            var = jnp.mean(jnp.square(x - mu), axis=-1, keepdims=True)
            return (x - mu) * jax.lax.rsqrt(var + eps) * g + b
        key = jax.random.key(seed)
        ks = jax.random.split(key, 12)
        s = 0.02
        return {'x': jax.random.randint(ks[0], (16, 128), 0, V), 'E': jax.random.normal(ks[1], (V, D), jnp.float32) * s, 'Wq': jax.random.normal(ks[2], (D, DH), jnp.float32) * s, 'bq': jnp.zeros((DH,), jnp.float32), 'Wk': jax.random.normal(ks[3], (D, DH), jnp.float32) * s, 'bk': jnp.zeros((DH,), jnp.float32), 'Wv': jax.random.normal(ks[4], (D, DH), jnp.float32) * s, 'bv': jnp.zeros((DH,), jnp.float32), 'Wo': jax.random.normal(ks[5], (D, D), jnp.float32) * s, 'bo': jnp.zeros((D,), jnp.float32), 'ln_g': jnp.ones((D,), jnp.float32), 'ln_b': jnp.zeros((D,), jnp.float32), 'W1': jax.random.normal(ks[6], (D, DFF), jnp.float32) * s, 'b1': jnp.zeros((DFF,), jnp.float32), 'W2': jax.random.normal(ks[7], (DFF, D), jnp.float32) * s, 'b2': jnp.zeros((D,), jnp.float32)}
    _L0_tok_all = _L0_tok_setup()
    _L0_tok_in = {k: v for k, v in _L0_tok_all.items() if k in ('E', 'Wq', 'bq', 'Wk', 'bk', 'Wv', 'bv', 'Wo', 'bo', 'ln_g', 'ln_b', 'W1', 'b1', 'W2', 'b2')}
    del _L0_tok_all

    def _L0_attn_setup():
        import jax, jax.numpy as jnp
        import numpy as np
        B, S, IN, HID, H, D, FF = (8, 512, 128, 128, 8, 64, 512)
        EPS = 1e-05

        def layer_norm(x, g, b):
            m = jnp.mean(x, axis=-1, keepdims=True)
            v = jnp.mean(jnp.square(x - m), axis=-1, keepdims=True)
            return (x - m) * jax.lax.rsqrt(v + EPS) * g + b

        def delta_rule(q, k, v, beta):

            def step(W, inp):
                qt, kt, vt, bt = inp
                wk = jnp.einsum('bhde,bhe->bhd', W, kt)
                v_new = bt * (vt - wk)
                W = W + jnp.einsum('bhd,bhe->bhde', v_new, kt)
                out = jnp.einsum('bhde,bhe->bhd', W, qt)
                return (W, out)
            bsz = q.shape[1]
            W0 = jnp.zeros((bsz, H, D, D), dtype=q.dtype)
            _, outs = jax.lax.scan(step, W0, (q, k, v, beta))
            return outs

        def fast_ff(x, ln_g, ln_b, slow_w, out_w):
            slen, bsz, _ = x.shape
            h = layer_norm(x, ln_g, ln_b)
            qkvb = jnp.einsum('sbi,oi->sbo', h, slow_w).reshape(slen, bsz, H, 3 * D + 1)
            q, k, v, beta = jnp.split(qkvb, [D, 2 * D, 3 * D], axis=-1)
            q = jax.nn.softmax(q, axis=-1)
            k = jax.nn.softmax(k, axis=-1)
            beta = jax.nn.sigmoid(beta)
            attn = delta_rule(q, k, v, beta)
            o = jnp.einsum('sbd,od->sbo', attn.reshape(slen, bsz, H * D), out_w)
            return x + o

        def ffn(x, ln_g, ln_b, w1, b1, w2, b2):
            h = layer_norm(x, ln_g, ln_b)
            h = jax.nn.relu(jnp.einsum('sbi,fi->sbf', h, w1) + b1)
            return x + jnp.einsum('sbf,of->sbo', h, w2) + b2
        key = jax.random.key(seed)
        ks = jax.random.split(key, 8)
        s = 0.02
        return {'x': jax.random.normal(ks[0], (B, S, IN), jnp.float32), 'ip_w': s * jax.random.normal(ks[1], (HID, IN), jnp.float32), 'ip_b': jnp.zeros((HID,), jnp.float32), 'fw_ln_g': jnp.ones((2, HID), jnp.float32), 'fw_ln_b': jnp.zeros((2, HID), jnp.float32), 'fw_slow_w': s * jax.random.normal(ks[2], (2, H * (3 * D + 1), HID), jnp.float32), 'fw_out_w': s * jax.random.normal(ks[3], (2, HID, H * D), jnp.float32), 'ff_ln_g': jnp.ones((HID,), jnp.float32), 'ff_ln_b': jnp.zeros((HID,), jnp.float32), 'ff_w1': s * jax.random.normal(ks[4], (FF, HID), jnp.float32), 'ff_b1': jnp.zeros((FF,), jnp.float32), 'ff_w2': s * jax.random.normal(ks[5], (HID, FF), jnp.float32), 'ff_b2': jnp.zeros((HID,), jnp.float32)}
    _L0_attn_all = _L0_attn_setup()
    _L0_attn_in = {k: v for k, v in _L0_attn_all.items() if k in ('ip_w', 'ip_b', 'fw_ln_g', 'fw_ln_b', 'fw_slow_w', 'fw_out_w', 'ff_ln_g', 'ff_ln_b', 'ff_w1', 'ff_b1', 'ff_w2', 'ff_b2')}
    del _L0_attn_all

    def _L0_ffn_setup():
        import jax, jax.numpy as jnp
        import numpy as np
        B, S, D = (4, 256, 128)
        E = 16
        DH = 4 * D
        DS = 2 * D
        TOP_K = 2
        TEMP = 0.7
        SHARED_SCALE = 0.25
        EPS = 1e-05

        def layer_norm(x, g, b):
            mu = jnp.mean(x, axis=-1, keepdims=True)
            var = jnp.mean(jnp.square(x - mu), axis=-1, keepdims=True)
            return (x - mu) * jax.lax.rsqrt(var + EPS) * g + b
        key = jax.random.key(seed)
        ks = jax.random.split(key, 12)
        s = 0.02
        return {'x': jax.random.normal(ks[0], (B, S, D), jnp.float32), 'ln_in_g': jnp.ones((D,), jnp.float32), 'ln_in_b': jnp.zeros((D,), jnp.float32), 'router_w': jax.random.normal(ks[1], (D, E), jnp.float32) * s, 'router_b': jnp.zeros((E,), jnp.float32), 'ew1': jax.random.normal(ks[2], (E, D, DH), jnp.float32) * s, 'eb1': jnp.zeros((E, DH), jnp.float32), 'ew2': jax.random.normal(ks[3], (E, DH, D), jnp.float32) * s, 'eb2': jnp.zeros((E, D), jnp.float32), 'sw1': jax.random.normal(ks[4], (D, DS), jnp.float32) * s, 'sb1': jnp.zeros((DS,), jnp.float32), 'sw2': jax.random.normal(ks[5], (DS, D), jnp.float32) * s, 'sb2': jnp.zeros((D,), jnp.float32), 'ff_ln_g': jnp.ones((D,), jnp.float32), 'ff_ln_b': jnp.zeros((D,), jnp.float32), 'ff_w1': jax.random.normal(ks[6], (D, DH), jnp.float32) * s, 'ff_b1': jnp.zeros((DH,), jnp.float32), 'ff_w2': jax.random.normal(ks[7], (DH, D), jnp.float32) * s, 'ff_b2': jnp.zeros((D,), jnp.float32)}
    _L0_ffn_all = _L0_ffn_setup()
    _L0_ffn_in = {k: v for k, v in _L0_ffn_all.items() if k in ('ln_in_g', 'ln_in_b', 'router_w', 'router_b', 'ew1', 'eb1', 'ew2', 'eb2', 'sw1', 'sb1', 'sw2', 'sb2', 'ff_ln_g', 'ff_ln_b', 'ff_w1', 'ff_b1', 'ff_w2', 'ff_b2')}
    del _L0_ffn_all

    def _L1_attn_setup():
        import jax, jax.numpy as jnp
        import numpy as np
        from jax import lax
        B_, L_, D_ = (4, 128, 128)
        HID, H2 = (128, 64)
        NL, DST, DCV, DIN, DTR = (3, 16, 4, 256, 32)

        def _silu(x):
            return x * jax.nn.sigmoid(x)

        def _layernorm(x, g, b):
            m = x.mean(-1, keepdims=True)
            v = x.var(-1, keepdims=True)
            return (x - m) / jnp.sqrt(v + 1e-05) * g + b

        def _mamba(x, wi, cw, cb, xpw, dw, db, Alog, Dp, wo):
            Bsz, Ls, _ = x.shape
            xz = jnp.einsum('bld,ed->ble', x, wi)
            xin, z = jnp.split(xz, 2, axis=-1)
            xpad = jnp.pad(xin, ((0, 0), (DCV - 1, 0), (0, 0)))
            u = cb + sum((xpad[:, k:k + Ls, :] * cw[:, k] for k in range(DCV)))
            u = _silu(u)
            xdbl = jnp.einsum('blc,ec->ble', u, xpw)
            dt_in = xdbl[..., :DTR]
            Bc = xdbl[..., DTR:DTR + DST]
            Cc = xdbl[..., DTR + DST:]
            dt = jax.nn.softplus(jnp.einsum('blr,cr->blc', dt_in, dw) + db)
            A = -jnp.exp(Alog)

            def step(h, inp):
                dt_t, B_t, C_t, u_t = inp
                dA = jnp.exp(dt_t[..., None] * A)
                h = dA * h + (dt_t * u_t)[..., None] * B_t[:, None, :]
                y = jnp.einsum('bcn,bn->bc', h, C_t)
                return (h, y)
            h0 = jnp.zeros((Bsz, DIN, DST), x.dtype)
            _, ys = lax.scan(step, h0, (dt.transpose(1, 0, 2), Bc.transpose(1, 0, 2), Cc.transpose(1, 0, 2), u.transpose(1, 0, 2)))
            y = ys.transpose(1, 0, 2) + u * Dp
            y = y * _silu(z)
            return jnp.einsum('blc,dc->bld', y, wo)

        def _lstm_dir(x, wih, whh, bih, bhh, reverse):
            Bsz = x.shape[0]

            def step(carry, xt):
                h, c = carry
                g = xt @ wih.T + h @ whh.T + bih + bhh
                i, f, gg, o = jnp.split(g, 4, axis=-1)
                c = jax.nn.sigmoid(f) * c + jax.nn.sigmoid(i) * jnp.tanh(gg)
                h = jax.nn.sigmoid(o) * jnp.tanh(c)
                return ((h, c), h)
            init = (jnp.zeros((Bsz, H2), x.dtype), jnp.zeros((Bsz, H2), x.dtype))
            _, hs = lax.scan(step, init, x.transpose(1, 0, 2), reverse=reverse)
            return hs.transpose(1, 0, 2)
        key = jax.random.key(seed)
        ks = jax.random.split(key, 16)
        rn = lambda k, s, sc=0.02: jax.random.normal(k, s, jnp.float32) * sc
        inp = {}
        inp['x'] = jax.random.normal(ks[0], (B_, L_, D_), jnp.float32)
        inp['in_proj_w'] = rn(ks[1], (NL, 2 * DIN, D_))
        inp['conv_w'] = rn(ks[2], (NL, DIN, DCV), 0.2)
        inp['conv_b'] = jnp.zeros((NL, DIN), jnp.float32)
        inp['x_proj_w'] = rn(ks[3], (NL, DTR + 2 * DST, DIN))
        inp['dt_proj_w'] = rn(ks[4], (NL, DIN, DTR), 0.1)
        inp['dt_proj_b'] = jnp.full((NL, DIN), -4.0, jnp.float32)
        inp['A_log'] = jnp.log(jnp.broadcast_to(jnp.arange(1, DST + 1, dtype=jnp.float32), (NL, DIN, DST)))
        inp['D_param'] = jnp.ones((NL, DIN), jnp.float32)
        inp['out_proj_w'] = rn(ks[5], (NL, D_, DIN))
        inp['ln_g'] = jnp.ones((NL, D_), jnp.float32)
        inp['ln_b'] = jnp.zeros((NL, D_), jnp.float32)
        inp['lstm_w_ih'] = rn(ks[6], (2, 4 * H2, D_), 0.05)
        inp['lstm_w_hh'] = rn(ks[7], (2, 4 * H2, H2), 0.05)
        inp['lstm_b_ih'] = jnp.zeros((2, 4 * H2), jnp.float32)
        inp['lstm_b_hh'] = jnp.zeros((2, 4 * H2), jnp.float32)
        inp['fusion_w'] = rn(ks[8], (HID, D_ + HID), 0.02)
        inp['fusion_b'] = jnp.zeros((HID,), jnp.float32)
        return inp
    _L1_attn_all = _L1_attn_setup()
    _L1_attn_in = {k: v for k, v in _L1_attn_all.items() if k in ('in_proj_w', 'conv_w', 'conv_b', 'x_proj_w', 'dt_proj_w', 'dt_proj_b', 'A_log', 'D_param', 'out_proj_w', 'ln_g', 'ln_b', 'lstm_w_ih', 'lstm_w_hh', 'lstm_b_ih', 'lstm_b_hh', 'fusion_w', 'fusion_b')}
    del _L1_attn_all

    def _L1_ffn_setup():
        import jax, jax.numpy as jnp
        import numpy as np
        E = 64
        K = 2
        D = 128
        H = 64
        NSH = 2
        ROUTE_SCALE = 2.5
        CAP = 256
        STD = 0.02
        key = jax.random.key(seed)
        ks = jax.random.split(key, 8)
        x = jax.random.normal(ks[0], (4, 512, D), dtype=jnp.float32)
        gate_w = jax.random.normal(ks[1], (E, D), dtype=jnp.float32) * STD
        w1 = jax.random.normal(ks[2], (E, D, H), dtype=jnp.float32) * STD
        w3 = jax.random.normal(ks[3], (E, D, H), dtype=jnp.float32) * STD
        w2 = jax.random.normal(ks[4], (E, H, D), dtype=jnp.float32) * STD
        sw1 = jax.random.normal(ks[5], (D, H * NSH), dtype=jnp.float32) * STD
        sw3 = jax.random.normal(ks[6], (D, H * NSH), dtype=jnp.float32) * STD
        sw2 = jax.random.normal(ks[7], (H * NSH, D), dtype=jnp.float32) * STD
        return {'x': x, 'gate_w': gate_w, 'w1': w1, 'w3': w3, 'w2': w2, 'sw1': sw1, 'sw3': sw3, 'sw2': sw2}
    _L1_ffn_all = _L1_ffn_setup()
    _L1_ffn_in = {k: v for k, v in _L1_ffn_all.items() if k in ('gate_w', 'w1', 'w3', 'w2', 'sw1', 'sw3', 'sw2')}
    del _L1_ffn_all
    return {'x': x, 'L0_tok_E': _L0_tok_in['E'], 'L0_tok_Wq': _L0_tok_in['Wq'], 'L0_tok_bq': _L0_tok_in['bq'], 'L0_tok_Wk': _L0_tok_in['Wk'], 'L0_tok_bk': _L0_tok_in['bk'], 'L0_tok_Wv': _L0_tok_in['Wv'], 'L0_tok_bv': _L0_tok_in['bv'], 'L0_tok_Wo': _L0_tok_in['Wo'], 'L0_tok_bo': _L0_tok_in['bo'], 'L0_tok_ln_g': _L0_tok_in['ln_g'], 'L0_tok_ln_b': _L0_tok_in['ln_b'], 'L0_tok_W1': _L0_tok_in['W1'], 'L0_tok_b1': _L0_tok_in['b1'], 'L0_tok_W2': _L0_tok_in['W2'], 'L0_tok_b2': _L0_tok_in['b2'], 'L0_attn_ip_w': _L0_attn_in['ip_w'], 'L0_attn_ip_b': _L0_attn_in['ip_b'], 'L0_attn_fw_ln_g': _L0_attn_in['fw_ln_g'], 'L0_attn_fw_ln_b': _L0_attn_in['fw_ln_b'], 'L0_attn_fw_slow_w': _L0_attn_in['fw_slow_w'], 'L0_attn_fw_out_w': _L0_attn_in['fw_out_w'], 'L0_attn_ff_ln_g': _L0_attn_in['ff_ln_g'], 'L0_attn_ff_ln_b': _L0_attn_in['ff_ln_b'], 'L0_attn_ff_w1': _L0_attn_in['ff_w1'], 'L0_attn_ff_b1': _L0_attn_in['ff_b1'], 'L0_attn_ff_w2': _L0_attn_in['ff_w2'], 'L0_attn_ff_b2': _L0_attn_in['ff_b2'], 'L0_ffn_ln_in_g': _L0_ffn_in['ln_in_g'], 'L0_ffn_ln_in_b': _L0_ffn_in['ln_in_b'], 'L0_ffn_router_w': _L0_ffn_in['router_w'], 'L0_ffn_router_b': _L0_ffn_in['router_b'], 'L0_ffn_ew1': _L0_ffn_in['ew1'], 'L0_ffn_eb1': _L0_ffn_in['eb1'], 'L0_ffn_ew2': _L0_ffn_in['ew2'], 'L0_ffn_eb2': _L0_ffn_in['eb2'], 'L0_ffn_sw1': _L0_ffn_in['sw1'], 'L0_ffn_sb1': _L0_ffn_in['sb1'], 'L0_ffn_sw2': _L0_ffn_in['sw2'], 'L0_ffn_sb2': _L0_ffn_in['sb2'], 'L0_ffn_ff_ln_g': _L0_ffn_in['ff_ln_g'], 'L0_ffn_ff_ln_b': _L0_ffn_in['ff_ln_b'], 'L0_ffn_ff_w1': _L0_ffn_in['ff_w1'], 'L0_ffn_ff_b1': _L0_ffn_in['ff_b1'], 'L0_ffn_ff_w2': _L0_ffn_in['ff_w2'], 'L0_ffn_ff_b2': _L0_ffn_in['ff_b2'], 'L1_attn_in_proj_w': _L1_attn_in['in_proj_w'], 'L1_attn_conv_w': _L1_attn_in['conv_w'], 'L1_attn_conv_b': _L1_attn_in['conv_b'], 'L1_attn_x_proj_w': _L1_attn_in['x_proj_w'], 'L1_attn_dt_proj_w': _L1_attn_in['dt_proj_w'], 'L1_attn_dt_proj_b': _L1_attn_in['dt_proj_b'], 'L1_attn_A_log': _L1_attn_in['A_log'], 'L1_attn_D_param': _L1_attn_in['D_param'], 'L1_attn_out_proj_w': _L1_attn_in['out_proj_w'], 'L1_attn_ln_g': _L1_attn_in['ln_g'], 'L1_attn_ln_b': _L1_attn_in['ln_b'], 'L1_attn_lstm_w_ih': _L1_attn_in['lstm_w_ih'], 'L1_attn_lstm_w_hh': _L1_attn_in['lstm_w_hh'], 'L1_attn_lstm_b_ih': _L1_attn_in['lstm_b_ih'], 'L1_attn_lstm_b_hh': _L1_attn_in['lstm_b_hh'], 'L1_attn_fusion_w': _L1_attn_in['fusion_w'], 'L1_attn_fusion_b': _L1_attn_in['fusion_b'], 'L1_ffn_gate_w': _L1_ffn_in['gate_w'], 'L1_ffn_w1': _L1_ffn_in['w1'], 'L1_ffn_w3': _L1_ffn_in['w3'], 'L1_ffn_w2': _L1_ffn_in['w2'], 'L1_ffn_sw1': _L1_ffn_in['sw1'], 'L1_ffn_sw3': _L1_ffn_in['sw3'], 'L1_ffn_sw2': _L1_ffn_in['sw2']}

def reference(x, L0_tok_E, L0_tok_Wq, L0_tok_bq, L0_tok_Wk, L0_tok_bk, L0_tok_Wv, L0_tok_bv, L0_tok_Wo, L0_tok_bo, L0_tok_ln_g, L0_tok_ln_b, L0_tok_W1, L0_tok_b1, L0_tok_W2, L0_tok_b2, L0_attn_ip_w, L0_attn_ip_b, L0_attn_fw_ln_g, L0_attn_fw_ln_b, L0_attn_fw_slow_w, L0_attn_fw_out_w, L0_attn_ff_ln_g, L0_attn_ff_ln_b, L0_attn_ff_w1, L0_attn_ff_b1, L0_attn_ff_w2, L0_attn_ff_b2, L0_ffn_ln_in_g, L0_ffn_ln_in_b, L0_ffn_router_w, L0_ffn_router_b, L0_ffn_ew1, L0_ffn_eb1, L0_ffn_ew2, L0_ffn_eb2, L0_ffn_sw1, L0_ffn_sb1, L0_ffn_sw2, L0_ffn_sb2, L0_ffn_ff_ln_g, L0_ffn_ff_ln_b, L0_ffn_ff_w1, L0_ffn_ff_b1, L0_ffn_ff_w2, L0_ffn_ff_b2, L1_attn_in_proj_w, L1_attn_conv_w, L1_attn_conv_b, L1_attn_x_proj_w, L1_attn_dt_proj_w, L1_attn_dt_proj_b, L1_attn_A_log, L1_attn_D_param, L1_attn_out_proj_w, L1_attn_ln_g, L1_attn_ln_b, L1_attn_lstm_w_ih, L1_attn_lstm_w_hh, L1_attn_lstm_b_ih, L1_attn_lstm_b_hh, L1_attn_fusion_w, L1_attn_fusion_b, L1_ffn_gate_w, L1_ffn_w1, L1_ffn_w3, L1_ffn_w2, L1_ffn_sw1, L1_ffn_sw3, L1_ffn_sw2):
    import jax
    import jax.numpy as jnp

    def _L0_tok_ref(x, E, Wq, bq, Wk, bk, Wv, bv, Wo, bo, ln_g, ln_b, W1, b1, W2, b2):
        import jax, jax.numpy as jnp
        import numpy as np
        import math
        V, D, H, N, DFF = (30522, 128, 8, 4, 512)
        DH = D // H

        def sinusoidal_pe(L, d):
            pos = jnp.arange(L, dtype=jnp.float32)[:, None]
            div = jnp.exp(jnp.arange(0, d, 2, dtype=jnp.float32) * (-math.log(10000.0) / d))
            pe = jnp.zeros((L, d), dtype=jnp.float32)
            pe = pe.at[:, 0::2].set(jnp.sin(pos * div))
            pe = pe.at[:, 1::2].set(jnp.cos(pos * div))
            return pe

        def layer_norm(x, g, b, eps=1e-05):
            mu = jnp.mean(x, axis=-1, keepdims=True)
            var = jnp.mean(jnp.square(x - mu), axis=-1, keepdims=True)
            return (x - mu) * jax.lax.rsqrt(var + eps) * g + b
        B, L = x.shape
        h = E[x] + sinusoidal_pe(L, D)[None, :, :]
        scale = 1.0 / math.sqrt(D / H)
        for _ in range(N):
            q = h @ Wq + bq
            k = h @ Wk + bk
            v = h @ Wv + bv
            s = jnp.einsum('bqd,bkd->bqk', q, k) * scale
            a = jax.nn.softmax(s, axis=1)
            o = jnp.einsum('bqk,bkd->bqd', a, v)
            concat = jnp.tile(o, (1, 1, H))
            attn = concat @ Wo + bo
            h1 = layer_norm(attn + h, ln_g, ln_b)
            ff = (h1 @ W1 + b1) @ W2 + b2
            h = layer_norm(h1 + ff, ln_g, ln_b)
        return h

    def _L0_attn_ref(x, ip_w, ip_b, fw_ln_g, fw_ln_b, fw_slow_w, fw_out_w, ff_ln_g, ff_ln_b, ff_w1, ff_b1, ff_w2, ff_b2):
        import jax, jax.numpy as jnp
        import numpy as np
        B, S, IN, HID, H, D, FF = (8, 512, 128, 128, 8, 64, 512)
        EPS = 1e-05

        def layer_norm(x, g, b):
            m = jnp.mean(x, axis=-1, keepdims=True)
            v = jnp.mean(jnp.square(x - m), axis=-1, keepdims=True)
            return (x - m) * jax.lax.rsqrt(v + EPS) * g + b

        def delta_rule(q, k, v, beta):

            def step(W, inp):
                qt, kt, vt, bt = inp
                wk = jnp.einsum('bhde,bhe->bhd', W, kt)
                v_new = bt * (vt - wk)
                W = W + jnp.einsum('bhd,bhe->bhde', v_new, kt)
                out = jnp.einsum('bhde,bhe->bhd', W, qt)
                return (W, out)
            bsz = q.shape[1]
            W0 = jnp.zeros((bsz, H, D, D), dtype=q.dtype)
            _, outs = jax.lax.scan(step, W0, (q, k, v, beta))
            return outs

        def fast_ff(x, ln_g, ln_b, slow_w, out_w):
            slen, bsz, _ = x.shape
            h = layer_norm(x, ln_g, ln_b)
            qkvb = jnp.einsum('sbi,oi->sbo', h, slow_w).reshape(slen, bsz, H, 3 * D + 1)
            q, k, v, beta = jnp.split(qkvb, [D, 2 * D, 3 * D], axis=-1)
            q = jax.nn.softmax(q, axis=-1)
            k = jax.nn.softmax(k, axis=-1)
            beta = jax.nn.sigmoid(beta)
            attn = delta_rule(q, k, v, beta)
            o = jnp.einsum('sbd,od->sbo', attn.reshape(slen, bsz, H * D), out_w)
            return x + o

        def ffn(x, ln_g, ln_b, w1, b1, w2, b2):
            h = layer_norm(x, ln_g, ln_b)
            h = jax.nn.relu(jnp.einsum('sbi,fi->sbf', h, w1) + b1)
            return x + jnp.einsum('sbf,of->sbo', h, w2) + b2
        out = jnp.einsum('bsi,hi->bsh', x, ip_w) + ip_b
        out = out.transpose(1, 0, 2)
        out = fast_ff(out, fw_ln_g[0], fw_ln_b[0], fw_slow_w[0], fw_out_w[0])
        out = ffn(out, ff_ln_g, ff_ln_b, ff_w1, ff_b1, ff_w2, ff_b2)
        out = fast_ff(out, fw_ln_g[1], fw_ln_b[1], fw_slow_w[1], fw_out_w[1])
        return out.transpose(1, 0, 2)

    def _L0_ffn_ref(x, ln_in_g, ln_in_b, router_w, router_b, ew1, eb1, ew2, eb2, sw1, sb1, sw2, sb2, ff_ln_g, ff_ln_b, ff_w1, ff_b1, ff_w2, ff_b2):
        import jax, jax.numpy as jnp
        import numpy as np
        B, S, D = (4, 256, 128)
        E = 16
        DH = 4 * D
        DS = 2 * D
        TOP_K = 2
        TEMP = 0.7
        SHARED_SCALE = 0.25
        EPS = 1e-05

        def layer_norm(x, g, b):
            mu = jnp.mean(x, axis=-1, keepdims=True)
            var = jnp.mean(jnp.square(x - mu), axis=-1, keepdims=True)
            return (x - mu) * jax.lax.rsqrt(var + EPS) * g + b
        h = layer_norm(x, ln_in_g, ln_in_b)
        gate = jax.nn.softmax((h @ router_w + router_b) / TEMP, axis=-1)
        vals, idx = jax.lax.top_k(gate, TOP_K)
        comb = jnp.sum(jax.nn.one_hot(idx, E, dtype=h.dtype) * vals[..., None], axis=-2)
        eh = jax.nn.silu(jnp.einsum('bsd,edh->ebsh', h, ew1) + eb1[:, None, None, :])
        ey = jnp.einsum('ebsh,ehd->ebsd', eh, ew2) + eb2[:, None, None, :]
        mix = jnp.einsum('bse,ebsd->bsd', comb, ey)
        shared = (jax.nn.silu(h @ sw1 + sb1) @ sw2 + sb2) * SHARED_SCALE
        moe_out = mix + shared
        fh = layer_norm(moe_out, ff_ln_g, ff_ln_b)
        ff_out = jax.nn.silu(fh @ ff_w1 + ff_b1) @ ff_w2 + ff_b2
        return x + moe_out + ff_out

    def _L1_attn_ref(x, in_proj_w, conv_w, conv_b, x_proj_w, dt_proj_w, dt_proj_b, A_log, D_param, out_proj_w, ln_g, ln_b, lstm_w_ih, lstm_w_hh, lstm_b_ih, lstm_b_hh, fusion_w, fusion_b):
        import jax, jax.numpy as jnp
        import numpy as np
        from jax import lax
        B_, L_, D_ = (4, 128, 128)
        HID, H2 = (128, 64)
        NL, DST, DCV, DIN, DTR = (3, 16, 4, 256, 32)

        def _silu(x):
            return x * jax.nn.sigmoid(x)

        def _layernorm(x, g, b):
            m = x.mean(-1, keepdims=True)
            v = x.var(-1, keepdims=True)
            return (x - m) / jnp.sqrt(v + 1e-05) * g + b

        def _mamba(x, wi, cw, cb, xpw, dw, db, Alog, Dp, wo):
            Bsz, Ls, _ = x.shape
            xz = jnp.einsum('bld,ed->ble', x, wi)
            xin, z = jnp.split(xz, 2, axis=-1)
            xpad = jnp.pad(xin, ((0, 0), (DCV - 1, 0), (0, 0)))
            u = cb + sum((xpad[:, k:k + Ls, :] * cw[:, k] for k in range(DCV)))
            u = _silu(u)
            xdbl = jnp.einsum('blc,ec->ble', u, xpw)
            dt_in = xdbl[..., :DTR]
            Bc = xdbl[..., DTR:DTR + DST]
            Cc = xdbl[..., DTR + DST:]
            dt = jax.nn.softplus(jnp.einsum('blr,cr->blc', dt_in, dw) + db)
            A = -jnp.exp(Alog)

            def step(h, inp):
                dt_t, B_t, C_t, u_t = inp
                dA = jnp.exp(dt_t[..., None] * A)
                h = dA * h + (dt_t * u_t)[..., None] * B_t[:, None, :]
                y = jnp.einsum('bcn,bn->bc', h, C_t)
                return (h, y)
            h0 = jnp.zeros((Bsz, DIN, DST), x.dtype)
            _, ys = lax.scan(step, h0, (dt.transpose(1, 0, 2), Bc.transpose(1, 0, 2), Cc.transpose(1, 0, 2), u.transpose(1, 0, 2)))
            y = ys.transpose(1, 0, 2) + u * Dp
            y = y * _silu(z)
            return jnp.einsum('blc,dc->bld', y, wo)

        def _lstm_dir(x, wih, whh, bih, bhh, reverse):
            Bsz = x.shape[0]

            def step(carry, xt):
                h, c = carry
                g = xt @ wih.T + h @ whh.T + bih + bhh
                i, f, gg, o = jnp.split(g, 4, axis=-1)
                c = jax.nn.sigmoid(f) * c + jax.nn.sigmoid(i) * jnp.tanh(gg)
                h = jax.nn.sigmoid(o) * jnp.tanh(c)
                return ((h, c), h)
            init = (jnp.zeros((Bsz, H2), x.dtype), jnp.zeros((Bsz, H2), x.dtype))
            _, hs = lax.scan(step, init, x.transpose(1, 0, 2), reverse=reverse)
            return hs.transpose(1, 0, 2)
        m = x
        for i in range(NL):
            mo = _mamba(m, in_proj_w[i], conv_w[i], conv_b[i], x_proj_w[i], dt_proj_w[i], dt_proj_b[i], A_log[i], D_param[i], out_proj_w[i])
            m = _layernorm(m + mo, ln_g[i], ln_b[i])
        lf = _lstm_dir(x, lstm_w_ih[0], lstm_w_hh[0], lstm_b_ih[0], lstm_b_hh[0], False)
        lb = _lstm_dir(x, lstm_w_ih[1], lstm_w_hh[1], lstm_b_ih[1], lstm_b_hh[1], True)
        comb = jnp.concatenate([m, lf, lb], axis=-1)
        return comb @ fusion_w.T + fusion_b

    def _L1_ffn_ref(x, gate_w, w1, w3, w2, sw1, sw3, sw2):
        import jax, jax.numpy as jnp
        import numpy as np
        E = 64
        K = 2
        D = 128
        H = 64
        NSH = 2
        ROUTE_SCALE = 2.5
        CAP = 256
        STD = 0.02
        bs, slen, d = x.shape
        xf = x.reshape(-1, d)
        logits = xf @ gate_w.T
        scores = jax.nn.sigmoid(logits.astype(jnp.float32))
        top_scores, top_idx = jax.lax.top_k(scores, K)
        top_scores = top_scores / (top_scores.sum(-1, keepdims=True) + 1e-20)
        top_scores = top_scores * ROUTE_SCALE
        flat_e = top_idx.reshape(-1)
        x_pairs = jnp.repeat(xf, K, axis=0)
        oh = jax.nn.one_hot(flat_e, E, dtype=jnp.int32)
        pos = jnp.take_along_axis(jnp.cumsum(oh, axis=0), flat_e[:, None], axis=1)[:, 0] - 1
        buf = jnp.zeros((E, CAP, d), dtype=xf.dtype).at[flat_e, pos].set(x_pairs, mode='drop')
        h = jax.nn.silu(jnp.einsum('ecd,edh->ech', buf, w1)) * jnp.einsum('ecd,edh->ech', buf, w3)
        y = jnp.einsum('ech,ehd->ecd', h, w2)
        valid = (pos < CAP)[:, None]
        y_pairs = jnp.where(valid, y[flat_e, jnp.minimum(pos, CAP - 1)], 0.0)
        routed = (y_pairs.reshape(-1, K, d) * top_scores[..., None].astype(xf.dtype)).sum(axis=1)
        shared = jax.nn.silu(xf @ sw1) * (xf @ sw3) @ sw2
        return (shared + routed).reshape(bs, slen, d)
    h = _L0_tok_ref(x, L0_tok_E, L0_tok_Wq, L0_tok_bq, L0_tok_Wk, L0_tok_bk, L0_tok_Wv, L0_tok_bv, L0_tok_Wo, L0_tok_bo, L0_tok_ln_g, L0_tok_ln_b, L0_tok_W1, L0_tok_b1, L0_tok_W2, L0_tok_b2)
    h = h + _L0_attn_ref(_layernorm(h, axis=-1), L0_attn_ip_w, L0_attn_ip_b, L0_attn_fw_ln_g, L0_attn_fw_ln_b, L0_attn_fw_slow_w, L0_attn_fw_out_w, L0_attn_ff_ln_g, L0_attn_ff_ln_b, L0_attn_ff_w1, L0_attn_ff_b1, L0_attn_ff_w2, L0_attn_ff_b2)
    h = h + _L0_ffn_ref(_layernorm(h, axis=-1), L0_ffn_ln_in_g, L0_ffn_ln_in_b, L0_ffn_router_w, L0_ffn_router_b, L0_ffn_ew1, L0_ffn_eb1, L0_ffn_ew2, L0_ffn_eb2, L0_ffn_sw1, L0_ffn_sb1, L0_ffn_sw2, L0_ffn_sb2, L0_ffn_ff_ln_g, L0_ffn_ff_ln_b, L0_ffn_ff_w1, L0_ffn_ff_b1, L0_ffn_ff_w2, L0_ffn_ff_b2)
    h = h + _L1_attn_ref(_layernorm(h, axis=-1), L1_attn_in_proj_w, L1_attn_conv_w, L1_attn_conv_b, L1_attn_x_proj_w, L1_attn_dt_proj_w, L1_attn_dt_proj_b, L1_attn_A_log, L1_attn_D_param, L1_attn_out_proj_w, L1_attn_ln_g, L1_attn_ln_b, L1_attn_lstm_w_ih, L1_attn_lstm_w_hh, L1_attn_lstm_b_ih, L1_attn_lstm_b_hh, L1_attn_fusion_w, L1_attn_fusion_b)
    h = h + _L1_ffn_ref(_layernorm(h, axis=-1), L1_ffn_gate_w, L1_ffn_w1, L1_ffn_w3, L1_ffn_w2, L1_ffn_sw1, L1_ffn_sw3, L1_ffn_sw2)
    return h

_drawn_inputs = setup_inputs


def setup_inputs(seed=0):
    import zlib

    import numpy as np

    out = dict(_drawn_inputs(seed))
    spreads = {'L0_tok_bq': (0.0, 0.8),
     'L0_tok_bk': (0.0, 0.8),
     'L0_tok_bv': (0.0, 0.1),
     'L0_tok_bo': (0.0, 0.1),
     'L0_tok_ln_g': (1.0, 0.2),
     'L0_tok_ln_b': (0.0, 0.1),
     'L0_tok_b1': (0.0, 0.1),
     'L0_tok_b2': (0.0, 0.1),
     'L0_attn_ip_b': (0.0, 0.1),
     'L0_attn_fw_ln_g': (1.0, 0.6),
     'L0_attn_fw_ln_b': (0.0, 0.8),
     'L0_attn_ff_ln_g': (1.0, 0.6),
     'L0_attn_ff_ln_b': (0.0, 0.8),
     'L0_attn_ff_b1': (0.0, 0.331),
     'L0_attn_ff_b2': (0.0, 0.1),
     'L0_ffn_ln_in_g': (1.0, 0.6),
     'L0_ffn_ln_in_b': (0.0, 0.8),
     'L0_ffn_router_b': (0.0, 0.8),
     'L0_ffn_eb1': (0.0, 0.8),
     'L0_ffn_eb2': (0.0, 0.746),
     'L0_ffn_sb1': (0.0, 0.8),
     'L0_ffn_sb2': (0.0, 0.325),
     'L0_ffn_ff_ln_g': (1.0, 0.6),
     'L0_ffn_ff_ln_b': (0.0, 0.8),
     'L0_ffn_ff_b1': (0.0, 0.8),
     'L0_ffn_ff_b2': (0.0, 0.1),
     'L1_attn_conv_b': (0.0, 0.8),
     'L1_attn_dt_proj_b': (-4.0, 0.6),
     'L1_attn_D_param': (1.0, 0.6),
     'L1_attn_ln_g': (1.0, 0.2),
     'L1_attn_ln_b': (0.0, 0.641),
     'L1_attn_lstm_b_ih': (0.0, 0.8),
     'L1_attn_lstm_b_hh': (0.0, 0.8),
     'L1_attn_fusion_b': (0.0, 0.1)}
    factors = {'L0_tok_Wq': 8.0,
     'L0_tok_Wk': 8.0,
     'L0_ffn_router_w': 4.747,
     'L0_ffn_ew1': 8.0,
     'L0_ffn_ew2': 8.0,
     'L0_ffn_sw1': 8.0,
     'L0_ffn_sw2': 7.815,
     'L1_attn_in_proj_w': 8.0,
     'L1_attn_conv_w': 8.0,
     'L1_attn_x_proj_w': 8.0,
     'L1_attn_dt_proj_w': 8.0,
     'L1_attn_A_log': 8.0,
     'L1_attn_out_proj_w': 8.0,
     'L1_attn_lstm_w_ih': 3.071,
     'L1_attn_lstm_w_hh': 8.0,
     'L1_ffn_gate_w': 8.0,
     'L1_ffn_w1': 8.0,
     'L1_ffn_w3': 8.0,
     'L1_ffn_w2': 8.0,
     'L1_ffn_sw1': 8.0,
     'L1_ffn_sw3': 8.0,
     'L1_ffn_sw2': 8.0}
    for name, (base, spread) in spreads.items():
        noise = np.random.default_rng([zlib.crc32(name.encode()), seed]).standard_normal(out[name].shape)
        drawn = base * np.exp(spread * noise) if base else spread * noise
        out[name] = jnp.asarray(drawn.astype(out[name].dtype))
    for name, factor in factors.items():
        out[name] = (out[name] * factor).astype(out[name].dtype)
    return out
```

```python
import numpy as np
from contextlib import ExitStack
import concourse.bass as bass
from concourse import mybir
from concourse.bass import ds

FP32 = mybir.dt.float32
BF16 = mybir.dt.bfloat16
U32 = mybir.dt.uint32
ALU = mybir.AluOpType
ACT = mybir.ActivationFunctionType
AX = mybir.AxisListType

P = 128
BATCH = 16
D = 128
GROUPS = 4
GS = BATCH // GROUPS
GT = GS * P
EPS = 1e-5


class Model:
    pass


def open_semaphores(nc, names):
    return {n: nc.alloc_semaphore(n) for n in names.split()}


def close_semaphores(nc, sems):
    for s in sems.values():
        nc.gpsimd.sem_clear(s)
    nc.all_engine_barrier()
    for s in sems.values():
        nc.release_semaphore(s)


def normalise_stats(nc, dve, psum, stats, moments, var_eps, s, count):
    for j in range(GS):
        last = nc.vector.bn_stats(stats[:, j, :], psum[:, j, :])
    last.then_inc(s["ln_stats"], 1)
    dve.wait_ge(s["ln_stats"], count)
    nc.vector.memset(var_eps, 0.0)
    for j in range(GS):
        last = nc.vector.bn_aggr(moments[:, j, :], stats[:, j, :])
    last.then_inc(s["ln_moments"], 1)
    dve.wait_ge(s["ln_moments"], count)
    nc.vector.tensor_scalar(var_eps, moments[:, :, 1], EPS, None, ALU.add).then_inc(s["ln_var"], 1)


NORM_SEMS = "ln_stats ln_moments ln_var ln_rstd xh_done xT_mm xT_done "


def norm_buffers(sb, tag):
    return dict(stats=sb(tag + "_stats", [P, GROUPS, GS, 6]), mom=sb(tag + "_mom", [P, GROUPS, GS, 2]),
                           var=sb(tag + "_var", [P, GROUPS, GS]), rstd=sb(tag + "_rstd", [P, GROUPS, GS]),
                           xh=sb(tag + "_xh", [P, GROUPS, GS, D]))


def norm_vector(nc, dve, src, n, s, k):
    for g in range(GROUPS + 1):
        if g < GROUPS:
            normalise_stats(nc, dve, src(g), n["stats"][:, g], n["mom"][:, g], n["var"][:, g, :], s, GROUPS * k + g + 1)
        if g > 0:
            f = g - 1
            dve.wait_ge(s["ln_rstd"], GROUPS * k + f + 1)
            for j in range(GS):
                last = nc.vector.tensor_scalar(n["xh"][:, f, j, :], src(f)[:, j, :], n["mom"][:, f, j, 0:1],
                                               n["rstd"][:, f, j:j + 1], ALU.subtract, ALU.mult)
            last.then_inc(s["xh_done"], 1)


def norm_pool(nc, pool, n, m, s, k):
    for g in range(GROUPS):
        pool.wait_ge(s["ln_var"], GROUPS * k + g + 1)
        nc.gpsimd.tensor_tensor(n["rstd"][:, g, :], n["var"][:, g, :], m.neg_half[:, 0:GS], ALU.pow).then_inc(s["ln_rstd"], 1)


def norm_transpose(nc, pe, dst, n, m, s, k):
    for g in range(GROUPS):
        pe.wait_ge(s["xh_done"], GROUPS * k + g + 1)
        for j in range(GS):
            last = nc.tensor.transpose(dst(g)[:, j, :], n["xh"][:, g, j, :], m.ident)
        last.then_inc(s["xT_mm"], 1)


def norm_scale(nc, act, dst, src, gain_bias, s, k):
    for g in range(GROUPS):
        act.wait_ge(s["xT_mm"], GROUPS * k + g + 1)
        if gain_bias is None:
            last = nc.scalar.activation(dst(g), src(g), ACT.Copy)
        else:
            last = nc.scalar.activation(dst(g), src(g), ACT.Identity, bias=gain_bias[:, 1:2], scale=gain_bias[:, 0:1])
        last.then_inc(s["xT_done"], 1)


def token_stage(nc, io, m):
    LAYERS, DH, HEADS = 4, 16, 8
    FF = 512
    s = open_semaphores(nc, "w_in idx_in e_in emb_done embT ht_ready qk_mm q_done k_done v_mm v_done "
                            "sc_mm mx_done exp_done rz_done vn_done o_mm o_done attn_mm ln_stats ln_moments ln_var "
                            "ln_rstd xh_done xT_mm h1_ready ff_mm setup_mm setup_dve setup_act htok_mm htok_done")
    with ExitStack() as mem:
        def sb(name, shape, dt=FP32):
            return mem.enter_context(nc.sbuf_tensor(name, shape, dt))
        wq = sb("t_wq", [P, 3, DH])
        bqk = sb("t_bqk", [DH, 2])
        bqs = sb("t_bqs", [DH, 1])
        bv = sb("t_bv", [P, DH])
        wo8 = sb("t_wo8", [DH, HEADS, D])
        wo = sb("t_wo", [32, D])
        lngb = sb("t_lngb", [P, 2])
        w1T = sb("t_w1T", [P, FF // P, D])
        w2 = sb("t_w2", [P, FF // P, D])
        b1c = sb("t_b1c", [P, FF // P])
        b2r = sb("t_b2r", [1, D])
        pe_tab = sb("t_pe", [P, D])
        idx = sb("t_idx", [P, BATCH], mybir.dt.int32)
        emb = sb("t_emb", [P, BATCH, D])
        wff = sb("t_wff", [P, D])
        cff = sb("t_cff", [1, GT])
        hT = sb("t_hT", [P, GROUPS, GT])
        h1T = sb("t_h1T", [P, GROUPS, GT])
        qT = sb("t_qT", [DH, GROUPS, GT])
        kT = sb("t_kT", [DH, GROUPS, GT])
        v = sb("t_v", [P, GROUPS, GS, DH])
        vn = sb("t_vn", [P, GROUPS, GS, DH])
        nmx = sb("t_nmx", [P, GROUPS, GS])
        zs = sb("t_zs", [P, GROUPS, GS])
        rz = sb("t_rz", [P, GROUPS, GS])
        es = sb("t_es", [P, GROUPS, GS, P])
        oT = sb("t_oT", [32, GROUPS, GT])
        stats = sb("t_stats", [P, GROUPS, GS, 6])
        mom = sb("t_mom", [P, GROUPS, GS, 2])
        var = sb("t_var", [P, GROUPS, GS])
        rstd = sb("t_rstd", [P, GROUPS, GS])
        xh = sb("t_xh", [P, GROUPS, GS, D])
        X = [m.bank[2 * g] for g in range(GROUPS)]
        Y = [m.bank[2 * g + 1] for g in range(GROUPS)]
        X4 = [b[:, :].rearrange("p (j c) -> p j c", j=GS) for b in X]
        Y4 = [b[:, :].rearrange("p (j c) -> p j c", j=GS) for b in Y]
        ident = m.ident
        n_w = [0]
        with nc.Block() as block:
            @block.sync
            def _(sp):
                sp.dma_start(idx[:, :], io["x_t"]).then_inc(s["idx_in"], 16)
                for dst, src in [(wq[:, 0, :], io["L0_tok_Wq"]), (wq[:, 1, :], io["L0_tok_Wk"]), (wq[:, 2, :], io["L0_tok_Wv"]),
                                 (bqk[:, 0:1], io["L0_tok_bq"]), (bqk[:, 1:2], io["L0_tok_bk"]), (bv[:, :], io["L0_tok_bv"]),
                                 (wo8[:, :, :], io["L0_tok_Wo"]), (wo[DH:DH + 1, :], io["L0_tok_bo"]),
                                 (lngb[:, 0:1], io["L0_tok_ln_g"]), (lngb[:, 1:2], io["L0_tok_ln_b"]),
                                 (w1T[:, :, :], io["L0_tok_W1"]), (w2[:, :, :], io["L0_tok_W2"]), (b1c[:, :], io["L0_tok_b1"]),
                                 (b2r[:, :], io["L0_tok_b2"]), (pe_tab[:, :], io["pe_table"])]:
                    sp.dma_start(dst, src).then_inc(s["w_in"], 16)
                    n_w[0] += 16

            @block.gpsimd
            def _(pool):
                pool.wait_ge(s["idx_in"], 16)
                for b in range(BATCH):
                    nc.gpsimd.indirect_dma_start(
                        out=emb[:, b, :], out_offset=None, in_=io["L0_tok_E"],
                        in_offset=bass.IndirectOffsetOnAxis(ap=idx[:, b:b + 1].bitcast(U32), axis=0)).then_inc(m.embedded, 16)
                nc.gpsimd.memset(oT[:, :, :], 1.0).then_inc(s["setup_act"], 1)
                with pool.Fori(0, LAYERS) as layer:
                    for k in range(2):
                        for g in range(GROUPS):
                            pool.wait_ge(s["ln_var"], layer * 8 + (4 * k + g + 1))
                            nc.gpsimd.tensor_tensor(rstd[:, g, :], var[:, g, :], m.neg_half[:, 0:GS],
                                                    ALU.pow).then_inc(s["ln_rstd"], 1)

            @block.scalar
            def _(act):
                act.wait_ge(s["w_in"], n_w[0])
                nc.scalar.activation(bqs[:, :], bqk[:, 0:1], ACT.Copy, scale=0.25).then_inc(s["setup_act"], 1)
                act.wait_ge(s["setup_act"], 2)
                act.wait_ge(s["embT"], GROUPS)
                for g in range(GROUPS):
                    last = nc.scalar.activation(hT[:, g, :], X[g][:, :], ACT.Copy)
                    last.then_inc(s["ht_ready"], 1)
                with act.Fori(0, LAYERS) as layer:
                    for g in range(GROUPS):
                        act.wait_ge(s["qk_mm"], layer * 4 + (g + 1))
                        nc.scalar.activation(qT[:, g, :], X[g][0:DH, :], ACT.Identity, bias=bqs[:, 0:1],
                                             scale=0.25).then_inc(s["q_done"], 1)
                    for g in range(GROUPS):
                        act.wait_ge(s["mx_done"], layer * 4 + (g + 1))
                        for j in range(GS):
                            last = nc.scalar.activation(es[:, g, j, :], Y4[g][:, j, :], ACT.Exp, bias=nmx[:, g, j:j + 1],
                                                        accum_out=zs[:, g, j:j + 1])
                        last.then_inc(s["exp_done"], 1)
                    for g in range(GROUPS):
                        act.wait_ge(s["o_mm"], layer * 4 + (g + 1))
                        nc.scalar.activation(oT[0:DH, g, :], X[g][0:DH, :], ACT.Copy).then_inc(s["o_done"], 1)
                    for k in range(2):
                        dst = (h1T, hT)[k]
                        for g in range(GROUPS):
                            act.wait_ge(s["xT_mm"], layer * 8 + (4 * k + g + 1))
                            nc.scalar.activation(dst[:, g, :], X[g][:, :], ACT.Identity, bias=lngb[:, 1:2],
                                                 scale=lngb[:, 0:1]).then_inc((s["h1_ready"], s["ht_ready"])[k], 1)

            @block.vector
            def _(dve):
                dve.wait_ge(s["w_in"], n_w[0])
                nc.vector.tensor_reduce(out=wo[0:DH, :], in_=wo8[:, :, :].rearrange("p h d -> p d h"),
                                        axis=AX.X, op=ALU.add).then_inc(s["setup_dve"], 1)
                dve.wait_ge(s["setup_mm"], 1)
                nc.vector.tensor_copy(wff[:, :], X[0][:, 0:D])
                for j in range(GS):
                    last = nc.vector.tensor_copy(cff[:, j * D:(j + 1) * D], Y[0][0:1, 0:D])
                last.then_inc(s["setup_dve"], 1)
                dve.wait_ge(m.embedded, 16 * BATCH)
                for b in range(BATCH):
                    last = nc.vector.tensor_tensor(emb[:, b, :], emb[:, b, :], pe_tab[:, :], ALU.add)
                last.then_inc(s["emb_done"], 1)
                with dve.Fori(0, LAYERS) as layer:
                    for g in range(GROUPS):
                        dve.wait_ge(s["qk_mm"], layer * 4 + (g + 1))
                        nc.vector.tensor_scalar(kT[:, g, :], Y[g][0:DH, :], bqk[:, 1:2], None,
                                                ALU.add).then_inc(s["k_done"], 1)
                    for g in range(GROUPS):
                        dve.wait_ge(s["v_mm"], layer * 4 + (g + 1))
                        nc.vector.tensor_tensor(v[:, g, :, :], X[g][:, 0:GS * DH].rearrange("p (j e) -> p j e", j=GS),
                                                bv[:, :].unsqueeze(1).to_broadcast([P, GS, DH]),
                                                ALU.add).then_inc(s["v_done"], 1)
                        dve.wait_ge(s["sc_mm"], layer * 4 + (g + 1))
                        nc.vector.tensor_reduce(out=nmx[:, g, :], in_=Y4[g], axis=AX.X, op=ALU.max,
                                                negate=True).then_inc(s["mx_done"], 1)
                    for g in range(GROUPS):
                        dve.wait_ge(s["exp_done"], layer * 4 + (g + 1))
                        nc.vector.reciprocal(rz[:, g, :], zs[:, g, :]).then_inc(s["rz_done"], 1)
                        dve.wait_ge(s["rz_done"], layer * 4 + (g + 1))
                        nc.vector.tensor_tensor(vn[:, g, :, :], v[:, g, :, :],
                                                rz[:, g, :].unsqueeze(2).to_broadcast([P, GS, DH]),
                                                ALU.mult).then_inc(s["vn_done"], 1)
                    for k in range(2):
                        for g in range(GROUPS + 1):
                            if g < GROUPS:
                                dve.wait_ge((s["attn_mm"], s["ff_mm"])[k], layer * 4 + (g + 1))
                                normalise_stats(nc, dve, Y4[g], stats[:, g], mom[:, g], var[:, g, :], s,
                                                layer * 8 + (4 * k + g + 1))
                            if g > 0:
                                f = g - 1
                                dve.wait_ge(s["ln_rstd"], layer * 8 + (4 * k + f + 1))
                                for j in range(GS):
                                    last = nc.vector.tensor_scalar(xh[:, f, j, :], Y4[f][:, j, :], mom[:, f, j, 0:1],
                                                                   rstd[:, f, j:j + 1], ALU.subtract, ALU.mult)
                                last.then_inc(s["xh_done"], 1)
                for g in range(GROUPS):
                    dve.wait_ge(s["htok_mm"], g + 1)
                    nc.vector.tensor_copy(m.h[:, GS * g:GS * (g + 1), :], X4[g]).then_inc(s["htok_done"], 1)
                dve.wait_ge(s["htok_done"], GROUPS)

            @block.tensor
            def _(pe):
                pe.wait_ge(s["w_in"], n_w[0])
                for c in range(FF // P):
                    nc.tensor.matmul(X[0][:, 0:D], w1T[:, c, :], w2[:, c, :], start=(c == 0), stop=False)
                nc.tensor.matmul(X[0][:, 0:D], ident, ident, start=False, stop=True)
                for c in range(FF // P):
                    nc.tensor.matmul(Y[0][0:1, 0:D], b1c[:, c:c + 1], w2[:, c, :], start=(c == 0), stop=False)
                nc.tensor.matmul(Y[0][0:1, 0:D], m.ones_row[0:1, 0:1], b2r[:, :], start=False, stop=True).then_inc(s["setup_mm"], 1)
                pe.wait_ge(s["setup_dve"], 2)
                pe.wait_ge(s["emb_done"], 1)
                for g in range(GROUPS):
                    for j in range(GS):
                        last = nc.tensor.transpose(X4[g][:, j, :], emb[:, GS * g + j, :], ident)
                    last.then_inc(s["embT"], 1)
                with pe.Fori(0, LAYERS) as layer:
                    for g in range(GROUPS):
                        pe.wait_ge(s["ht_ready"], layer * 4 + (g + 1))
                        nc.tensor.matmul(X[g][0:DH, :], wq[:, 0, :], hT[:, g, :], start=True, stop=True)
                        nc.tensor.matmul(Y[g][0:DH, :], wq[:, 1, :], hT[:, g, :], start=True, stop=True).then_inc(s["qk_mm"], 1)
                    for g in range(GROUPS):
                        pe.wait_ge(s["q_done"], layer * 4 + (g + 1))
                        for j in range(GS):
                            last = nc.tensor.matmul(X[g][:, j * DH:(j + 1) * DH], hT[:, g, j * P:(j + 1) * P], wq[:, 2, :],
                                                    start=True, stop=True)
                        last.then_inc(s["v_mm"], 1)
                        pe.wait_ge(s["k_done"], layer * 4 + (g + 1))
                        for j in range(GS):
                            last = nc.tensor.matmul(Y4[g][:, j, :], kT[:, g, j * P:(j + 1) * P], qT[:, g, j * P:(j + 1) * P],
                                                    start=True, stop=True)
                        last.then_inc(s["sc_mm"], 1)
                    for g in range(GROUPS):
                        pe.wait_ge(s["vn_done"], layer * 4 + (g + 1))
                        for j in range(GS):
                            last = nc.tensor.matmul(X4[g][0:DH, j, :], vn[:, g, j, :], es[:, g, j, :], start=True, stop=True)
                        last.then_inc(s["o_mm"], 1)
                    for g in range(GROUPS):
                        pe.wait_ge(s["o_done"], layer * 4 + (g + 1))
                        for j in range(GS):
                            nc.tensor.matmul(Y4[g][:, j, :], oT[0:DH + 1, g, j * P:(j + 1) * P], wo[0:DH + 1, :],
                                             start=True, stop=False)
                            last = nc.tensor.matmul(Y4[g][:, j, :], hT[:, g, j * P:(j + 1) * P], ident, start=False, stop=True)
                        last.then_inc(s["attn_mm"], 1)
                    for k in range(2):
                        for g in range(GROUPS):
                            pe.wait_ge(s["xh_done"], layer * 8 + (4 * k + g + 1))
                            for j in range(GS):
                                last = nc.tensor.transpose(X4[g][:, j, :], xh[:, g, j, :], ident)
                            last.then_inc(s["xT_mm"], 1)
                        if k == 0:
                            for g in range(GROUPS):
                                pe.wait_ge(s["h1_ready"], layer * 4 + (g + 1))
                                for j in range(GS):
                                    nc.tensor.matmul(Y4[g][:, j, :], m.ones_row[0:1, 0:P], cff[:, 0:D], start=True, stop=False)
                                    last = nc.tensor.matmul(Y4[g][:, j, :], h1T[:, g, j * P:(j + 1) * P], wff[:, :],
                                                            start=False, stop=True)
                                last.then_inc(s["ff_mm"], 1)
                for g in range(GROUPS):
                    pe.wait_ge(s["ht_ready"], 4 * LAYERS + g + 1)
                    for j in range(GS):
                        last = nc.tensor.transpose(X4[g][:, j, :], hT[:, g, j * P:(j + 1) * P], ident)
                    last.then_inc(s["htok_mm"], 1)
    close_semaphores(nc, s)

def attention_input_stage(nc, io, m):
    s = open_semaphores(nc, NORM_SEMS + "w_in out_mm out_done")
    with ExitStack() as mem:
        def sb(name, shape, dt=FP32):
            return mem.enter_context(nc.sbuf_tensor(name, shape, dt))
        w = sb("ip_w", [P, D])
        b = sb("ip_b", [1, D])
        n = norm_buffers(sb, "ip")
        xT = sb("ip_xT", [P, GROUPS, GT])
        bank4 = [k[:, :].rearrange("p (j c) -> p j c", j=GS) for k in m.bank]
        with nc.Block() as block:
            @block.sync
            def _(sp):
                sp.dma_start(w[:, :], io["L0_attn_ip_w"]).then_inc(s["w_in"], 16)
                sp.dma_start(b[:, :], io["L0_attn_ip_b"]).then_inc(s["w_in"], 16)

            @block.gpsimd
            def _(pool):
                norm_pool(nc, pool, n, m, s, 0)

            @block.scalar
            def _(act):
                norm_scale(nc, act, lambda g: xT[:, g, :], lambda g: m.bank[2 * g], None, s, 0)

            @block.vector
            def _(dve):
                norm_vector(nc, dve, lambda g: m.h[:, GS * g:GS * (g + 1), :], n, s, 0)
                for g in range(GROUPS):
                    dve.wait_ge(s["out_mm"], g + 1)
                    nc.vector.tensor_copy(m.res[:, GS * g:GS * (g + 1), :], bank4[2 * g + 1]).then_inc(s["out_done"], 1)
                dve.wait_ge(s["out_done"], GROUPS)

            @block.tensor
            def _(pe):
                norm_transpose(nc, pe, lambda g: bank4[2 * g], n, m, s, 0)
                pe.wait_ge(s["w_in"], 32)
                for g in range(GROUPS):
                    pe.wait_ge(s["xT_done"], g + 1)
                    for j in range(GS):
                        nc.tensor.matmul(bank4[2 * g + 1][:, j, :], m.ones_row[0:1, 0:P], b[:, :], start=True, stop=False)
                        last = nc.tensor.matmul(bank4[2 * g + 1][:, j, :], xT[:, g, j * P:(j + 1) * P], w[:, :],
                                                start=False, stop=True)
                    last.then_inc(s["out_mm"], 1)
    close_semaphores(nc, s)


def ffn_stage(nc, io, m, tag, w, src, dst, func):
    FF = 512
    FC = FF // P
    s = open_semaphores(nc, NORM_SEMS + "w_in up_mm up_done down_mm down_done")
    with ExitStack() as mem:
        def sb(name, shape, dt=FP32):
            return mem.enter_context(nc.sbuf_tensor(name, shape, dt))
        gb = sb(tag + "_gb", [P, 2])
        w1_sb = sb(tag + "_w1", [P, FF])
        b1_sb = sb(tag + "_b1", [P, FC])
        w2_sb = sb(tag + "_w2", [P, FC, D])
        b2_sb = sb(tag + "_b2", [1, D])
        n = norm_buffers(sb, tag)
        xT = sb(tag + "_xT", [P, GROUPS, GT])
        up = sb(tag + "_up", [P, 2, FC, GT])
        bank4 = [k[:, :].rearrange("p (j c) -> p j c", j=GS) for k in m.bank]
        with nc.Block() as block:
            @block.sync
            def _(sp):
                for dst, src in [(gb[:, 0:1], w["ln_g"]), (gb[:, 1:2], w["ln_b"]), (w1_sb[:, :], w["w1"]),
                                 (b1_sb[:, :], w["b1"]), (w2_sb[:, :, :], w["w2"]), (b2_sb[:, :], w["b2"])]:
                    sp.dma_start(dst, src).then_inc(s["w_in"], 16)

            @block.gpsimd
            def _(pool):
                norm_pool(nc, pool, n, m, s, 0)

            @block.scalar
            def _(act):
                act.wait_ge(s["w_in"], 96)
                norm_scale(nc, act, lambda g: xT[:, g, :], lambda g: m.bank[g], gb, s, 0)
                for g in range(GROUPS):
                    if g >= 2:
                        act.wait_ge(s["down_mm"], g - 1)
                    for c in range(FC):
                        act.wait_ge(s["up_mm"], FC * g + c + 1)
                        nc.scalar.activation(up[:, g % 2, c, :], m.bank[c], func,
                                             bias=b1_sb[:, c:c + 1]).then_inc(s["up_done"], 1)

            @block.vector
            def _(dve):
                norm_vector(nc, dve, lambda g: src[:, GS * g:GS * (g + 1), :], n, s, 0)
                for g in range(GROUPS):
                    dve.wait_ge(s["down_mm"], g + 1)
                    nc.vector.tensor_tensor(dst[:, GS * g:GS * (g + 1), :], dst[:, GS * g:GS * (g + 1), :],
                                            bank4[4 + g], ALU.add).then_inc(s["down_done"], 1)
                dve.wait_ge(s["down_done"], GROUPS)

            @block.tensor
            def _(pe):
                norm_transpose(nc, pe, lambda g: bank4[g], n, m, s, 0)
                pe.wait_ge(s["w_in"], 96)
                for g in range(GROUPS + 1):
                    if g < GROUPS:
                        pe.wait_ge(s["xT_done"], GROUPS)
                        for c in range(FC):
                            if g > 0:
                                pe.wait_ge(s["up_done"], FC * (g - 1) + c + 1)
                            nc.tensor.matmul(m.bank[c], w1_sb[:, c * P:(c + 1) * P], xT[:, g, :], start=True,
                                             stop=True).then_inc(s["up_mm"], 1)
                    if g > 0:
                        f = g - 1
                        pe.wait_ge(s["up_done"], FC * g)
                        for j in range(GS):
                            nc.tensor.matmul(bank4[4 + f][:, j, :], m.ones_row[0:1, 0:P], b2_sb[:, :], start=True, stop=False)
                            for c in range(FC):
                                last = nc.tensor.matmul(bank4[4 + f][:, j, :], up[:, f % 2, c, j * P:(j + 1) * P], w2_sb[:, c, :],
                                                        start=False, stop=(c == FC - 1))
                        last.then_inc(s["down_mm"], 1)
    close_semaphores(nc, s)


def fast_weight_stage(nc, io, m, layer):
    H, DH = 8, 64
    HQ = 4
    LEVELS = 4
    FULL = LEVELS - 1
    VECTOR_LINKS = 9
    s = open_semaphores(nc, "w_in ln_stats ln_var ln_rstd xh_done xT_mm hT_done qk_mm v_mm shift_q shift_k exp_qk exp_b links qkv_done vb_done "
                            "kT_mm kT_done at_mm a_mm minus_at minus_a pt_done coff_done i_minus_at x2_done xt2_done y_mm w_done "
                            "xt_mm x_mm xt_done x_done bt_mm bt_done r_mm r_done u_mm u_done o_mm o_done out_mm out_done")
    with ExitStack() as mem:
        def sb(name, shape, dt=FP32):
            return mem.enter_context(nc.sbuf_tensor("fw%d_%s" % (layer, name), shape, dt))
        gb = sb("gb", [P, 2])
        wqkv = sb("wqkv", [P, 3, H * DH])
        wb = sb("wb", [P, H])
        wo = sb("wo", [P, H // 2, D])
        masks = sb("masks", [P, 9, P])
        stats, mom, var, rstd = sb("stats", [P, 6]), sb("mom", [P, 2]), sb("var", [P, 1]), sb("rstd", [P, 1])
        xh, hT = sb("xh", [P, D]), sb("hT", [P, P])
        mx = sb("mx", [P, 2, H])
        shifted = sb("shifted", [P, 2, H, DH])
        ez = sb("ez", [P, 2, H, DH])
        zs, rz = sb("zs", [P, 2, H]), sb("rz", [P, 2, H])
        eb, beta, rzb = sb("eb", [P, H]), sb("beta", [P, H]), sb("rzb", [P, H])
        qn, kn, kb, vb = (sb(x, [P, H, DH]) for x in ("qn", "kn", "kb", "vb"))
        qT, kT, kbT = (sb(x, [P, H // 2, P]) for x in ("qT", "kT", "kbT"))
        MT, PT = (sb(x, [P, 2, HQ, P]) for x in ("MT", "PT"))
        coff = sb("coff", [P, 2, HQ, P])
        X, W, nBT = (sb(x, [P, 2, HQ, P]) for x in ("X", "W", "nBT"))
        XTs = [sb("XT%d" % x, [P, 2, HQ, P]) for x in range(2)]
        R, U = (sb(x, [P, 2, HQ, DH]) for x in ("R", "U"))
        OT = sb("OT", [P, H // 2, P])
        misc, bq, bk, bv = m.bank[0], m.bank[1], m.bank[2], m.bank[3]
        xT_ps, beta_ps, out_ps = misc[:, 0:P], misc[:, P:P + H], misc[:, 2 * P:3 * P]
        first = [m.bank[4], m.bank[6]]
        second = [m.bank[5], m.bank[7]]
        A4 = [b[:, :].rearrange("p (j c) -> p j c", j=HQ) for b in first]
        B4 = [b[:, :].rearrange("p (j c) -> p j c", j=HQ) for b in second]
        both = [m.psum[:, 4 + 2 * Q:6 + 2 * Q, :].rearrange("p f (j c) -> p f j c", j=HQ) for Q in range(2)]
        heads = [b[:, :].rearrange("p (h e) -> p h e", h=H) for b in (bq, bk, bv)]
        pairs = [b[:, :].rearrange("p (h c) -> p h c", h=H // 2) for b in (bq, bk, bv)]
        a_ps = m.psum[:, 1:3, :].rearrange("p f (j c) -> p f j c", j=HQ)
        MINUS_SUB, MINUS_UPPER, PAIRS_T, M_OFF, M_CAUSAL, M_LEVEL = range(6)

        def mask(k):
            return masks[:, k, :].unsqueeze(1).to_broadcast([P, HQ, P])

        def mask4(k):
            return masks[:, k, :].unsqueeze(1).unsqueeze(1).to_broadcast([P, 2, 2, P])

        eye = m.ident.unsqueeze(1).to_broadcast([P, HQ, P])

        def by_parity(x, Q):
            return x[:, Q].rearrange("p (f j) c -> p f j c", f=2)

        def over_e(x):
            return x.unsqueeze(2).to_broadcast([P, H, DH])

        def tile(b):
            return m.res[:, ds(b, 1), :].rearrange("p o d -> p (o d)") if not isinstance(b, int) else m.res[:, b, :]

        with nc.Block() as block:
            @block.sync
            def _(sp):
                for dst, src in [(gb[:, 0:1], io["L0_attn_fw_ln_g"][layer]), (gb[:, 1:2], io["L0_attn_fw_ln_b"][layer]),
                                 (wqkv[:, :, :], io["fw_qkv"][layer]), (wb[:, :], io["fw_beta"][layer]), (wo[:, :, :], io["fw_out"][layer]),
                                 (masks[:, :, :], io["fw_masks"])]:
                    sp.dma_start(dst, src).then_inc(s["w_in"], 16)

            @block.gpsimd
            def _(pool):
                pool.wait_ge(s["w_in"], 96)

                def rstd_step(f):
                    pool.wait_ge(s["ln_var"], f + 1)
                    nc.gpsimd.tensor_tensor(rstd[:, :], var[:, :], m.neg_half[:, 0:1], ALU.pow).then_inc(s["ln_rstd"], 1)

                def at_eye(b, Q):
                    pool.wait_ge(s["minus_at"], 2 * b + (Q + 1))
                    nc.gpsimd.tensor_tensor(MT[:, Q], MT[:, Q], eye, ALU.add).then_inc(s["i_minus_at"], 1)

                def pairs(b, Q):
                    pool.wait_ge(s["i_minus_at"], 2 * b + (Q + 1))
                    nc.gpsimd.tensor_tensor(XTs[0][:, Q], MT[:, Q], mask(PAIRS_T), ALU.mult).then_inc(s["xt2_done"], 1)

                rstd_step(0)

                def body(b, front):
                    if front:
                        rstd_step(b + 1)
                    at_eye(b, 0)
                    at_eye(b, 1)
                    pairs(b, 0)
                    pairs(b, 1)

                with pool.Fori(0, BATCH - 1) as b:
                    body(b, True)
                body(BATCH - 1, False)

            @block.scalar
            def _(act):
                act.wait_ge(s["w_in"], 96)

                def f_hT(f):
                    act.wait_ge(s["xT_mm"], f + 1)
                    nc.scalar.activation(hT[:, :], xT_ps, ACT.Identity, bias=gb[:, 1:2], scale=gb[:, 0:1]).then_inc(s["hT_done"], 1)

                def f_exp(f):
                    act.wait_ge(s["shift_q"], f + 1)
                    nc.scalar.activation(ez[:, 0], shifted[:, 0], ACT.Exp).then_inc(s["exp_qk"], 1)
                    act.wait_ge(s["shift_k"], f + 1)
                    nc.scalar.activation(ez[:, 1], shifted[:, 1], ACT.Exp).then_inc(s["exp_qk"], 1)
                    act.wait_ge(s["v_mm"], f + 1)
                    nc.scalar.activation(eb[:, :], beta_ps, ACT.Exp, scale=-1.0).then_inc(s["exp_b"], 1)

                def f_transposed(f):
                    for n, (dst, src) in enumerate(((kbT, bq), (qT, bk), (kT, bv))):
                        act.wait_ge(s["kT_mm"], 3 * f + (n + 1))
                        nc.scalar.activation(dst[:, :, :].rearrange("p a b -> p (a b)"), src[:, :], ACT.Copy).then_inc(s["kT_done"], 1)

                f_hT(0)
                f_exp(0)
                f_transposed(0)

                def body(b, front):
                    if front:
                        f_hT(b + 1)
                    for l in range(LEVELS):
                        for Q in range(2):
                            act.wait_ge(s["xt_mm"], 2 * LEVELS * b + (2 * l + Q + 1))
                            nc.scalar.activation(XTs[(l + 1) % 2][:, Q], A4[Q], ACT.Copy).then_inc(s["xt_done"], 1)
                            if l < FULL:
                                act.wait_ge(s["x_mm"], 2 * FULL * b + (2 * l + Q + 1))
                                nc.scalar.activation(X[:, Q], B4[Q], ACT.Copy).then_inc(s["x_done"], 1)
                        if l == 1 and front:
                            f_exp(b + 1)
                    for Q in range(2):
                        act.wait_ge(s["bt_mm"], 2 * b + (Q + 1))
                        nc.scalar.activation(nBT[:, Q], B4[Q], ACT.Copy, scale=-1.0).then_inc(s["bt_done"], 1)
                    if front:
                        f_transposed(b + 1)
                    for Q in range(2):
                        act.wait_ge(s["o_mm"], 2 * b + (Q + 1))
                        nc.scalar.activation(OT[:, 2 * Q:2 * Q + 2, :], B4[Q][:, 0:2, :], ACT.Copy).then_inc(s["o_done"], 1)

                with act.Fori(0, BATCH - 1) as b:
                    body(b, True)
                body(BATCH - 1, False)

            @block.vector
            def _(dve):
                dve.wait_ge(s["w_in"], 96)

                def f_norm(f):
                    nc.vector.bn_stats(stats[:, :], tile(f)).then_inc(s["ln_stats"], 1)
                    dve.wait_ge(s["ln_stats"], 3 * f + 1)
                    nc.vector.memset(var[:, :], 0.0)
                    nc.vector.bn_aggr(mom[:, :], stats[:, :]).then_inc(s["ln_stats"], 1)
                    dve.wait_ge(s["ln_stats"], 3 * f + 2)
                    nc.vector.tensor_scalar(var[:, :], mom[:, 1:2], EPS, None, ALU.add).then_inc(s["ln_var"], 1)
                    dve.wait_ge(s["ln_rstd"], f + 1)
                    nc.vector.tensor_scalar(xh[:, :], tile(f), mom[:, 0:1], rstd[:, 0:1], ALU.subtract,
                                            ALU.mult).then_inc(s["xh_done"], 1)
                    dve.wait_ge(s["xh_done"], f + 1)
                    nc.vector.memset(var[:, :], 0.0).then_inc(s["ln_stats"], 1)

                def f_shift(f):
                    dve.wait_ge(s["qk_mm"], f + 1)
                    for n in range(2):
                        nc.vector.tensor_reduce(out=mx[:, n, :], in_=heads[n], axis=AX.X, op=ALU.max).then_inc(s["links"], 1)
                        dve.wait_ge(s["links"], VECTOR_LINKS * f + (n + 1))
                        nc.vector.tensor_tensor(shifted[:, n], heads[n], over_e(mx[:, n, :]),
                                                ALU.subtract).then_inc((s["shift_q"], s["shift_k"])[n], 1)

                def f_softmax(f):
                    for n in range(2):
                        dve.wait_ge(s["exp_qk"], 2 * f + (n + 1))
                        nc.vector.tensor_reduce(out=zs[:, n, :], in_=ez[:, n], axis=AX.X, op=ALU.add).then_inc(s["links"], 1)
                    dve.wait_ge(s["links"], VECTOR_LINKS * f + 4)
                    nc.vector.reciprocal(rz[:, :, :], zs[:, :, :]).then_inc(s["links"], 1)
                    dve.wait_ge(s["exp_b"], f + 1)
                    nc.vector.tensor_scalar(beta[:, :], eb[:, :], 1.0, None, ALU.add).then_inc(s["links"], 1)
                    dve.wait_ge(s["links"], VECTOR_LINKS * f + 6)
                    nc.vector.reciprocal(beta[:, :], beta[:, :]).then_inc(s["links"], 1)
                    dve.wait_ge(s["links"], VECTOR_LINKS * f + 7)
                    nc.vector.tensor_tensor(rzb[:, :], beta[:, :], rz[:, 1, :], ALU.mult).then_inc(s["links"], 1)
                    nc.vector.tensor_tensor(qn[:, :, :], ez[:, 0], over_e(rz[:, 0, :]), ALU.mult)
                    nc.vector.tensor_tensor(kn[:, :, :], ez[:, 1], over_e(rz[:, 1, :]), ALU.mult)
                    dve.wait_ge(s["links"], VECTOR_LINKS * f + 8)
                    nc.vector.tensor_tensor(kb[:, :, :], ez[:, 1], over_e(rzb[:, :]), ALU.mult).then_inc(s["qkv_done"], 1)

                def f_value(f):
                    dve.wait_ge(s["v_mm"], f + 1)
                    nc.vector.tensor_tensor(vb[:, :, :], heads[2], over_e(beta[:, :]), ALU.mult).then_inc(s["vb_done"], 1)
                    dve.wait_ge(s["vb_done"], f + 1)
                    nc.vector.memset(mx[:, 0, :], 0.0).then_inc(s["links"], 1)

                f_norm(0)
                f_shift(0)
                f_softmax(0)
                f_value(0)

                def add_out(b):
                    dve.wait_ge(s["out_mm"], b)
                    nc.vector.tensor_tensor(tile(b - 1), out_ps, tile(b - 1), ALU.add).then_inc(s["out_done"], 1)

                def body(b, front, back):
                    def minus_at(Q):
                        dve.wait_ge(s["at_mm"], 2 * b + (Q + 1))
                        nc.vector.tensor_tensor(by_parity(MT, Q), both[Q][:, :, 0:2], mask4(MINUS_UPPER), ALU.mult).then_inc(s["minus_at"], 1)

                    def causal(Q):
                        nc.vector.tensor_tensor(by_parity(PT, Q), both[Q][:, :, 2:4], mask4(M_CAUSAL), ALU.mult).then_inc(s["pt_done"], 1)

                    def minus_a(Q):
                        nc.vector.tensor_tensor(by_parity(X, Q), a_ps[:, :, 2 * Q:2 * Q + 2], mask4(MINUS_SUB), ALU.mult).then_inc(s["minus_a"], 1)

                    def a_eye(Q):
                        dve.wait_ge(s["minus_a"], 2 * b + (Q + 1))
                        nc.vector.tensor_tensor(X[:, Q], X[:, Q], eye, ALU.add).then_inc(s["x2_done"], 1)

                    if front:
                        f_norm(b + 1)
                    dve.wait_ge(s["a_mm"], b + 1)
                    minus_a(0)
                    a_eye(0)
                    minus_a(1)
                    minus_at(0)
                    causal(0)
                    if back:
                        add_out(b)
                    minus_at(1)
                    causal(1)
                    a_eye(1)
                    for l in range(LEVELS):
                        for Q in range(2):
                            dve.wait_ge(s["y_mm"], 2 * LEVELS * b + (2 * l + Q + 1))
                            nc.vector.tensor_tensor(W[:, Q], B4[Q], mask(M_LEVEL + l), ALU.mult).then_inc(s["w_done"], 1)
                        if l == 0:
                            for Q in range(2):
                                nc.vector.tensor_tensor(by_parity(coff, Q), a_ps[:, :, 2 * Q:2 * Q + 2], mask4(M_OFF), ALU.mult).then_inc(s["coff_done"], 1)
                        if l == 1 and front:
                            f_shift(b + 1)
                        if l == 2 and front:
                            f_softmax(b + 1)
                    for Q in range(2):
                        dve.wait_ge(s["r_mm"], 2 * b + (Q + 1))
                        nc.vector.tensor_copy(R[:, Q], first[Q][:, 0:HQ * DH].rearrange("p (h e) -> p h e", h=HQ)).then_inc(s["r_done"], 1)
                    if front:
                        f_value(b + 1)
                    for k in range(3):
                        for Q in range(2):
                            at = HQ * DH * ((k + 1) % 2)
                            dve.wait_ge(s["u_mm"], 6 * b + (2 * k + Q + 1))
                            nc.vector.tensor_tensor(U[:, Q], first[Q][:, at:at + HQ * DH].rearrange("p (h e) -> p h e", h=HQ), R[:, Q],
                                                    ALU.add).then_inc(s["u_done"], 1)

                body(0, True, False)
                with dve.Fori(1, BATCH - 1) as b:
                    body(b, True, True)
                body(BATCH - 1, False, True)
                add_out(BATCH)
                dve.wait_ge(s["out_done"], BATCH)

            @block.tensor
            def _(pe):
                pe.wait_ge(s["w_in"], 96)

                def f_xT(f):
                    pe.wait_ge(s["xh_done"], f + 1)
                    nc.tensor.transpose(xT_ps, xh[:, :], m.ident).then_inc(s["xT_mm"], 1)

                def f_qk(f):
                    pe.wait_ge(s["hT_done"], f + 1)
                    for n, bank in enumerate((bq, bk)):
                        last = nc.tensor.matmul(bank[:, :], hT[:, :], wqkv[:, n, :], start=True, stop=True)
                    last.then_inc(s["qk_mm"], 1)

                def f_v(f):
                    pe.wait_ge(s["hT_done"], f + 1)
                    nc.tensor.matmul(beta_ps, hT[:, :], wb[:, :], start=True, stop=True)
                    nc.tensor.matmul(bv[:, :], hT[:, :], wqkv[:, 2, :], start=True, stop=True).then_inc(s["v_mm"], 1)

                def f_transposes(f):
                    pe.wait_ge(s["qkv_done"], f + 1)
                    for n, (src, dst) in enumerate(((kb, pairs[0]), (qn, pairs[1]), (kn, pairs[2]))):
                        if n == 2:
                            pe.wait_ge(s["vb_done"], f + 1)
                        for h in range(H // 2):
                            last = nc.tensor.transpose(dst[:, h, :], src[:, 2 * h:2 * h + 2, :].rearrange("p h e -> p (h e)"), m.ident)
                        last.then_inc(s["kT_mm"], 1)

                f_xT(0)
                f_qk(0)
                f_v(0)
                f_transposes(0)

                def output(b):
                    pe.wait_ge(s["o_done"], 2 * b)
                    for h in range(H // 2):
                        last = nc.tensor.matmul(out_ps, OT[:, h, :], wo[:, h, :], start=(h == 0), stop=(h == H // 2 - 1))
                    last.then_inc(s["out_mm"], 1)

                def body(b, front, back):
                    pe.wait_ge(s["kT_done"], 3 * b + 3)

                    def scores(Q, dst, at, left, right, sem):
                        for h in range(HQ):
                            lo, pr = DH * (h // 2), 2 * Q + h % 2
                            last = nc.tensor.matmul(dst[:, h // 2, at + h % 2, :], left[lo:lo + DH, pr, :], right[lo:lo + DH, pr, :],
                                                    start=True, stop=True)
                        if sem is not None:
                            last.then_inc(sem, 1)

                    scores(0, a_ps, 0, kbT, kT, None)
                    scores(1, a_ps, 2, kbT, kT, s["a_mm"])
                    if back:
                        pe.wait_ge(s["o_done"], 2 * b)
                    scores(0, both[0], 0, kT, kbT, None)
                    scores(0, both[0], 2, kT, qT, s["at_mm"])
                    if back:
                        pe.wait_ge(s["exp_b"], b + 1)
                        output(b)
                    scores(1, both[1], 0, kT, kbT, None)
                    scores(1, both[1], 2, kT, qT, s["at_mm"])
                    if front:
                        if back:
                            pe.wait_ge(s["out_done"], b)
                        f_xT(b + 1)
                    for l in range(LEVELS):
                        for Q in range(2):
                            if l == 0:
                                pe.wait_ge(s["i_minus_at"], 2 * b + (Q + 1))
                                pe.wait_ge(s["x2_done"], 2 * b + (Q + 1))
                                pe.wait_ge(s["pt_done"], 2 * b + (Q + 1))
                            else:
                                pe.wait_ge(s["x_done"], 2 * FULL * b + (2 * (l - 1) + Q + 1))
                            for h in range(HQ):
                                last = nc.tensor.matmul(B4[Q][:, h, :], MT[:, Q, h, :], X[:, Q, h, :], start=True, stop=True)
                            last.then_inc(s["y_mm"], 1)
                            if l == 0 and Q == 0 and front:
                                f_v(b + 1)
                        for Q in range(2):
                            pe.wait_ge(s["w_done"], 2 * LEVELS * b + (2 * l + Q + 1))
                            if l == 0:
                                pe.wait_ge(s["xt2_done"], 2 * b + (Q + 1))
                            else:
                                pe.wait_ge(s["xt_done"], 2 * LEVELS * b + (2 * (l - 1) + Q + 1))
                            for h in range(HQ):
                                last = nc.tensor.matmul(A4[Q][:, h, :], W[:, Q, h, :], XTs[l % 2][:, Q, h, :], start=True, stop=True)
                            last.then_inc(s["xt_mm"], 1)
                            if l < FULL:
                                for h in range(HQ):
                                    last = nc.tensor.matmul(B4[Q][:, h, :], XTs[l % 2][:, Q, h, :], W[:, Q, h, :], start=True, stop=True)
                                last.then_inc(s["x_mm"], 1)
                        if l == 0 and front:
                            pe.wait_ge(s["coff_done"], 2 * b + 2)
                            f_qk(b + 1)
                    for Q in range(2):
                        pe.wait_ge(s["xt_done"], 2 * LEVELS * b + (2 * FULL + Q + 1))
                        for h in range(HQ):
                            last = nc.tensor.matmul(B4[Q][:, h, :], coff[:, Q, h, :], XTs[0][:, Q, h, :], start=True, stop=True)
                        last.then_inc(s["bt_mm"], 1)
                        for h in range(HQ):
                            last = nc.tensor.matmul(first[Q][:, h * DH:(h + 1) * DH], XTs[0][:, Q, h, :], vb[:, HQ * Q + 2 * (h % 2) + h // 2, :], start=True, stop=True)
                        last.then_inc(s["r_mm"], 1)
                    for k in range(3):
                        for Q in range(2):
                            if k == 0:
                                pe.wait_ge(s["bt_done"], 2 * b + (Q + 1))
                                pe.wait_ge(s["r_done"], 2 * b + (Q + 1))
                            else:
                                pe.wait_ge(s["u_done"], 6 * b + (2 * (k - 1) + Q + 1))
                            at = HQ * DH * ((k + 1) % 2)
                            for h in range(HQ):
                                last = nc.tensor.matmul(first[Q][:, at + h * DH:at + (h + 1) * DH], nBT[:, Q, h, :],
                                                        (R if k == 0 else U)[:, Q, h, :], start=True, stop=True)
                            last.then_inc(s["u_mm"], 1)
                        if k == 0 and front:
                            f_transposes(b + 1)
                    for Q in range(2):
                        pe.wait_ge(s["u_done"], 6 * b + (4 + Q + 1))
                        for h in range(HQ):
                            lo = DH * (h // 2)
                            last = nc.tensor.matmul(B4[Q][lo:lo + DH, h % 2, :], U[:, Q, h, :], PT[:, Q, h, :], start=True, stop=True)
                        last.then_inc(s["o_mm"], 1)

                body(0, True, False)
                with pe.Fori(1, BATCH - 1) as b:
                    body(b, True, True)
                body(BATCH - 1, False, True)
                output(BATCH)
    close_semaphores(nc, s)


def attention_stage(nc, io, m):
    with nc.sbuf_tensor("res", [P, BATCH, D], FP32) as res:
        m.res = res
        attention_input_stage(nc, io, m)
        fast_weight_stage(nc, io, m, 0)
        ffn_stage(nc, io, m, "af", dict(ln_g=io["L0_attn_ff_ln_g"], ln_b=io["L0_attn_ff_ln_b"], w1=io["L0_attn_ff_w1"], b1=io["L0_attn_ff_b1"],
                                                   w2=io["L0_attn_ff_w2"], b2=io["L0_attn_ff_b2"]), res, res, ACT.Relu)
        fast_weight_stage(nc, io, m, 1)
        add_stage(nc, m, res)


def add_stage(nc, m, res):
    s = open_semaphores(nc, "added")
    with nc.Block() as block:
        @block.vector
        def _(dve):
            nc.vector.tensor_tensor(m.h[:, :, :], m.h[:, :, :], res[:, :, :], ALU.add).then_inc(s["added"], 1)
            dve.wait_ge(s["added"], 1)
    close_semaphores(nc, s)


DIN, NSTATE, NTAPS, DTR = 256, 16, 4, 32
HALVES = DIN // P


def recurrent_input_stage(nc, io, m):
    s = open_semaphores(nc, NORM_SEMS)
    with ExitStack() as mem:
        def sb(name, shape, dt=FP32):
            return mem.enter_context(nc.sbuf_tensor(name, shape, dt))
        n = norm_buffers(sb, "ri")
        bank4 = [k.rearrange("p (j c) -> p j c", j=GS) for k in m.bank]
        with nc.Block() as block:
            @block.gpsimd
            def _(pool):
                norm_pool(nc, pool, n, m, s, 0)

            @block.scalar
            def _(act):
                norm_scale(nc, act, lambda g: m.xT[:, g, :], lambda g: m.bank[g], None, s, 0)
                act.wait_ge(s["xT_done"], GROUPS)

            @block.vector
            def _(dve):
                norm_vector(nc, dve, lambda g: m.h[:, GS * g:GS * (g + 1), :], n, s, 0)

            @block.tensor
            def _(pe):
                norm_transpose(nc, pe, lambda g: bank4[g], n, m, s, 0)
    close_semaphores(nc, s)


def mamba_input_stage(nc, io, m, z, layer, src):
    s = open_semaphores(nc, "w_in padded in_mm in_done taps conv_done u_done")
    with ExitStack() as mem:
        def sb(name, shape, dt=FP32):
            return mem.enter_context(nc.sbuf_tensor("mi%d_%s" % (layer, name), shape, dt))
        w = sb("w", [P, 2 * DIN])
        cw = sb("cw", [P, HALVES, NTAPS])
        cb = sb("cb", [P, HALVES])
        xpad = sb("xpad", [P, HALVES, BATCH, P + NTAPS - 1])
        conv = sb("conv", [P, HALVES, BATCH, P])
        with nc.Block() as block:
            @block.sync
            def _(sp):
                for dst, a in [(w[:, :], io["L1_attn_in_proj_w"][layer]), (cw[:, :, :], io["L1_attn_conv_w"][layer]),
                               (cb[:, :], io["L1_attn_conv_b"][layer])]:
                    sp.dma_start(dst, a).then_inc(s["w_in"], 16)

            @block.gpsimd
            def _(pool):
                nc.gpsimd.memset(xpad[:, :, :, 0:NTAPS - 1], 0.0).then_inc(s["padded"], 1)

            @block.tensor
            def _(pe):
                pe.wait_ge(s["w_in"], 48)
                for g in range(GROUPS):
                    for c in range(2 * HALVES):
                        if g >= 2:
                            pe.wait_ge(s["in_done"], 4 * (g - 2) + c + 1)
                        nc.tensor.matmul(m.bank[4 * (g % 2) + c], w[:, c * P:(c + 1) * P], src[:, g, :], start=True,
                                         stop=True).then_inc(s["in_mm"], 1)

            @block.scalar
            def _(act):
                for g in range(GROUPS):
                    for c in range(2 * HALVES):
                        act.wait_ge(s["in_mm"], 4 * g + c + 1)
                        bank = m.bank[4 * (g % 2) + c]
                        if c < HALVES:
                            nc.scalar.activation(xpad[:, c, GS * g:GS * (g + 1), NTAPS - 1:], bank.rearrange("p (j c) -> p j c", j=GS),
                                                 ACT.Copy).then_inc(s["in_done"], 1)
                        else:
                            nc.scalar.activation(z["gate"][:, c - HALVES, g * GT:(g + 1) * GT], bank, ACT.Silu).then_inc(s["in_done"], 1)
                for g in range(GROUPS):
                    act.wait_ge(s["conv_done"], g + 1)
                    nc.scalar.activation(z["u"][:, :, g * GT:(g + 1) * GT],
                                         conv[:, :, GS * g:GS * (g + 1), :].rearrange("p f j c -> p f (j c)"), ACT.Silu).then_inc(s["u_done"], 1)
                act.wait_ge(s["u_done"], GROUPS)

            @block.vector
            def _(dve):
                dve.wait_ge(s["w_in"], 48)
                dve.wait_ge(s["padded"], 1)
                for g in range(GROUPS):
                    seqs = slice(GS * g, GS * (g + 1))
                    dve.wait_ge(s["in_done"], 4 * g + HALVES)
                    for k in range(NTAPS):
                        if k > 0:
                            dve.wait_ge(s["taps"], (NTAPS - 1) * g + k)
                        for f in range(HALVES):
                            tap = xpad[:, f, seqs, k:k + P]
                            if k == 0:
                                last = nc.vector.tensor_scalar(conv[:, f, seqs, :], tap, cw[:, f, 0:1], cb[:, f:f + 1], ALU.mult, ALU.add)
                            else:
                                last = nc.vector.scalar_tensor_tensor(out=conv[:, f, seqs, :], in0=tap, scalar=cw[:, f, k:k + 1],
                                                                      in1=conv[:, f, seqs, :], op0=ALU.mult, op1=ALU.add)
                        last.then_inc(s["conv_done"] if k == NTAPS - 1 else s["taps"], 1)
    close_semaphores(nc, s)


def mamba_step_size_stage(nc, io, m, z, layer):
    s = open_semaphores(nc, "w_in dbl_mm dtin_done hi_done rest_done mid_done split_done dt_mm x_done abs_done exp_done ln_done "
                            "w_done d_done t_done dt_done a_exp dtu_done")
    with ExitStack() as mem:
        def sb(name, shape, dt=FP32):
            return mem.enter_context(nc.sbuf_tensor("ms%d_%s" % (layer, name), shape, dt))
        xw = sb("xw", [P, HALVES, DTR + 2 * NSTATE])
        dw = sb("dw", [DTR, DIN])
        db = sb("db", [P, HALVES])
        dtin = sb("dtin", [DTR, GROUPS, GT])
        rest = sb("rest", [32, GROUPS, GT])
        e = sb("e", [P, HALVES, BATCH * P])
        w = sb("w", [P, HALVES, BATCH * P])
        ln = sb("ln", [P, HALVES, BATCH * P])
        with nc.Block() as block:
            @block.sync
            def _(sp):
                for dst, a in [(xw[:, :, :], io["L1_attn_x_proj_w"][layer]), (dw[:, :], io["L1_attn_dt_proj_w"][layer]),
                               (db[:, :], io["L1_attn_dt_proj_b"][layer]), (z["a"][:, :, :], io["L1_attn_A_log"][layer])]:
                    sp.dma_start(dst, a).then_inc(s["w_in"], 16)

            @block.tensor
            def _(pe):
                pe.wait_ge(s["w_in"], 64)
                for g in range(GROUPS):
                    for f in range(HALVES):
                        last = nc.tensor.matmul(m.bank[g][0:DTR + 2 * NSTATE, :], xw[:, f, :], z["u"][:, f, g * GT:(g + 1) * GT],
                                                start=(f == 0), stop=(f == HALVES - 1))
                    last.then_inc(s["dbl_mm"], 1)
                for f in range(HALVES):
                    for g in range(GROUPS):
                        if f == 0:
                            pe.wait_ge(s["dtin_done"], g + 1)
                        else:
                            pe.wait_ge(s["x_done"], g + 1)
                        nc.tensor.matmul(m.bank[4 + g], dw[:, f * P:(f + 1) * P], dtin[:, g, :], start=True, stop=True).then_inc(s["dt_mm"], 1)

            @block.scalar
            def _(act):
                act.wait_ge(s["w_in"], 64)
                nc.scalar.activation(z["a"][:, :, :], z["a"][:, :, :], ACT.Exp).then_inc(s["a_exp"], 1)
                for g in range(GROUPS):
                    act.wait_ge(s["dbl_mm"], g + 1)
                    nc.scalar.activation(dtin[:, g, :], m.bank[g][0:DTR, :], ACT.Copy).then_inc(s["dtin_done"], 1)
                for f in range(HALVES):
                    for g in range(GROUPS):
                        act.wait_ge(s["dt_mm"], GROUPS * f + g + 1)
                        nc.scalar.activation(z["dt"][:, f, g * GT:(g + 1) * GT], m.bank[4 + g], ACT.Identity,
                                             bias=db[:, f:f + 1]).then_inc(s["x_done"], 1)
                for f in range(HALVES):
                    act.wait_ge(s["x_done"], GROUPS * (f + 1))
                    nc.scalar.activation(e[:, f, :], z["dt"][:, f, :], ACT.Abs).then_inc(s["abs_done"], 1)
                    act.wait_ge(s["abs_done"], f + 1)
                    nc.scalar.activation(e[:, f, :], e[:, f, :], ACT.Exp, scale=-1.0).then_inc(s["exp_done"], 1)
                    act.wait_ge(s["exp_done"], f + 1)
                    nc.scalar.activation(ln[:, f, :], e[:, f, :], ACT.Ln, bias=m.ones_col[:, 0:1]).then_inc(s["ln_done"], 1)

            @block.vector
            def _(dve):
                dve.wait_ge(s["a_exp"], 1)
                nc.vector.tensor_scalar(z["a"][:, :, :], z["a"][:, :, :], -1.0, None, ALU.mult).then_inc(s["a_exp"], 1)
                dve.wait_ge(s["a_exp"], 2)
                for g in range(GROUPS):
                    dve.wait_ge(s["dbl_mm"], g + 1)
                    nc.vector.tensor_copy(z["bc"][32:64, g, :], m.bank[g][32:64, :]).then_inc(s["hi_done"], 1)
                    dve.wait_ge(s["hi_done"], g + 1)
                    nc.vector.tensor_tensor(rest[:, g, :], m.bank[g][32:64, :], z["bc"][32:64, g, :], ALU.subtract).then_inc(s["rest_done"], 1)
                    dve.wait_ge(s["rest_done"], g + 1)
                    nc.vector.tensor_copy(z["bc"][0:32, g, :], rest[:, g, :]).then_inc(s["mid_done"], 1)
                    dve.wait_ge(s["mid_done"], g + 1)
                    nc.vector.tensor_tensor(z["bc"][64:96, g, :], rest[:, g, :], z["bc"][0:32, g, :], ALU.subtract).then_inc(s["split_done"], 1)
                dve.wait_ge(s["split_done"], GROUPS)
                for f in range(HALVES):
                    dve.wait_ge(s["exp_done"], f + 1)
                    nc.vector.tensor_scalar(w[:, f, :], e[:, f, :], 1.0, -1.0, ALU.add, ALU.add).then_inc(s["w_done"], 1)
                    dve.wait_ge(s["w_done"], f + 1)
                    dve.wait_ge(s["ln_done"], f + 1)
                    nc.vector.tensor_tensor(e[:, f, :], e[:, f, :], w[:, f, :], ALU.subtract)
                    nc.vector.scalar_tensor_tensor(out=ln[:, f, :], in0=w[:, f, :], scalar=0.0, in1=ln[:, f, :], op0=ALU.is_gt,
                                                   op1=ALU.mult).then_inc(s["d_done"], 1)
                    dve.wait_ge(s["d_done"], f + 1)
                    nc.vector.tensor_tensor(w[:, f, :], ln[:, f, :], e[:, f, :], ALU.add).then_inc(s["t_done"], 1)
                    dve.wait_ge(s["t_done"], f + 1)
                    nc.vector.scalar_tensor_tensor(out=z["dt"][:, f, :], in0=z["dt"][:, f, :], scalar=0.0, in1=w[:, f, :], op0=ALU.max,
                                                   op1=ALU.add).then_inc(s["dt_done"], 1)
                dve.wait_ge(s["dt_done"], HALVES)

            @block.gpsimd
            def _(pool):
                for f in range(HALVES):
                    pool.wait_ge(s["dt_done"], f + 1)
                    nc.gpsimd.tensor_tensor(z["dtu"][:, f, :], z["dt"][:, f, :], z["u"][:, f, :], ALU.mult).then_inc(s["dtu_done"], 1)
                pool.wait_ge(s["dtu_done"], HALVES)
    close_semaphores(nc, s)


def mamba_scan_stage(nc, io, m, z, layer):
    CHUNKS = 2
    CS = BATCH // CHUNKS
    CT = CS * P
    SCAN_CREDIT, HC_CREDIT, Y_CREDIT, DBU_CREDIT, COPY_CREDIT = 2, 4, 2, 2, 1
    s = open_semaphores(nc, "w_in zeroed b_mm c_mm c_copied decay_done dbu_done scan_done hc_done y_mm y_done")
    with ExitStack() as mem:
        def sb(name, shape, dt=FP32):
            return mem.enter_context(nc.sbuf_tensor("mc%d_%s" % (layer, name), shape, dt))
        dparam = sb("dparam", [P, HALVES])
        zeros = sb("zeros", [P, 512], BF16)
        decay = sb("decay", [P, HALVES, CS, P])
        dbu = sb("dbu", [P, HALVES, CT])
        states = sb("states", [P, HALVES, CT])
        hc = sb("hc", [P, HALVES, CT])
        c_sb = sb("c_sb", [P, 2, CT])
        b_ps = m.psum[:, 0:2, :].rearrange("p a b -> p (a b)")
        c_ps = m.psum[:, 2:4, :].rearrange("p a b -> p (a b)")
        y_ps = [m.psum[:, 4 + 2 * f:6 + 2 * f, :].rearrange("p a b -> p (a b)") for f in range(HALVES)]
        dt4 = z["dt"][:, :, :].rearrange("p f (b t) -> p f b t", b=BATCH)
        bc = z["bc"][:, :, :].rearrange("p g t -> p (g t)")
        with nc.Block() as block:
            @block.sync
            def _(sp):
                sp.dma_start(dparam[:, :], io["L1_attn_D_param"][layer]).then_inc(s["w_in"], 16)

            @block.gpsimd
            def _(pool):
                nc.gpsimd.memset(zeros[:, :], 0.0)
                nc.gpsimd.memset(decay[:, :, :, 0:1], 0.0).then_inc(s["zeroed"], 1)
                pool.sem_inc(s["hc_done"], HC_CREDIT)
                with pool.Fori(0, CHUNKS) as c, pool.Fori(0, NSTATE // 2) as i:
                    for u in range(2):
                        step = c * NSTATE + i * 2 + u
                        for f in range(HALVES):
                            half = c * (2 * NSTATE) + i * 4 + (2 * u + f)
                            pool.wait_ge(s["c_copied"], step + (COPY_CREDIT + 1))
                            pool.wait_ge(s["y_mm"], half + (Y_CREDIT - 1))
                            pool.wait_ge(s["scan_done"], half + (SCAN_CREDIT + 1))
                            nc.gpsimd.tensor_tensor(hc[:, f, :], states[:, f, :], c_sb[:, u, :], ALU.mult).then_inc(s["hc_done"], 1)

            @block.scalar
            def _(act):
                act.wait_ge(s["zeroed"], 1)
                act.sem_inc(s["c_copied"], COPY_CREDIT)
                with act.Fori(0, CHUNKS) as c, act.Fori(0, NSTATE // 2) as i:
                    for u in range(2):
                        step = c * NSTATE + i * 2 + u
                        for f in range(HALVES):
                            half = c * (2 * NSTATE) + i * 4 + (2 * u + f)
                            act.wait_ge(s["scan_done"], half + (SCAN_CREDIT - 1))
                            nc.scalar.activation(decay[:, f, :, 1:P], dt4[:, f, ds(c * CS, CS), 1:P], ACT.Exp,
                                                 scale=z["a"][:, f, ds(i * 2 + u, 1)]).then_inc(s["decay_done"], 1)
                        act.wait_ge(s["c_mm"], step + 1)
                        act.wait_ge(s["hc_done"], step * 2 + (HC_CREDIT - 2))
                        nc.scalar.activation(c_sb[:, u, :], c_ps, ACT.Copy).then_inc(s["c_copied"], 1)

            @block.vector
            def _(dve):
                dve.wait_ge(s["w_in"], 16)
                dve.sem_inc(s["dbu_done"], DBU_CREDIT)
                dve.sem_inc(s["scan_done"], SCAN_CREDIT)
                dve.sem_inc(s["y_done"], HALVES)
                with dve.Fori(0, CHUNKS) as c:
                    with dve.Fori(0, NSTATE // 2) as i:
                        for u in range(2):
                            step = c * NSTATE + i * 2 + u
                            for f in range(HALVES):
                                half = c * (2 * NSTATE) + i * 4 + (2 * u + f)
                                dve.wait_ge(s["b_mm"], step + 1)
                                nc.vector.tensor_tensor(dbu[:, f, :], b_ps, z["dtu"][:, f, ds(c * CT, CT)],
                                                        ALU.mult).then_inc(s["dbu_done"], 1)
                                dve.wait_ge(s["decay_done"], half + 1)
                                dve.wait_ge(s["hc_done"], half + (HC_CREDIT - 1))
                                dve.wait_ge(s["dbu_done"], half + (DBU_CREDIT + 1))
                                nc.vector.tensor_tensor_scan(out=states[:, f, :], data0=decay[:, f, :, :].rearrange("p b t -> p (b t)"),
                                                             data1=dbu[:, f, :], initial=0.0, op0=ALU.mult,
                                                             op1=ALU.add).then_inc(s["scan_done"], 1)
                    dve.wait_ge(s["y_mm"], c * (2 * NSTATE) + (2 * NSTATE + Y_CREDIT))
                    for f in range(HALVES):
                        nc.vector.scalar_tensor_tensor(out=z["y"][:, f, ds(c * CT, CT)], in0=z["u"][:, f, ds(c * CT, CT)],
                                                       scalar=dparam[:, f:f + 1], in1=y_ps[f], op0=ALU.mult,
                                                       op1=ALU.add).then_inc(s["y_done"], 1)
                dve.wait_ge(s["y_done"], HALVES + HALVES * CHUNKS)

            @block.tensor
            def _(pe):
                pe.wait_ge(s["zeroed"], 1)
                pe.sem_inc(s["y_mm"], Y_CREDIT)

                def broadcast(c, step, n):
                    pe.wait_ge(s["dbu_done"], step * 2 + DBU_CREDIT)
                    for k in range(2):
                        last = nc.tensor.matmul(b_ps[:, k * 512:(k + 1) * 512], m.select[:, ds(n, 1), :].rearrange("p o c -> p (o c)"),
                                                bc[0:96, ds(c * CT + k * 512, 512)], start=True, stop=True)
                    last.then_inc(s["b_mm"], 1)
                    pe.wait_ge(s["c_copied"], step + COPY_CREDIT)
                    for k in range(2):
                        last = nc.tensor.matmul(c_ps[:, k * 512:(k + 1) * 512], m.select[:, ds(n + NSTATE, 1), :].rearrange("p o c -> p (o c)"),
                                                bc[0:96, ds(c * CT + k * 512, 512)], start=True, stop=True)
                    last.then_inc(s["c_mm"], 1)

                def accumulate(half):
                    for f in range(HALVES):
                        pe.wait_ge(s["hc_done"], half + (f + HC_CREDIT + 1))
                        for k in range(2):
                            last = nc.tensor.matmul(y_ps[f][:, k * 512:(k + 1) * 512], m.ident, hc[:, f, k * 512:(k + 1) * 512],
                                                    start=False, stop=False, skip_group_check=True)
                        last.then_inc(s["y_mm"], 1)

                with pe.Fori(0, CHUNKS) as c:
                    pe.wait_ge(s["y_done"], c * HALVES + HALVES)
                    for k in range(2 * HALVES):
                        nc.tensor.matmul(m.bank[4 + k], zeros[:, 0:P], zeros[:, :], start=True, stop=False, skip_group_check=True)
                    broadcast(c, c * NSTATE, c * 0)
                    with pe.Fori(0, NSTATE // 2 - 1) as i:
                        for u in range(2):
                            broadcast(c, c * NSTATE + i * 2 + (u + 1), i * 2 + (u + 1))
                            accumulate(c * (2 * NSTATE) + i * 4 + 2 * u)
                    last_two = NSTATE - 2
                    broadcast(c, c * NSTATE + (last_two + 1), c * 0 + (last_two + 1))
                    accumulate(c * (2 * NSTATE) + 2 * last_two)
                    accumulate(c * (2 * NSTATE) + 2 * (last_two + 1))
    close_semaphores(nc, s)


def mamba_output_stage(nc, io, m, z, layer, src):
    s = open_semaphores(nc, NORM_SEMS + "w_in gated out_mm")
    with ExitStack() as mem:
        def sb(name, shape, dt=FP32):
            return mem.enter_context(nc.sbuf_tensor("mo%d_%s" % (layer, name), shape, dt))
        w = sb("w", [P, HALVES, D])
        gb = sb("gb", [P, 2])
        n = norm_buffers(sb, "mo%d" % layer)
        bank4 = [k.rearrange("p (j c) -> p j c", j=GS) for k in m.bank]
        with nc.Block() as block:
            @block.sync
            def _(sp):
                for dst, a in [(w[:, :, :], io["L1_attn_out_proj_w"][layer]), (gb[:, 0:1], io["L1_attn_ln_g"][layer]),
                               (gb[:, 1:2], io["L1_attn_ln_b"][layer])]:
                    sp.dma_start(dst, a).then_inc(s["w_in"], 16)

            @block.gpsimd
            def _(pool):
                norm_pool(nc, pool, n, m, s, 0)

            @block.scalar
            def _(act):
                act.wait_ge(s["w_in"], 48)
                norm_scale(nc, act, lambda g: m.mT[:, g, :], lambda g: m.bank[2 * g], gb, s, 0)
                act.wait_ge(s["xT_done"], GROUPS)

            @block.vector
            def _(dve):
                for g in range(GROUPS):
                    cols = slice(g * GT, (g + 1) * GT)
                    nc.vector.tensor_tensor(z["y"][:, :, cols], z["y"][:, :, cols], z["gate"][:, :, cols], ALU.mult).then_inc(s["gated"], 1)
                for g in range(1):
                    dve.wait_ge(s["out_mm"], GROUPS)
                norm_vector(nc, dve, lambda g: bank4[2 * g + 1], n, s, 0)

            @block.tensor
            def _(pe):
                pe.wait_ge(s["w_in"], 48)
                for g in range(GROUPS):
                    pe.wait_ge(s["gated"], g + 1)
                    for j in range(GS):
                        cols = slice(g * GT + j * P, g * GT + (j + 1) * P)
                        for f in range(HALVES):
                            nc.tensor.matmul(bank4[2 * g + 1][:, j, :], z["y"][:, f, cols], w[:, f, :], start=(f == 0), stop=False)
                        last = nc.tensor.matmul(bank4[2 * g + 1][:, j, :], src[:, g, j * P:(j + 1) * P], m.ident, start=False, stop=True)
                    last.then_inc(s["out_mm"], 1)
                norm_transpose(nc, pe, lambda g: bank4[2 * g], n, m, s, 0)
    close_semaphores(nc, s)


def lstm_stage(nc, io, m):
    GATES, HD = 4, 64
    UNROLL = 4
    CELL = 2
    s = open_semaphores(nc, "w_in scaled bias_done zeroed g_mm g_done step_mm gates_done in_part f_part cell_done tanh_done hidden_done out_done")
    with ExitStack() as mem:
        def sb(name, shape, dt=FP32):
            return mem.enter_context(nc.sbuf_tensor("ls_" + name, shape, dt))
        wih = sb("wih", [P, 2, GATES * HD])
        whh = sb("whh", [P, GATES, P])
        bias = sb("bias", [P, 2, GATES])
        bsum = sb("bsum", [P, GATES])
        pre = sb("pre", [P, P, GATES, BATCH])
        hs = sb("hs", [P, P + 1, BATCH])
        gates = sb("gates", [P, GATES, BATCH])
        cell, part_f, part_i, tc = (sb(x, [P, BATCH]) for x in ("cell", "part_f", "part_i", "tc"))
        step_ps = [m.bank[6][:, 0:GATES * BATCH], m.bank[7][:, 0:GATES * BATCH]]
        with nc.Block() as block:
            @block.sync
            def _(sp):
                for dst, a in [(wih[:, :, :], io["lstm_w_ih"]), (whh[:, :, :], io["lstm_w_hh"]), (bias[:, :, :], io["lstm_bias"])]:
                    sp.dma_start(dst, a).then_inc(s["w_in"], 16)

            @block.gpsimd
            def _(pool):
                nc.gpsimd.memset(hs[:, 0:1, :], 0.0)
                nc.gpsimd.memset(cell[:, :], 0.0).then_inc(s["zeroed"], 1)

            @block.scalar
            def _(act):
                act.wait_ge(s["bias_done"], 2)
                for g in range(GROUPS):
                    for q in range(GATES):
                        act.wait_ge(s["g_mm"], GATES * g + q + 1)
                        bank = m.bank[q][:, :].rearrange("p (b t) -> p b t", b=GS)
                        for d in range(2):
                            rows = slice(HD * d, HD * (d + 1))
                            dst = pre[rows, :, q, GS * g:GS * (g + 1)].rearrange("p t b -> p b t")
                            if d == 1:
                                dst = dst[:, :, ::-1]
                            last = nc.scalar.activation(dst, bank[rows], ACT.Identity, bias=bsum[rows, q:q + 1],
                                                        scale=1.0 if q == CELL else 0.5)
                        last.then_inc(s["g_done"], 1)
                with act.Fori(0, P // UNROLL) as i:
                    for u in range(UNROLL):
                        act.wait_ge(s["step_mm"], i * UNROLL + (u + 1))
                        nc.scalar.activation(gates[:, :, :].rearrange("p q b -> p (q b)"), step_ps[u % 2], ACT.Tanh).then_inc(s["gates_done"], 1)
                        act.wait_ge(s["cell_done"], i * UNROLL + (u + 1))
                        nc.scalar.activation(tc[:, :], cell[:, :], ACT.Tanh, scale=0.5).then_inc(s["tanh_done"], 1)

            @block.vector
            def _(dve):
                dve.wait_ge(s["w_in"], 48)
                for q in range(GATES):
                    last = nc.vector.tensor_scalar(whh[:, q, :], whh[:, q, :], 0.5 if q == CELL else 0.25, None, ALU.mult)
                last.then_inc(s["scaled"], 1)
                nc.vector.tensor_tensor(bsum[:, :], bias[:, 0, :], bias[:, 1, :], ALU.add).then_inc(s["bias_done"], 1)
                dve.wait_ge(s["bias_done"], 1)
                for q in range(GATES):
                    last = nc.vector.tensor_scalar(bsum[:, q:q + 1], bsum[:, q:q + 1], 1.0 if q == CELL else 0.5, None, ALU.mult)
                last.then_inc(s["bias_done"], 1)
                dve.wait_ge(s["zeroed"], 1)
                with dve.Fori(0, P // UNROLL) as i:
                    for u in range(UNROLL):
                        at = i * UNROLL + (u + 1)
                        dve.wait_ge(s["gates_done"], at)
                        nc.vector.scalar_tensor_tensor(out=part_f[:, :], in0=gates[:, 1, :], scalar=1.0, in1=cell[:, :], op0=ALU.add,
                                                       op1=ALU.mult).then_inc(s["f_part"], 1)
                        nc.vector.scalar_tensor_tensor(out=part_i[:, :], in0=gates[:, 0, :], scalar=1.0, in1=gates[:, 2, :], op0=ALU.add,
                                                       op1=ALU.mult).then_inc(s["in_part"], 1)
                        dve.wait_ge(s["in_part"], at)
                        nc.vector.scalar_tensor_tensor(out=cell[:, :], in0=part_f[:, :], scalar=0.5, in1=part_i[:, :], op0=ALU.mult,
                                                       op1=ALU.add).then_inc(s["cell_done"], 1)
                        dve.wait_ge(s["tanh_done"], at)
                        nc.vector.scalar_tensor_tensor(out=hs[:, ds(at, 1), :].rearrange("p o b -> p (o b)"), in0=gates[:, 3, :], scalar=1.0,
                                                       in1=tc[:, :], op0=ALU.add, op1=ALU.mult).then_inc(s["hidden_done"], 1)
                dve.wait_ge(s["hidden_done"], P + 1)
                by_seq = m.lstmT[:, :].rearrange("p (b t) -> p b t", b=BATCH)
                nc.vector.tensor_scalar(by_seq[0:HD], hs[0:HD, 1:P + 1, :].rearrange("p t b -> p b t"), 0.5, None, ALU.mult)
                nc.vector.tensor_scalar(by_seq[HD:P, :, ::-1], hs[HD:P, 1:P + 1, :].rearrange("p t b -> p b t"), 0.5, None,
                                        ALU.mult).then_inc(s["out_done"], 1)
                dve.wait_ge(s["out_done"], 1)

            @block.tensor
            def _(pe):
                pe.wait_ge(s["w_in"], 48)
                for g in range(GROUPS):
                    for q in range(GATES):
                        if g > 0:
                            pe.wait_ge(s["g_done"], GATES * (g - 1) + q + 1)
                        for d in range(2):
                            last = nc.tensor.matmul(m.bank[q][HD * d:HD * (d + 1), :], wih[:, d, q * HD:(q + 1) * HD], m.xT[:, g, :],
                                                    start=True, stop=True)
                        last.then_inc(s["g_mm"], 1)
                pe.wait_ge(s["g_done"], GATES * GROUPS)
                pe.wait_ge(s["scaled"], 1)
                pe.wait_ge(s["zeroed"], 1)
                pe.sem_inc(s["hidden_done"], 1)
                with pe.Fori(0, P // UNROLL) as i:
                    for u in range(UNROLL):
                        nc.tensor.matmul(step_ps[u % 2], m.ident, pre[:, ds(i * UNROLL + u, 1), :, :].rearrange("p o q b -> p (o q b)"),
                                         start=True, stop=False, skip_group_check=True)
                        pe.wait_ge(s["hidden_done"], i * UNROLL + (u + 1))
                        for q in range(GATES):
                            last = nc.tensor.matmul(step_ps[u % 2][:, q * BATCH:(q + 1) * BATCH], whh[:, q, :],
                                                    hs[:, ds(i * UNROLL + u, 1), :].rearrange("p o b -> p (o b)"),
                                                    start=False, stop=(q == GATES - 1), skip_group_check=True)
                        last.then_inc(s["step_mm"], 1)
    close_semaphores(nc, s)


def fusion_stage(nc, io, m):
    s = open_semaphores(nc, "w_in out_mm added")
    with ExitStack() as mem:
        w = mem.enter_context(nc.sbuf_tensor("fu_w", [P, 2, D], FP32))
        b = mem.enter_context(nc.sbuf_tensor("fu_b", [1, D], FP32))
        bank4 = [k.rearrange("p (j c) -> p j c", j=GS) for k in m.bank]
        with nc.Block() as block:
            @block.sync
            def _(sp):
                sp.dma_start(w[:, :, :], io["L1_attn_fusion_w"]).then_inc(s["w_in"], 16)
                sp.dma_start(b[:, :], io["L1_attn_fusion_b"]).then_inc(s["w_in"], 16)

            @block.vector
            def _(dve):
                for g in range(GROUPS):
                    dve.wait_ge(s["out_mm"], g + 1)
                    seqs = slice(GS * g, GS * (g + 1))
                    nc.vector.tensor_tensor(m.h[:, seqs, :], m.h[:, seqs, :], bank4[g], ALU.add).then_inc(s["added"], 1)
                dve.wait_ge(s["added"], GROUPS)

            @block.tensor
            def _(pe):
                pe.wait_ge(s["w_in"], 32)
                for g in range(GROUPS):
                    for j in range(GS):
                        cols = slice(j * P, (j + 1) * P)
                        nc.tensor.matmul(bank4[g][:, j, :], m.ones_row[0:1, 0:P], b[:, :], start=True, stop=False)
                        nc.tensor.matmul(bank4[g][:, j, :], m.mT[:, g, cols], w[:, 0, :], start=False, stop=False)
                        last = nc.tensor.matmul(bank4[g][:, j, :], m.lstmT[:, g * GT + j * P:g * GT + (j + 1) * P], w[:, 1, :],
                                                start=False, stop=True)
                    last.then_inc(s["out_mm"], 1)
    close_semaphores(nc, s)


def recurrent_stage(nc, io, m):
    with ExitStack() as mem:
        def sb(name, shape, dt=FP32):
            return mem.enter_context(nc.sbuf_tensor(name, shape, dt))
        m.xT = sb("xT", [P, GROUPS, GT])
        m.mT = sb("mT", [P, GROUPS, GT])
        m.lstmT = sb("lstmT", [P, BATCH * P])
        recurrent_input_stage(nc, io, m)
        lstm_stage(nc, io, m)
        with ExitStack() as inner:
            def sbi(name, shape, dt=FP32):
                return inner.enter_context(nc.sbuf_tensor(name, shape, dt))
            m.select = sbi("select", [96, 2 * NSTATE, P], BF16)
            z = dict(u=sbi("u", [P, HALVES, BATCH * P]), gate=sbi("gate", [P, HALVES, BATCH * P]),
                                dt=sbi("dt", [P, HALVES, BATCH * P]), dtu=sbi("dtu", [P, HALVES, BATCH * P]),
                                y=sbi("y", [P, HALVES, BATCH * P]), a=sbi("a", [P, HALVES, NSTATE]),
                                bc=sbi("bc", [96, GROUPS, GT], BF16))
            selector_stage(nc, io, m)
            for layer in range(3):
                src = m.xT if layer == 0 else m.mT
                mamba_input_stage(nc, io, m, z, layer, src)
                mamba_step_size_stage(nc, io, m, z, layer)
                mamba_scan_stage(nc, io, m, z, layer)
                mamba_output_stage(nc, io, m, z, layer, src)
        fusion_stage(nc, io, m)


def selector_stage(nc, io, m):
    s = open_semaphores(nc, "w_in made")
    with nc.sbuf_tensor("which", [96, 2 * NSTATE], FP32) as which:
        with nc.Block() as block:
            @block.sync
            def _(sp):
                sp.dma_start(which[:, :], io["selector"]).then_inc(s["w_in"], 16)

            @block.vector
            def _(dve):
                dve.wait_ge(s["w_in"], 16)
                nc.vector.tensor_copy(m.select[:, :, :], which[:, :].unsqueeze(2).to_broadcast([96, 2 * NSTATE, P])).then_inc(s["made"], 1)
                dve.wait_ge(s["made"], 1)
    close_semaphores(nc, s)



SLOT_TILE = 256


def routing_buffers(sb, tag, experts):
    n = BATCH
    return dict(
        E=experts, scores=sb(tag + "_scores", [P, n, experts]), top=sb(tag + "_top", [P, n, 8]),
        index=sb(tag + "_index", [P, n, 8], U32), indexf=sb(tag + "_indexf", [P, 2, n]),
        chosen=[sb(tag + "_chosen%d" % k, [P, n, experts]) for k in range(2)], both=sb(tag + "_both", [P, n, experts]),
        before=sb(tag + "_before", [P, n + 1, experts]), place=sb(tag + "_place", [P, n, experts]),
        product=sb(tag + "_product", [P, n, experts]), pos=sb(tag + "_pos", [P, 2, n]),
        iota=sb(tag + "_iota", [P, experts]), earlier=sb(tag + "_earlier", [P, P]), ones=sb(tag + "_ones", [P, P]))


def choose_two(nc, dve, r, s):
    n, E = BATCH, r["E"]
    for b in range(n):
        last = nc.vector.max(out=r["top"][:, b, :], in_=r["scores"][:, b, :])
    last.then_inc(s["top_done"], 1)
    dve.wait_ge(s["top_done"], 1)
    for b in range(n):
        last = nc.vector.max_index(r["index"][:, b, :], r["top"][:, b, :], r["scores"][:, b, :])
    last.then_inc(s["index_done"], 1)
    dve.wait_ge(s["index_done"], 1)
    nc.vector.tensor_copy(r["indexf"][:, :, :], r["index"][:, :, 0:2].rearrange("p n k -> p k n")).then_inc(s["indexf_done"], 1)
    dve.wait_ge(s["indexf_done"], 1)
    for k in range(2):
        last = nc.vector.tensor_tensor(r["chosen"][k][:, :, :], r["iota"][:, :].unsqueeze(1).to_broadcast([P, n, E]),
                                       r["indexf"][:, k, :].unsqueeze(2).to_broadcast([P, n, E]), ALU.is_equal)
    last.then_inc(s["chosen_done"], 1)
    nc.vector.memset(r["before"][:, 0, :], 0.0).then_inc(s["before_done"], 1)
    dve.wait_ge(s["chosen_done"], 1)
    nc.vector.tensor_tensor(r["both"][:, :, :], r["chosen"][0][:, :, :], r["chosen"][1][:, :, :], ALU.add).then_inc(s["both_done"], 1)
    dve.wait_ge(s["both_done"], 1)
    for b in range(n):
        dve.wait_ge(s["before_done"], b + 1)
        nc.vector.tensor_tensor(r["before"][:, b + 1, :], r["before"][:, b, :], r["both"][:, b, :], ALU.add).then_inc(s["before_done"], 1)


def count_earlier(nc, pe, r, dst, s):
    pe.wait_ge(s["before_done"], BATCH + 1)
    for b in range(BATCH):
        nc.tensor.matmul(dst[:, b, :], r["earlier"][:, :], r["both"][:, b, :], start=True, stop=False, skip_group_check=True)
        last = nc.tensor.matmul(dst[:, b, :], r["ones"][:, :], r["before"][:, b, :], start=False, stop=True, skip_group_check=True)
    last.then_inc(s["count_mm"], 1)


def pick(nc, dve, r, table, s, base):
    for k in range(2):
        if k > 0:
            dve.wait_ge(s["picked"], base + k)
        nc.vector.tensor_tensor(r["product"][:, :, :], r["chosen"][k][:, :, :], table, ALU.mult).then_inc(s["product_done"], 1)
        dve.wait_ge(s["product_done"], base + k + 1)
        nc.vector.tensor_reduce(out=r["pos"][:, k, :], in_=r["product"][:, :, :], axis=AX.X, op=ALU.add).then_inc(s["picked"], 1)
    dve.wait_ge(s["picked"], base + 2)


ROUTE_SEMS = ("top_done index_done indexf_done chosen_done before_done both_done count_mm product_done picked ")


def scatter_rows(nc, pool, rows_of, slots, buffer, last_slot, scattered):
    for b in range(BATCH):
        for k in range(2):
            nc.gpsimd.indirect_dma_start(out=buffer, out_offset=bass.IndirectOffsetOnAxis(ap=slots[:, k, b:b + 1], axis=0),
                                         in_=rows_of(b), in_offset=None, bounds_check=last_slot,
                                         oob_is_err=False).then_inc(scattered, 16)


def combine_stage(nc, io, m, tag, buffer, slots, weights, dst, gathered):
    s = open_semaphores(nc, "first_done second_done")
    with ExitStack() as mem:
        ys = mem.enter_context(nc.sbuf_tensor(tag + "_y", [P, 2, BATCH, D], FP32))
        with nc.Block() as block:
            @block.gpsimd
            def _(pool):
                for b in range(BATCH):
                    for k in range(2):
                        nc.gpsimd.indirect_dma_start(out=ys[:, k, b, :], out_offset=None, in_=buffer,
                                                     in_offset=bass.IndirectOffsetOnAxis(ap=slots[:, k, b:b + 1], axis=0)).then_inc(gathered, 16)

            @block.vector
            def _(dve):
                dve.wait_ge(gathered, 16 * 2 * BATCH)
                for k in range(2):
                    if k > 0:
                        dve.wait_ge(s["first_done"], 1)
                    for b in range(BATCH):
                        last = nc.vector.scalar_tensor_tensor(out=dst[:, b, :], in0=ys[:, k, b, :], scalar=weights[:, k, b:b + 1],
                                                              in1=dst[:, b, :], op0=ALU.mult, op1=ALU.add)
                    last.then_inc((s["first_done"], s["second_done"])[k], 1)
                dve.wait_ge(s["second_done"], 1)
    close_semaphores(nc, s)


E1, FF1, SHARED1 = 16, 512, 256
TILES1 = 2 * BATCH * P // SLOT_TILE + E1
TEMPERATURE = 0.7


def mixture1_norm_stage(nc, io, m, x):
    s = open_semaphores(nc, NORM_SEMS + "w_in")
    with ExitStack() as mem:
        def sb(name, shape, dt=FP32):
            return mem.enter_context(nc.sbuf_tensor(name, shape, dt))
        n0, n1 = norm_buffers(sb, "n0"), norm_buffers(sb, "n1")
        n0["xh"] = x["x1"][:, :, :].rearrange("p (g j) d -> p g j d", g=GROUPS)
        n1["xh"] = x["xh"][:, :, :].rearrange("p (g j) d -> p g j d", g=GROUPS)
        bank4 = [k.rearrange("p (j c) -> p j c", j=GS) for k in m.bank]
        with nc.Block() as block:
            @block.sync
            def _(sp):
                sp.dma_start(x["gb"][:, 0:1], io["L0_ffn_ln_in_g"]).then_inc(s["w_in"], 16)
                sp.dma_start(x["gb"][:, 1:2], io["L0_ffn_ln_in_b"]).then_inc(s["w_in"], 16)

            @block.gpsimd
            def _(pool):
                norm_pool(nc, pool, n0, m, s, 0)
                norm_pool(nc, pool, n1, m, s, 1)

            @block.scalar
            def _(act):
                act.wait_ge(s["w_in"], 32)
                for g in range(GROUPS):
                    act.wait_ge(s["xT_mm"], g + 1)
                    nc.scalar.activation(x["hT"][:, g, :], m.bank[g], ACT.Identity, bias=x["gb"][:, 1:2], scale=x["gb"][:, 0:1]).then_inc(s["xT_done"], 1)
                act.wait_ge(s["xT_done"], GROUPS)

            @block.vector
            def _(dve):
                norm_vector(nc, dve, lambda g: m.h[:, GS * g:GS * (g + 1), :], n0, s, 0)
                dve.wait_ge(s["xh_done"], GROUPS)
                norm_vector(nc, dve, lambda g: n0["xh"][:, g], n1, s, 1)
                dve.wait_ge(s["xh_done"], 2 * GROUPS)

            @block.tensor
            def _(pe):
                for g in range(GROUPS):
                    pe.wait_ge(s["xh_done"], GROUPS + g + 1)
                    for j in range(GS):
                        last = nc.tensor.transpose(bank4[g][:, j, :], n1["xh"][:, g, j, :], m.ident)
                    last.then_inc(s["xT_mm"], 1)
    close_semaphores(nc, s)


def mixture1_route_stage(nc, io, m, x):
    s = open_semaphores(nc, ROUTE_SEMS + "w_in logit_mm max_done shift_done exp_done sum_done rz_done gate_done tiles_mm tiles_done ends_done "
                            "base_done place_done slot_done te_done weights_done comb_done combT_mm combT_done bias_mm bias_done up_mm up_done down_mm down_done")
    with ExitStack() as mem:
        def sb(name, shape, dt=FP32):
            return mem.enter_context(nc.sbuf_tensor(name, shape, dt))
        r = routing_buffers(sb, "r1", E1)
        w = sb("r1_w", [P, E1])
        b = sb("r1_b", [1, E1])
        eb2 = sb("r1_eb2", [E1, D])
        sw1 = sb("r1_sw1", [P, SHARED1])
        sb1 = sb("r1_sb1", [P, SHARED1 // P])
        sw2 = sb("r1_sw2", [P, SHARED1 // P, D])
        sb2 = sb("r1_sb2", [1, D])
        mx, zs = sb("r1_mx", [P, BATCH]), sb("r1_zs", [P, BATCH])
        shifted = sb("r1_shifted", [P, BATCH, E1])
        counts = sb("r1_counts", [P, E1])
        tiles_i = sb("r1_tiles_i", [P, E1], mybir.dt.int32)
        tiles, ends, base = sb("r1_tiles", [P, E1]), sb("r1_ends", [P, E1]), sb("r1_base", [P, E1])
        iota_t = sb("r1_iota_t", [1, TILES1])
        past = sb("r1_past", [1, TILES1, E1])
        tef = sb("r1_tef", [1, TILES1])
        comb = sb("r1_comb", [P, BATCH, E1])
        combT = sb("r1_combT", [E1, GROUPS, GT])
        up = sb("r1_up", [P, GROUPS, SHARED1 // P, GT])
        bank4 = [k.rearrange("p (j c) -> p j c", j=GS) for k in m.bank]
        small = m.bank[0][:, 0:BATCH * E1].rearrange("p (b e) -> p b e", b=BATCH)
        FC = SHARED1 // P

        def over_e(a):
            return a.unsqueeze(2).to_broadcast([P, BATCH, E1])

        def over_b(a):
            return a.unsqueeze(1).to_broadcast([P, BATCH, E1])

        with nc.Block() as block:
            @block.sync
            def _(sp):
                for dst, src in [(w[:, :], io["L0_ffn_router_w"]), (b[:, :], io["L0_ffn_router_b"]), (eb2[:, :], io["L0_ffn_eb2"]),
                                 (sw1[:, :], io["L0_ffn_sw1"]), (sb1[:, :], io["L0_ffn_sb1"]), (sw2[:, :, :], io["L0_ffn_sw2"]),
                                 (sb2[:, :], io["L0_ffn_sb2"]), (r["iota"][:, :], io["iota"][:, 0:E1]), (iota_t[:, :], io["iota"][0:1, 0:TILES1]),
                                 (r["earlier"][:, :], io["earlier"])]:
                    sp.dma_start(dst, src).then_inc(s["w_in"], 16)

            @block.gpsimd
            def _(pool):
                nc.gpsimd.memset(r["ones"][:, :], 1.0).then_inc(s["w_in"], 16)

            @block.scalar
            def _(act):
                act.wait_ge(s["w_in"], 176)
                act.wait_ge(s["shift_done"], 1)
                nc.scalar.activation(r["scores"][:, :, :], shifted[:, :, :], ACT.Exp, scale=1.0 / TEMPERATURE).then_inc(s["exp_done"], 1)
                for g in range(GROUPS):
                    for c in range(FC):
                        act.wait_ge(s["up_mm"], FC * g + c + 1)
                        nc.scalar.activation(up[:, g, c, :], m.bank[2 + c], ACT.Silu, bias=sb1[:, c:c + 1]).then_inc(s["up_done"], 1)

            @block.vector
            def _(dve):
                dve.wait_ge(s["w_in"], 176)
                dve.wait_ge(s["logit_mm"], 1)
                nc.vector.tensor_reduce(out=mx[:, :], in_=small, axis=AX.X, op=ALU.max).then_inc(s["max_done"], 1)
                dve.wait_ge(s["max_done"], 1)
                nc.vector.tensor_tensor(shifted[:, :, :], small, over_e(mx[:, :]), ALU.subtract).then_inc(s["shift_done"], 1)
                dve.wait_ge(s["exp_done"], 1)
                nc.vector.tensor_reduce(out=zs[:, :], in_=r["scores"][:, :, :], axis=AX.X, op=ALU.add).then_inc(s["sum_done"], 1)
                dve.wait_ge(s["sum_done"], 1)
                nc.vector.reciprocal(zs[:, :], zs[:, :]).then_inc(s["rz_done"], 1)
                dve.wait_ge(s["rz_done"], 1)
                nc.vector.tensor_tensor(r["scores"][:, :, :], r["scores"][:, :, :], over_e(zs[:, :]), ALU.mult).then_inc(s["gate_done"], 1)
                dve.wait_ge(s["gate_done"], 1)
                choose_two(nc, dve, r, s)
                nc.vector.tensor_copy(x["weights"][:, :, :], r["top"][:, :, 0:2].rearrange("p n k -> p k n")).then_inc(s["weights_done"], 1)
                nc.vector.tensor_tensor(comb[:, :, :], r["scores"][:, :, :], r["both"][:, :, :], ALU.mult).then_inc(s["comb_done"], 1)
                dve.wait_ge(s["tiles_mm"], 1)
                nc.vector.tensor_scalar(counts[:, :], m.bank[1][:, 0:E1], float(SLOT_TILE - 1), None, ALU.add).then_inc(s["tiles_done"], 1)
                dve.wait_ge(s["tiles_done"], 1)
                nc.vector.tensor_copy(tiles_i[:, :], counts[:, :]).then_inc(s["tiles_done"], 1)
                dve.wait_ge(s["tiles_done"], 2)
                nc.vector.tensor_scalar(tiles_i[:, :], tiles_i[:, :], SLOT_TILE.bit_length() - 1, None,
                                        ALU.logical_shift_right).then_inc(s["tiles_done"], 1)
                dve.wait_ge(s["tiles_done"], 3)
                nc.vector.tensor_copy(tiles[:, :], tiles_i[:, :]).then_inc(s["tiles_done"], 1)
                dve.wait_ge(s["tiles_done"], 4)
                nc.vector.tensor_tensor_scan(out=ends[:, :], data0=r["ones"][:, 0:E1], data1=tiles[:, :], initial=0.0, op0=ALU.mult,
                                             op1=ALU.add).then_inc(s["ends_done"], 1)
                dve.wait_ge(s["ends_done"], 1)
                nc.vector.tensor_tensor(base[:, :], ends[:, :], tiles[:, :], ALU.subtract).then_inc(s["base_done"], 1)
                dve.wait_ge(s["base_done"], 1)
                nc.vector.tensor_scalar(base[:, :], base[:, :], float(SLOT_TILE), None, ALU.mult).then_inc(s["base_done"], 1)
                dve.wait_ge(s["base_done"], 2)
                dve.wait_ge(s["count_mm"], 1)
                nc.vector.tensor_tensor(r["place"][:, :, :], small, over_b(base[:, :]), ALU.add).then_inc(s["place_done"], 1)
                dve.wait_ge(s["place_done"], 1)
                pick(nc, dve, r, r["place"][:, :, :], s, 0)
                nc.vector.tensor_copy(x["slots"][:, :, :], r["pos"][:, :, :]).then_inc(s["slot_done"], 1)
                nc.vector.tensor_tensor(past[:, :, :], ends[0:1, :].unsqueeze(1).to_broadcast([1, TILES1, E1]),
                                        iota_t[:, :].unsqueeze(2).to_broadcast([1, TILES1, E1]), ALU.is_le).then_inc(s["te_done"], 1)
                dve.wait_ge(s["te_done"], 1)
                nc.vector.tensor_reduce(out=tef[:, :], in_=past[:, :, :], axis=AX.X, op=ALU.add).then_inc(s["te_done"], 1)
                dve.wait_ge(s["te_done"], 2)
                nc.vector.tensor_scalar(x["tile_expert"][:, :], tef[:, :], float(E1 - 1), None, ALU.min).then_inc(s["te_done"], 1)
                for g in range(GROUPS):
                    dve.wait_ge(s["combT_mm"], g + 1)
                    nc.vector.tensor_copy(combT[:, g, :], m.bank[4 + g % 2][0:E1, :]).then_inc(s["combT_done"], 1)
                    dve.wait_ge(s["bias_mm"], g + 1)
                    nc.vector.tensor_copy(x["moe"][:, GS * g:GS * (g + 1), :], bank4[6]).then_inc(s["bias_done"], 1)
                    dve.wait_ge(s["bias_done"], g + 1)
                    dve.wait_ge(s["down_mm"], g + 1)
                    nc.vector.scalar_tensor_tensor(out=x["moe"][:, GS * g:GS * (g + 1), :], in0=bank4[7], scalar=0.25,
                                                   in1=x["moe"][:, GS * g:GS * (g + 1), :], op0=ALU.mult, op1=ALU.add).then_inc(s["down_done"], 1)
                dve.wait_ge(s["down_done"], GROUPS)
                dve.wait_ge(s["te_done"], 3)
                dve.wait_ge(s["slot_done"], 1)
                dve.wait_ge(s["weights_done"], 1)

            @block.tensor
            def _(pe):
                pe.wait_ge(s["w_in"], 176)
                for t in range(BATCH):
                    nc.tensor.matmul(small[:, t, :], m.ones_row[0:1, 0:P], b[:, :], start=True, stop=False, skip_group_check=True)
                    last = nc.tensor.matmul(small[:, t, :], x["hT"][:, t // GS, t % GS * P:(t % GS + 1) * P], w[:, :], start=False, stop=True,
                                            skip_group_check=True)
                last.then_inc(s["logit_mm"], 1)
                for g in range(GROUPS):
                    for c in range(FC):
                        if g > 0:
                            pe.wait_ge(s["up_done"], FC * (g - 1) + c + 1)
                        nc.tensor.matmul(m.bank[2 + c], sw1[:, c * P:(c + 1) * P], x["hT"][:, g, :], start=True, stop=True).then_inc(s["up_mm"], 1)
                count_earlier(nc, pe, r, small, s)
                nc.tensor.matmul(m.bank[1][:, 0:E1], r["ones"][:, :], r["before"][:, BATCH, :], start=True, stop=True).then_inc(s["tiles_mm"], 1)
                pe.wait_ge(s["comb_done"], 1)
                for g in range(GROUPS):
                    if g >= 2:
                        pe.wait_ge(s["combT_done"], g - 1)
                    for j in range(GS):
                        last = nc.tensor.transpose(bank4[4 + g % 2][0:E1, j, :], comb[:, GS * g + j, :], m.ident)
                    last.then_inc(s["combT_mm"], 1)
                    pe.wait_ge(s["combT_done"], g + 1)
                    if g > 0:
                        pe.wait_ge(s["down_done"], g)
                    for j in range(GS):
                        last = nc.tensor.matmul(bank4[6][:, j, :], combT[:, g, j * P:(j + 1) * P], eb2[:, :], start=True, stop=True)
                    last.then_inc(s["bias_mm"], 1)
                    pe.wait_ge(s["up_done"], FC * (g + 1))
                    for j in range(GS):
                        nc.tensor.matmul(bank4[7][:, j, :], m.ones_row[0:1, 0:P], sb2[:, :], start=True, stop=False)
                        for c in range(FC):
                            last = nc.tensor.matmul(bank4[7][:, j, :], up[:, g, c, j * P:(j + 1) * P], sw2[:, c, :], start=False,
                                                    stop=(c == FC - 1))
                    last.then_inc(s["down_mm"], 1)
    close_semaphores(nc, s)


def mixture1_expert_stage(nc, io, m, x):
    FC = FF1 // P
    LOADS = 4
    HT = SLOT_TILE // P
    s = open_semaphores(nc, "in0 in1 xT_mm xT_done up_mm up_done down_mm down_done stored0 stored1")
    loaded, stored = [s["in0"], s["in1"]], [s["stored0"], s["stored1"]]
    with ExitStack() as mem:
        def sb(name, shape, dt=FP32):
            return mem.enter_context(nc.sbuf_tensor(name, shape, dt))
        xs = sb("e1_x", [P, 2, HT, D])
        w1 = sb("e1_w1", [P, 2, FF1])
        b1 = sb("e1_b1", [P, 2, FC])
        w2 = sb("e1_w2", [P, 2, FC, D])
        xT = sb("e1_xT", [P, 2, SLOT_TILE])
        up = sb("e1_up", [P, 2, FC, SLOT_TILE])
        ys = sb("e1_y", [P, 2, HT, D])
        rows_in = io["slots1_x"].rearrange("(t j p) d -> t p j d", j=HT, p=P)
        rows_out = io["slots1_y"].rearrange("(t j p) d -> t p j d", j=HT, p=P)
        xT_ps = [m.bank[u][:, 0:SLOT_TILE].rearrange("p (j c) -> p j c", j=HT) for u in range(2)]
        up_ps = [m.bank[2 + c][:, 0:SLOT_TILE] for c in range(FC)]
        down_ps = [m.bank[6 + u][:, 0:SLOT_TILE].rearrange("p (j c) -> p j c", j=HT) for u in range(2)]
        with nc.Block() as block:
            @block.gpsimd
            def _(pool):
                pool.wait_ge(m.slots_zeroed, m.slots_zeroed_count)
                scatter_rows(nc, pool, lambda b: x["xh"][:, b, :], x["slots"], io["slots1_x"], TILES1 * SLOT_TILE - 1, m.scattered1)

            @block.sync
            def _(sp):
                sp.wait_ge(m.scattered1, 16 * 2 * BATCH)
                sp.sem_inc(s["down_mm"], 2)
                with sp.Fori(0, TILES1 // 2) as i:
                    for u in range(2):
                        t = i * 2 + u
                        e = sp.value_load(x["tile_expert"][0:1, ds(t, 1)], min_val=0, max_val=E1 - 1)
                        sp.wait_ge(s["down_mm"], t + 1)
                        sp.dma_start(xs[:, u], rows_in[ds(t, 1)].rearrange("o p j d -> p (o j) d")).then_inc(loaded[u], 16)
                        sp.dma_start(w1[:, u], io["L0_ffn_ew1"][ds(e, 1)].rearrange("o p f -> p (o f)")).then_inc(loaded[u], 16)
                        sp.dma_start(b1[:, u], io["L0_ffn_eb1"][ds(e, 1)].rearrange("o p f -> p (o f)")).then_inc(loaded[u], 16)
                        sp.dma_start(w2[:, u], io["L0_ffn_ew2"][ds(e, 1)].rearrange("o p c d -> p (o c) d")).then_inc(loaded[u], 16)

            @block.scalar
            def _(act):
                act.sem_inc(s["stored0"], 16)
                act.sem_inc(s["stored1"], 16)

                def act_up(t, u):
                    for c in range(FC):
                        act.wait_ge(s["up_mm"], t * FC + (c + 1))
                        nc.scalar.activation(up[:, u, c, :], up_ps[c], ACT.Silu, bias=b1[:, u, c:c + 1]).then_inc(s["up_done"], 1)

                with act.Fori(0, TILES1 // 2) as i:
                    for u in range(2):
                        t = i * 2 + u
                        act_up(t, u)
                        act.wait_ge(s["down_done"], t + 1)
                        act.dma_start(rows_out[ds(t, 1)].rearrange("o p j d -> p (o j) d"), ys[:, u]).then_inc(stored[u], 16)
                act.wait_ge(s["stored0"], 16 * (TILES1 // 2 + 1))
                act.wait_ge(s["stored1"], 16 * (TILES1 // 2 + 1))

            @block.vector
            def _(dve):
                def turn(t, u):
                    dve.wait_ge(s["xT_mm"], t + 1)
                    nc.vector.tensor_scalar(xT[:, u, :].rearrange("p (j c) -> p j c", j=HT), xT_ps[u], x["gb"][:, 0:1], x["gb"][:, 1:2],
                                            ALU.mult, ALU.add).then_inc(s["xT_done"], 1)

                turn(0, 0)
                with dve.Fori(0, TILES1 // 2 - 1) as i:
                    for u in range(2):
                        t = i * 2 + u
                        turn(t + 1, 1 - u)
                        dve.wait_ge(stored[u], i * 16 + 16)
                        dve.wait_ge(s["down_mm"], t + 3)
                        nc.vector.tensor_copy(ys[:, u], down_ps[u]).then_inc(s["down_done"], 1)
                for u in range(2):
                    t = TILES1 - 2 + u
                    if u == 0:
                        turn(t + 1, 1)
                    dve.wait_ge(stored[u], 16 * (TILES1 // 2))
                    dve.wait_ge(s["down_mm"], t + 3)
                    nc.vector.tensor_copy(ys[:, u], down_ps[u]).then_inc(s["down_done"], 1)

            @block.tensor
            def _(pe):
                pe.sem_inc(s["up_done"], FC)

                def turn(t, i, u):
                    pe.wait_ge(loaded[u], i * (16 * LOADS) + 16 * LOADS)
                    for j in range(HT):
                        last = nc.tensor.transpose(xT_ps[u][:, j, :], xs[:, u, j, :], m.ident)
                    last.then_inc(s["xT_mm"], 1)

                def expand(t, u):
                    pe.wait_ge(s["xT_done"], t + 1)
                    for c in range(FC):
                        pe.wait_ge(s["up_done"], t * FC + (c + 1))
                        nc.tensor.matmul(up_ps[c], w1[:, u, c * P:(c + 1) * P], xT[:, u, :], start=True, stop=True).then_inc(s["up_mm"], 1)

                def contract(t, u):
                    pe.wait_ge(s["up_done"], t * FC + 2 * FC)
                    for j in range(HT):
                        for c in range(FC):
                            last = nc.tensor.matmul(down_ps[u][:, j, :], up[:, u, c, j * P:(j + 1) * P], w2[:, u, c, :], start=(c == 0),
                                                    stop=(c == FC - 1))
                    last.then_inc(s["down_mm"], 1)

                turn(0, 0, 0)
                expand(0, 0)
                with pe.Fori(0, TILES1 // 2 - 1) as i:
                    turn(i * 2 + 1, i, 1)
                    expand(i * 2 + 1, 1)
                    contract(i * 2, 0)
                    turn(i * 2 + 2, i + 1, 0)
                    expand(i * 2 + 2, 0)
                    contract(i * 2 + 1, 1)
                turn(TILES1 - 1, TILES1 // 2 - 1, 1)
                expand(TILES1 - 1, 1)
                contract(TILES1 - 2, 0)
                contract(TILES1 - 1, 1)
    close_semaphores(nc, s)


def mixture1_stage(nc, io, m):
    with ExitStack() as mem:
        def sb(name, shape, dt=FP32):
            return mem.enter_context(nc.sbuf_tensor(name, shape, dt))
        x = dict(x1=sb("x1", [P, BATCH, D]), xh=sb("x1h", [P, BATCH, D]), hT=sb("x1T", [P, GROUPS, GT]), gb=sb("x1_gb", [P, 2]),
                            slots=sb("slots1", [P, 2, BATCH], U32), weights=sb("weights1", [P, 2, BATCH]),
                            tile_expert=sb("tile_expert", [1, TILES1], mybir.dt.int32), moe=sb("moe1", [P, BATCH, D]))
        mixture1_norm_stage(nc, io, m, x)
        mixture1_route_stage(nc, io, m, x)
        mixture1_expert_stage(nc, io, m, x)
        combine_stage(nc, io, m, "c1", io["slots1_y"], x["slots"], x["weights"], x["moe"], m.gathered1)
        add_stage(nc, m, x["x1"])
        add_stage(nc, m, x["moe"])
        ffn_stage(nc, io, m, "f1", dict(ln_g=io["L0_ffn_ff_ln_g"], ln_b=io["L0_ffn_ff_ln_b"], w1=io["L0_ffn_ff_w1"], b1=io["L0_ffn_ff_b1"],
                                                   w2=io["L0_ffn_ff_w2"], b2=io["L0_ffn_ff_b2"]), x["moe"], m.h, ACT.Silu)


E2, H2 = 64, 64
CAP = SLOT_TILE


def mixture2_route_stage(nc, io, m, x):
    s = open_semaphores(nc, NORM_SEMS + ROUTE_SEMS + "w_in logit_mm scores_done sum_done eps_done rz_done norm_done over_done capped_done "
                            "valid_done slot_base slot_done shift_done weight_done up_mm silu_done gated_done down_mm down_done")
    with ExitStack() as mem:
        def sb(name, shape, dt=FP32):
            return mem.enter_context(nc.sbuf_tensor(name, shape, dt))
        n = norm_buffers(sb, "n2")
        n["xh"] = x["xh"][:, :, :].rearrange("p (g j) d -> p g j d", g=GROUPS)
        r = routing_buffers(sb, "r2", E2)
        hT = sb("r2_hT", [P, GROUPS, GT])
        w = sb("r2_w", [P, E2])
        sw1, sw3, sw2 = sb("r2_sw1", [P, P]), sb("r2_sw3", [P, P]), sb("r2_sw2", [P, D])
        zs = sb("r2_zs", [P, BATCH])
        top = sb("r2_tops", [P, 2, BATCH])
        capped, over, valid, slotf = (sb("r2_" + k, [P, 2, BATCH]) for k in ("capped", "over", "valid", "slotf"))
        act1, gated = sb("r2_act1", [P, 2, GT]), sb("r2_gated", [P, 2, GT])
        bank4 = [k.rearrange("p (j c) -> p j c", j=GS) for k in m.bank]
        wide = m.psum[:, 0:2, :].rearrange("p a (b e) -> p (a b) e", e=E2)
        with nc.Block() as block:
            @block.sync
            def _(sp):
                for dst, src in [(w[:, :], io["L1_ffn_gate_w"]), (sw1[:, :], io["L1_ffn_sw1"]), (sw3[:, :], io["L1_ffn_sw3"]), (sw2[:, :], io["L1_ffn_sw2"]),
                                 (r["iota"][:, :], io["iota"][:, 0:E2]), (r["earlier"][:, :], io["earlier"])]:
                    sp.dma_start(dst, src).then_inc(s["w_in"], 16)

            @block.gpsimd
            def _(pool):
                nc.gpsimd.memset(r["ones"][:, :], 1.0).then_inc(s["w_in"], 16)
                norm_pool(nc, pool, n, m, s, 0)

            @block.scalar
            def _(act):
                act.wait_ge(s["w_in"], 112)
                norm_scale(nc, act, lambda g: hT[:, g, :], lambda g: m.bank[4 + g], None, s, 0)
                act.wait_ge(s["logit_mm"], 1)
                nc.scalar.activation(r["scores"][:, :, :], wide, ACT.Sigmoid).then_inc(s["scores_done"], 1)
                for g in range(GROUPS):
                    act.wait_ge(s["up_mm"], g + 1)
                    if g >= 2:
                        act.wait_ge(s["gated_done"], g - 1)
                    nc.scalar.activation(act1[:, g % 2, :], m.bank[2], ACT.Silu).then_inc(s["silu_done"], 1)

            @block.vector
            def _(dve):
                dve.wait_ge(s["w_in"], 112)
                norm_vector(nc, dve, lambda g: m.h[:, GS * g:GS * (g + 1), :], n, s, 0)
                dve.wait_ge(s["xh_done"], GROUPS)
                for g in range(GROUPS):
                    dve.wait_ge(s["silu_done"], g + 1)
                    if g >= 2:
                        dve.wait_ge(s["down_mm"], g - 1)
                    nc.vector.tensor_tensor(gated[:, g % 2, :], act1[:, g % 2, :], m.bank[3], ALU.mult).then_inc(s["gated_done"], 1)
                dve.wait_ge(s["scores_done"], 1)
                choose_two(nc, dve, r, s)
                nc.vector.tensor_copy(top[:, :, :], r["top"][:, :, 0:2].rearrange("p n k -> p k n")).then_inc(s["norm_done"], 1)
                dve.wait_ge(s["norm_done"], 1)
                nc.vector.tensor_tensor(zs[:, :], top[:, 0, :], top[:, 1, :], ALU.add).then_inc(s["sum_done"], 1)
                dve.wait_ge(s["sum_done"], 1)
                nc.vector.tensor_scalar(zs[:, :], zs[:, :], 1e-20, None, ALU.add).then_inc(s["eps_done"], 1)
                dve.wait_ge(s["eps_done"], 1)
                nc.vector.reciprocal(zs[:, :], zs[:, :]).then_inc(s["rz_done"], 1)
                dve.wait_ge(s["rz_done"], 1)
                nc.vector.tensor_tensor(top[:, :, :], top[:, :, :], zs[:, :].unsqueeze(1).to_broadcast([P, 2, BATCH]),
                                        ALU.mult).then_inc(s["norm_done"], 1)
                dve.wait_ge(s["count_mm"], 1)
                pick(nc, dve, r, wide, s, 0)
                nc.vector.tensor_scalar(valid[:, :, :], r["pos"][:, :, :], float(CAP), 2.5, ALU.is_lt, ALU.mult).then_inc(s["valid_done"], 1)
                nc.vector.tensor_scalar(over[:, :, :], r["pos"][:, :, :], float(CAP), float(2 * E2 * CAP), ALU.is_ge, ALU.mult).then_inc(s["over_done"], 1)
                nc.vector.tensor_scalar(capped[:, :, :], r["pos"][:, :, :], float(CAP - 1), None, ALU.min).then_inc(s["capped_done"], 1)
                dve.wait_ge(s["capped_done"], 1)
                dve.wait_ge(s["norm_done"], 2)
                nc.vector.tensor_tensor(x["weights"][:, :, :], top[:, :, :], valid[:, :, :], ALU.mult).then_inc(s["weight_done"], 1)
                nc.vector.scalar_tensor_tensor(out=slotf[:, :, :], in0=r["indexf"][:, :, :], scalar=float(CAP), in1=capped[:, :, :], op0=ALU.mult,
                                               op1=ALU.add).then_inc(s["slot_base"], 1)
                dve.wait_ge(s["slot_base"], 1)
                nc.vector.tensor_copy(x["slots"][:, :, :], slotf[:, :, :]).then_inc(s["slot_done"], 1)
                nc.vector.tensor_tensor(over[:, :, :], over[:, :, :], slotf[:, :, :], ALU.add).then_inc(s["shift_done"], 1)
                dve.wait_ge(s["shift_done"], 1)
                nc.vector.tensor_copy(x["targets"][:, :, :], over[:, :, :]).then_inc(s["slot_done"], 1)
                for g in range(GROUPS):
                    dve.wait_ge(s["down_mm"], g + 1)
                    nc.vector.tensor_tensor(m.h[:, GS * g:GS * (g + 1), :], m.h[:, GS * g:GS * (g + 1), :], bank4[4 + g],
                                            ALU.add).then_inc(s["down_done"], 1)
                dve.wait_ge(s["down_done"], GROUPS)
                dve.wait_ge(s["slot_done"], 2)
                dve.wait_ge(s["weight_done"], 1)

            @block.tensor
            def _(pe):
                pe.wait_ge(s["w_in"], 112)
                norm_transpose(nc, pe, lambda g: bank4[4 + g], n, m, s, 0)
                for t in range(BATCH):
                    pe.wait_ge(s["xT_done"], t // GS + 1)
                    last = nc.tensor.matmul(wide[:, t, :], hT[:, t // GS, t % GS * P:(t % GS + 1) * P], w[:, :], start=True, stop=True)
                last.then_inc(s["logit_mm"], 1)
                for g in range(GROUPS):
                    if g > 0:
                        pe.wait_ge(s["gated_done"], g)
                    nc.tensor.matmul(m.bank[2], sw1[:, :], hT[:, g, :], start=True, stop=True)
                    nc.tensor.matmul(m.bank[3], sw3[:, :], hT[:, g, :], start=True, stop=True).then_inc(s["up_mm"], 1)
                    if g > 0:
                        for j in range(GS):
                            last = nc.tensor.matmul(bank4[4 + g - 1][:, j, :], gated[:, (g - 1) % 2, j * P:(j + 1) * P], sw2[:, :], start=True,
                                                    stop=True)
                        last.then_inc(s["down_mm"], 1)
                pe.wait_ge(s["gated_done"], GROUPS)
                for j in range(GS):
                    last = nc.tensor.matmul(bank4[4 + GROUPS - 1][:, j, :], gated[:, (GROUPS - 1) % 2, j * P:(j + 1) * P], sw2[:, :], start=True,
                                            stop=True)
                last.then_inc(s["down_mm"], 1)
                pe.wait_ge(s["scores_done"], 1)
                count_earlier(nc, pe, r, wide, s)
    close_semaphores(nc, s)


def mixture2_expert_stage(nc, io, m, x):
    LOADS = 4
    HT = SLOT_TILE // P
    s = open_semaphores(nc, "in0 in1 xT_mm xT_done up_mm silu_done gated_done down_mm down_done stored0 stored1")
    loaded, stored = [s["in0"], s["in1"]], [s["stored0"], s["stored1"]]
    with ExitStack() as mem:
        def sb(name, shape, dt=FP32):
            return mem.enter_context(nc.sbuf_tensor(name, shape, dt))
        xs = sb("e2_x", [P, 2, HT, D])
        w13 = sb("e2_w13", [P, 2, 2, H2])
        w2 = sb("e2_w2", [H2, 2, D])
        xT = sb("e2_xT", [P, 2, SLOT_TILE])
        act1 = sb("e2_act1", [H2, 2, SLOT_TILE])
        gated = sb("e2_gated", [H2, 2, SLOT_TILE])
        ys = sb("e2_y", [P, 2, HT, D])
        rows_in = io["slots2_x"].rearrange("(t j p) d -> t p j d", j=HT, p=P)
        rows_out = io["slots2_y"].rearrange("(t j p) d -> t p j d", j=HT, p=P)
        xT_ps = [m.bank[u][:, 0:SLOT_TILE].rearrange("p (j c) -> p j c", j=HT) for u in range(2)]
        up_ps = [m.bank[2 + u][0:H2, :].rearrange("p (k c) -> p k c", k=2) for u in range(2)]
        down_ps = [m.bank[4 + u][:, 0:SLOT_TILE].rearrange("p (j c) -> p j c", j=HT) for u in range(2)]
        with nc.Block() as block:
            @block.gpsimd
            def _(pool):
                scatter_rows(nc, pool, lambda b: x["xh"][:, b, :], x["targets"], io["slots2_x"], E2 * CAP - 1, m.scattered2)

            @block.sync
            def _(sp):
                sp.wait_ge(m.scattered2, 16 * 2 * BATCH)
                sp.sem_inc(s["down_mm"], 2)
                with sp.Fori(0, E2 // 2) as i:
                    for u in range(2):
                        e = i * 2 + u
                        sp.wait_ge(s["down_mm"], e + 1)
                        sp.dma_start(xs[:, u], rows_in[ds(e, 1)].rearrange("o p j d -> p (o j) d")).then_inc(loaded[u], 16)
                        sp.dma_start(w13[:, u, 0], io["L1_ffn_w1"][ds(e, 1)].rearrange("o p f -> p (o f)")).then_inc(loaded[u], 16)
                        sp.dma_start(w13[:, u, 1], io["L1_ffn_w3"][ds(e, 1)].rearrange("o p f -> p (o f)")).then_inc(loaded[u], 16)
                        sp.dma_start(w2[:, u], io["L1_ffn_w2"][ds(e, 1)].rearrange("o p d -> p (o d)")).then_inc(loaded[u], 16)

            @block.scalar
            def _(act):
                act.sem_inc(s["stored0"], 16)
                act.sem_inc(s["stored1"], 16)
                with act.Fori(0, E2 // 2) as i:
                    for u in range(2):
                        e = i * 2 + u
                        act.wait_ge(s["up_mm"], e + 1)
                        nc.scalar.activation(act1[:, u, :], up_ps[u][:, 0, :], ACT.Silu).then_inc(s["silu_done"], 1)
                        act.wait_ge(s["down_done"], e + 1)
                        act.dma_start(rows_out[ds(e, 1)].rearrange("o p j d -> p (o j) d"), ys[:, u]).then_inc(stored[u], 16)
                act.wait_ge(s["stored0"], 16 * (E2 // 2 + 1))
                act.wait_ge(s["stored1"], 16 * (E2 // 2 + 1))

            @block.vector
            def _(dve):
                def turn(e, u):
                    dve.wait_ge(s["xT_mm"], e + 1)
                    nc.vector.tensor_copy(xT[:, u, :].rearrange("p (j c) -> p j c", j=HT), xT_ps[u]).then_inc(s["xT_done"], 1)

                def gate(e, i, u):
                    dve.wait_ge(s["silu_done"], e + 1)
                    nc.vector.tensor_tensor(gated[:, u, :], act1[:, u, :], up_ps[u][:, 1, :], ALU.mult).then_inc(s["gated_done"], 1)
                    dve.wait_ge(stored[u], i * 16 + 16)
                    dve.wait_ge(s["down_mm"], e + 3)
                    nc.vector.tensor_copy(ys[:, u], down_ps[u]).then_inc(s["down_done"], 1)

                turn(0, 0)
                with dve.Fori(0, E2 // 2 - 1) as i:
                    for u in range(2):
                        turn(i * 2 + (u + 1), 1 - u)
                        gate(i * 2 + u, i, u)
                turn(E2 - 1, 1)
                gate(E2 - 2, E2 // 2 - 1, 0)
                gate(E2 - 1, E2 // 2 - 1, 1)

            @block.tensor
            def _(pe):
                def turn(i, u):
                    pe.wait_ge(loaded[u], i * (16 * LOADS) + 16 * LOADS)
                    for j in range(HT):
                        last = nc.tensor.transpose(xT_ps[u][:, j, :], xs[:, u, j, :], m.ident)
                    last.then_inc(s["xT_mm"], 1)

                def expand(e, u):
                    pe.wait_ge(s["xT_done"], e + 1)
                    for k in range(2):
                        last = nc.tensor.matmul(up_ps[u][:, k, :], w13[:, u, k, :], xT[:, u, :], start=True, stop=True)
                    last.then_inc(s["up_mm"], 1)

                def contract(e, u):
                    pe.wait_ge(s["gated_done"], e + 1)
                    for j in range(HT):
                        last = nc.tensor.matmul(down_ps[u][:, j, :], gated[:, u, j * P:(j + 1) * P], w2[:, u, :], start=True, stop=True)
                    last.then_inc(s["down_mm"], 1)

                turn(0, 0)
                expand(0, 0)
                with pe.Fori(0, E2 // 2 - 1) as i:
                    turn(i, 1)
                    expand(i * 2 + 1, 1)
                    contract(i * 2, 0)
                    turn(i + 1, 0)
                    expand(i * 2 + 2, 0)
                    contract(i * 2 + 1, 1)
                turn(E2 // 2 - 1, 1)
                expand(E2 - 1, 1)
                contract(E2 - 2, 0)
                contract(E2 - 1, 1)
    close_semaphores(nc, s)


def mixture2_stage(nc, io, m):
    with ExitStack() as mem:
        def sb(name, shape, dt=FP32):
            return mem.enter_context(nc.sbuf_tensor(name, shape, dt))
        x = dict(xh=sb("x2h", [P, BATCH, D]), slots=sb("slots2", [P, 2, BATCH], U32), targets=sb("targets2", [P, 2, BATCH], U32),
                            weights=sb("weights2", [P, 2, BATCH]))
        mixture2_route_stage(nc, io, m, x)
        mixture2_expert_stage(nc, io, m, x)
        combine_stage(nc, io, m, "c2", io["slots2_y"], x["slots"], x["weights"], m.h, m.gathered2)


def clear_slots_stage(nc, io, m):
    m.slots_zeroed = nc.alloc_semaphore("slots_zeroed")
    s = open_semaphores(nc, "zeros_made")
    zeros = m.zeros
    with nc.Block() as block:
        @block.gpsimd
        def _(pool):
            nc.gpsimd.memset(zeros[:, :], 0.0).then_inc(s["zeros_made"], 1)

        @block.sync
        def _(sp):
            sp.wait_ge(s["zeros_made"], 1)
            count = 0
            per = zeros.shape[1] // D * P
            for buffer in (io["slots1_x"], io["slots2_x"]):
                for k in range(buffer.shape[0] // per):
                    sp.dma_start(buffer[k * per:(k + 1) * per, :].rearrange("(p r) d -> p (r d)", p=P), zeros[:, :]).then_inc(m.slots_zeroed, 16)
                    count += 16
            m.slots_zeroed_count = count
    close_semaphores(nc, s)



def setup_stage(nc, io, m):
    s = open_semaphores(nc, "zero_done const_done")
    with nc.Block() as block:
        @block.gpsimd
        def _(pool):
            nc.gpsimd.memset(m.ident_t[:, :], 0.0).then_inc(s["zero_done"], 1)
            nc.gpsimd.memset(m.ones_row[:, :], 1.0)
            nc.gpsimd.memset(m.ones_col[:, :], 1.0)
            nc.gpsimd.memset(m.neg_half[:, :], -0.5)
            pool.wait_ge(s["zero_done"], 1)
            nc.gpsimd.affine_select(out=m.ident_t[:, :], in_=m.ident_t[:, :], compare_op=ALU.not_equal, fill=1.0,
                                    base=0, pattern=[[-1, P]], channel_multiplier=1).then_inc(s["const_done"], 1)
            pool.wait_ge(s["const_done"], 1)
    close_semaphores(nc, s)


def store_stage(nc, io, m):
    s = open_semaphores(nc, "stored")
    with nc.Block() as block:
        @block.sync
        def _(sp):
            sp.dma_start(io["out"].rearrange("b t d -> t b d"), m.h[:, :, :]).then_inc(s["stored"], 16)
            sp.wait_ge(s["stored"], 16)
    close_semaphores(nc, s)


def program(nc, io):
    with ExitStack() as mem:
        m = Model()
        m.psum = mem.enter_context(nc.psum_tensor("psum", [P, 8, 512], FP32))
        m.bank = [m.psum[:, i, :] for i in range(8)]
        m.ident_t = mem.enter_context(nc.sbuf_tensor("ident", [P, P], FP32))
        m.ident = m.ident_t[:, :]
        m.ones_row = mem.enter_context(nc.sbuf_tensor("ones_row", [1, 512], FP32))
        m.ones_col = mem.enter_context(nc.sbuf_tensor("ones_col", [P, 1], FP32))
        m.neg_half = mem.enter_context(nc.sbuf_tensor("neg_half", [P, 64], FP32))
        m.h = mem.enter_context(nc.sbuf_tensor("h", [P, BATCH, D], FP32))
        m.zeros = mem.enter_context(nc.sbuf_tensor("zeros", [P, 16 * D], FP32))
        m.embedded = nc.alloc_semaphore("embedded")
        m.scattered1, m.gathered1 = nc.alloc_semaphore("scattered1"), nc.alloc_semaphore("gathered1")
        m.scattered2, m.gathered2 = nc.alloc_semaphore("scattered2"), nc.alloc_semaphore("gathered2")
        setup_stage(nc, io, m)
        clear_slots_stage(nc, io, m)
        for stage in (token_stage, attention_stage, mixture1_stage, recurrent_stage, mixture2_stage):
            stage(nc, io, m)
        store_stage(nc, io, m)


def column(a):
    a = np.asarray(a)
    return a.reshape(-1, 1) if a.size <= P else a.reshape(-1, P).T


def rows(a):
    a = np.asarray(a)
    return a.reshape(-1, P, a.shape[-1]).transpose(1, 0, 2)


def layouts(i):
    o = {}
    pos = np.arange(P, dtype=np.float32)[:, None]
    div = np.exp(np.arange(0, D, 2, dtype=np.float32) * np.float32(-np.log(10000.0) / D))
    pe = np.zeros((P, D), np.float32)
    pe[:, 0::2] = np.sin(pos * div)
    pe[:, 1::2] = np.cos(pos * div)
    o["pe_table"] = pe
    o["x_t"] = i["x"].T
    for n in ("E", "Wq", "Wk", "Wv"):
        o["L0_tok_" + n] = i["L0_tok_" + n]
    o["L0_tok_bq"] = column(i["L0_tok_bq"])
    o["L0_tok_bk"] = column(i["L0_tok_bk"])
    o["L0_tok_bv"] = np.broadcast_to(i["L0_tok_bv"], (P, 16))
    o["L0_tok_Wo"] = i["L0_tok_Wo"].reshape(8, 16, D).transpose(1, 0, 2)
    o["L0_tok_bo"] = i["L0_tok_bo"].reshape(1, D)
    o["L0_tok_ln_g"] = column(i["L0_tok_ln_g"])
    o["L0_tok_ln_b"] = column(i["L0_tok_ln_b"])
    o["L0_tok_W1"] = rows(i["L0_tok_W1"].T)
    o["L0_tok_W2"] = rows(i["L0_tok_W2"])
    o["L0_tok_b1"] = column(i["L0_tok_b1"])
    o["L0_tok_b2"] = i["L0_tok_b2"].reshape(1, D)
    o["L0_attn_ip_w"] = i["L0_attn_ip_w"].T
    for n in ("ip_b", "ff_b2"):
        o["L0_attn_" + n] = i["L0_attn_" + n].reshape(1, D)
    for n in ("ff_ln_g", "ff_ln_b", "ff_b1"):
        o["L0_attn_" + n] = column(i["L0_attn_" + n])
    o["L0_attn_ff_w1"] = i["L0_attn_ff_w1"].T
    o["L0_attn_ff_w2"] = rows(i["L0_attn_ff_w2"].T)
    o["L0_attn_fw_ln_g"] = i["L0_attn_fw_ln_g"][:, :, None]
    o["L0_attn_fw_ln_b"] = i["L0_attn_fw_ln_b"][:, :, None]
    slow = i["L0_attn_fw_slow_w"].reshape(2, 8, 193, D)
    o["fw_qkv"] = np.stack([slow[:, :, 64 * n:64 * n + 64].reshape(2, 512, D) for n in range(3)], 1).transpose(0, 3, 1, 2)
    o["fw_beta"] = slow[:, :, 192].transpose(0, 2, 1)
    o["fw_out"] = i["L0_attn_fw_out_w"].transpose(0, 2, 1).reshape(2, 4, P, D).transpose(0, 2, 1, 3)
    o["fw_masks"] = fast_weight_masks()
    for n in ("in_proj_w", "x_proj_w", "dt_proj_w", "out_proj_w"):
        o["L1_attn_" + n] = i["L1_attn_" + n].transpose(0, 2, 1)
    o["L1_attn_x_proj_w"] = o["L1_attn_x_proj_w"].reshape(3, 2, P, 64).transpose(0, 2, 1, 3)
    o["L1_attn_out_proj_w"] = o["L1_attn_out_proj_w"].reshape(3, 2, P, D).transpose(0, 2, 1, 3)
    o["L1_attn_conv_w"] = i["L1_attn_conv_w"].reshape(3, 2, P, 4).transpose(0, 2, 1, 3)
    o["L1_attn_A_log"] = i["L1_attn_A_log"].reshape(3, 2, P, 16).transpose(0, 2, 1, 3)
    for n in ("conv_b", "dt_proj_b", "D_param"):
        o["L1_attn_" + n] = i["L1_attn_" + n].reshape(3, 2, P).transpose(0, 2, 1)
    for n in ("ln_g", "ln_b"):
        o["L1_attn_" + n] = i["L1_attn_" + n][:, :, None]
    o["lstm_w_ih"] = i["L1_attn_lstm_w_ih"].transpose(2, 0, 1)
    whh = np.zeros((P, 4, P), np.float32)
    for d in range(2):
        whh[64 * d:64 * d + 64, :, 64 * d:64 * d + 64] = i["L1_attn_lstm_w_hh"][d].reshape(4, 64, 64).transpose(2, 0, 1)
    o["lstm_w_hh"] = whh
    o["lstm_bias"] = np.stack([i["L1_attn_lstm_b_ih"], i["L1_attn_lstm_b_hh"]]).reshape(2, 2, 4, 64).transpose(1, 3, 0, 2).reshape(P, 2, 4)
    o["L1_attn_fusion_w"] = rows(i["L1_attn_fusion_w"].T)
    o["L1_attn_fusion_b"] = i["L1_attn_fusion_b"].reshape(1, D)
    for n in ("ln_in_g", "ln_in_b", "sb1", "ff_ln_g", "ff_ln_b", "ff_b1"):
        o["L0_ffn_" + n] = column(i["L0_ffn_" + n])
    for n in ("router_w", "ew1", "eb2", "sw1", "ff_w1"):
        o["L0_ffn_" + n] = i["L0_ffn_" + n]
    for n in ("router_b", "sb2", "ff_b2"):
        o["L0_ffn_" + n] = i["L0_ffn_" + n].reshape(1, -1)
    for n in ("sw2", "ff_w2"):
        o["L0_ffn_" + n] = rows(i["L0_ffn_" + n])
    o["L0_ffn_eb1"] = i["L0_ffn_eb1"].reshape(16, 4, P).transpose(0, 2, 1)
    o["L0_ffn_ew2"] = i["L0_ffn_ew2"].reshape(16, 4, P, D).transpose(0, 2, 1, 3)
    o["L1_ffn_gate_w"] = i["L1_ffn_gate_w"].T
    for n in ("w1", "w3", "w2", "sw1", "sw3", "sw2"):
        o["L1_ffn_" + n] = i["L1_ffn_" + n]
    o["iota"] = np.broadcast_to(np.arange(64, dtype=np.float32), (P, 64))
    o["earlier"] = (np.arange(P)[:, None] < np.arange(P)[None, :]).astype(np.float32)
    o["selector"] = (np.arange(96)[:, None] % 32 == np.arange(32)[None, :]).astype(np.float32)
    return o


def fast_weight_masks():
    t, u = np.arange(P)[:, None], np.arange(P)[None, :]

    def level(l):
        z = 1 << l
        return (t // (2 * z) == u // (2 * z)) & (t // z % 2 == 1) & (u // z % 2 == 0)
    below = [-1 * level(0), -1 * (t < u), level(0).T | (t == u), t // 32 > u // 32, t <= u]
    return np.stack(below + [level(l) | (t == u) for l in range(1, 5)], 1).astype(np.float32)


def kernel(**inputs):
    import concourse.bacc as bacc
    from concourse.bass_utils import run_bass_kernel_spmd

    nc = bacc.Bacc("TRN2", target_bir_lowering=False, num_devices=1)
    arrays, aps = {}, {}
    for name, a in layouts({k: np.asarray(v) for k, v in inputs.items()}).items():
        a = np.ascontiguousarray(a)
        arrays["in_" + name] = a
        aps[name] = nc.dram_tensor("in_" + name, a.shape, mybir.dt.from_np(a.dtype), kind="ExternalInput").ap()
    aps["out"] = nc.dram_tensor("out_0_dram", (BATCH, P, D), FP32, kind="ExternalOutput").ap()
    for name, rows_of in (("slots1_x", TILES1 * SLOT_TILE), ("slots1_y", TILES1 * SLOT_TILE), ("slots2_x", E2 * CAP), ("slots2_y", E2 * CAP)):
        aps[name] = nc.dram_tensor(name, (rows_of, D), FP32, kind="Internal").ap()
    program(nc, aps)
    r = run_bass_kernel_spmd(nc, [arrays], core_ids=[0])
    return r.results[0]["out_0_dram"]
```

```python
import numpy as np
from contextlib import ExitStack
import concourse.bass as bass
from concourse import mybir
from concourse.bass import ds

FP32 = mybir.dt.float32
BF16 = mybir.dt.bfloat16
U32 = mybir.dt.uint32
ALU = mybir.AluOpType
ACT = mybir.ActivationFunctionType
AX = mybir.AxisListType

P = 128
BATCH = 16
D = 128
GROUPS = 4
GS = BATCH // GROUPS
GT = GS * P
EPS = 1e-5


class Model:
    pass


def open_semaphores(nc, names):
    return {n: nc.alloc_semaphore(n) for n in names.split()}


def close_semaphores(nc, sems):
    for s in sems.values():
        nc.gpsimd.sem_clear(s)
    nc.all_engine_barrier()
    for s in sems.values():
        nc.release_semaphore(s)


def normalise_stats(nc, dve, psum, stats, moments, var_eps, s, count):
    for j in range(GS):
        last = nc.vector.bn_stats(stats[:, j, :], psum[:, j, :])
    last.then_inc(s["ln_stats"], 1)
    dve.wait_ge(s["ln_stats"], count)
    nc.vector.memset(var_eps, 0.0)
    for j in range(GS):
        last = nc.vector.bn_aggr(moments[:, j, :], stats[:, j, :])
    last.then_inc(s["ln_moments"], 1)
    dve.wait_ge(s["ln_moments"], count)
    nc.vector.tensor_scalar(var_eps, moments[:, :, 1], EPS, None, ALU.add).then_inc(s["ln_var"], 1)


NORM_SEMS = "ln_stats ln_moments ln_var ln_rstd xh_done xT_mm xT_done "


def norm_buffers(sb, tag):
    return dict(stats=sb(tag + "_stats", [P, GROUPS, GS, 6]), mom=sb(tag + "_mom", [P, GROUPS, GS, 2]),
                           var=sb(tag + "_var", [P, GROUPS, GS]), rstd=sb(tag + "_rstd", [P, GROUPS, GS]),
                           xh=sb(tag + "_xh", [P, GROUPS, GS, D]))


def norm_vector(nc, dve, src, n, s, k):
    for g in range(GROUPS + 1):
        if g < GROUPS:
            normalise_stats(nc, dve, src(g), n["stats"][:, g], n["mom"][:, g], n["var"][:, g, :], s, GROUPS * k + g + 1)
        if g > 0:
            f = g - 1
            dve.wait_ge(s["ln_rstd"], GROUPS * k + f + 1)
            for j in range(GS):
                last = nc.vector.tensor_scalar(n["xh"][:, f, j, :], src(f)[:, j, :], n["mom"][:, f, j, 0:1],
                                               n["rstd"][:, f, j:j + 1], ALU.subtract, ALU.mult)
            last.then_inc(s["xh_done"], 1)


def norm_pool(nc, pool, n, m, s, k):
    for g in range(GROUPS):
        pool.wait_ge(s["ln_var"], GROUPS * k + g + 1)
        nc.gpsimd.tensor_tensor(n["rstd"][:, g, :], n["var"][:, g, :], m.neg_half[:, 0:GS], ALU.pow).then_inc(s["ln_rstd"], 1)


def norm_transpose(nc, pe, dst, n, m, s, k):
    for g in range(GROUPS):
        pe.wait_ge(s["xh_done"], GROUPS * k + g + 1)
        for j in range(GS):
            last = nc.tensor.transpose(dst(g)[:, j, :], n["xh"][:, g, j, :], m.ident)
        last.then_inc(s["xT_mm"], 1)


def norm_scale(nc, act, dst, src, gain_bias, s, k):
    for g in range(GROUPS):
        act.wait_ge(s["xT_mm"], GROUPS * k + g + 1)
        if gain_bias is None:
            last = nc.scalar.activation(dst(g), src(g), ACT.Copy)
        else:
            last = nc.scalar.activation(dst(g), src(g), ACT.Identity, bias=gain_bias[:, 1:2], scale=gain_bias[:, 0:1])
        last.then_inc(s["xT_done"], 1)


def token_stage(nc, io, m):
    LAYERS, DH, HEADS = 4, 16, 8
    FF = 512
    s = open_semaphores(nc, "w_in idx_in e_in emb_done embT ht_ready qk_mm q_done k_done v_mm v_done "
                            "sc_mm mx_done exp_done rz_done vn_done o_mm o_done attn_mm ln_stats ln_moments ln_var "
                            "ln_rstd xh_done xT_mm h1_ready ff_mm setup_mm setup_dve setup_act htok_mm htok_done")
    with ExitStack() as mem:
        def sb(name, shape, dt=FP32):
            return mem.enter_context(nc.sbuf_tensor(name, shape, dt))
        wq = sb("t_wq", [P, 3, DH])
        bqk = sb("t_bqk", [DH, 2])
        bqs = sb("t_bqs", [DH, 1])
        bv = sb("t_bv", [P, DH])
        wo8 = sb("t_wo8", [DH, HEADS, D])
        wo = sb("t_wo", [32, D])
        lngb = sb("t_lngb", [P, 2])
        w1T = sb("t_w1T", [P, FF // P, D])
        w2 = sb("t_w2", [P, FF // P, D])
        b1c = sb("t_b1c", [P, FF // P])
        b2r = sb("t_b2r", [1, D])
        pe_tab = sb("t_pe", [P, D])
        idx = sb("t_idx", [P, BATCH], mybir.dt.int32)
        emb = sb("t_emb", [P, BATCH, D])
        wff = sb("t_wff", [P, D])
        cff = sb("t_cff", [1, GT])
        hT = sb("t_hT", [P, GROUPS, GT])
        h1T = sb("t_h1T", [P, GROUPS, GT])
        qT = sb("t_qT", [DH, GROUPS, GT])
        kT = sb("t_kT", [DH, GROUPS, GT])
        v = sb("t_v", [P, GROUPS, GS, DH])
        vn = sb("t_vn", [P, GROUPS, GS, DH])
        nmx = sb("t_nmx", [P, GROUPS, GS])
        zs = sb("t_zs", [P, GROUPS, GS])
        rz = sb("t_rz", [P, GROUPS, GS])
        es = sb("t_es", [P, GROUPS, GS, P])
        oT = sb("t_oT", [32, GROUPS, GT])
        stats = sb("t_stats", [P, GROUPS, GS, 6])
        mom = sb("t_mom", [P, GROUPS, GS, 2])
        var = sb("t_var", [P, GROUPS, GS])
        rstd = sb("t_rstd", [P, GROUPS, GS])
        xh = sb("t_xh", [P, GROUPS, GS, D])
        X = [m.bank[2 * g] for g in range(GROUPS)]
        Y = [m.bank[2 * g + 1] for g in range(GROUPS)]
        X4 = [b[:, :].rearrange("p (j c) -> p j c", j=GS) for b in X]
        Y4 = [b[:, :].rearrange("p (j c) -> p j c", j=GS) for b in Y]
        ident = m.ident
        n_w = [0]
        with nc.Block() as block:
            @block.sync
            def _(sp):
                sp.dma_start(idx[:, :], io["x_t"]).then_inc(s["idx_in"], 16)
                for dst, src in [(wq[:, 0, :], io["L0_tok_Wq"]), (wq[:, 1, :], io["L0_tok_Wk"]), (wq[:, 2, :], io["L0_tok_Wv"]),
                                 (bqk[:, 0:1], io["L0_tok_bq"]), (bqk[:, 1:2], io["L0_tok_bk"]), (bv[:, :], io["L0_tok_bv"]),
                                 (wo8[:, :, :], io["L0_tok_Wo"]), (wo[DH:DH + 1, :], io["L0_tok_bo"]),
                                 (lngb[:, 0:1], io["L0_tok_ln_g"]), (lngb[:, 1:2], io["L0_tok_ln_b"]),
                                 (w1T[:, :, :], io["L0_tok_W1"]), (w2[:, :, :], io["L0_tok_W2"]), (b1c[:, :], io["L0_tok_b1"]),
                                 (b2r[:, :], io["L0_tok_b2"]), (pe_tab[:, :], io["pe_table"])]:
                    sp.dma_start(dst, src).then_inc(s["w_in"], 16)
                    n_w[0] += 16

            @block.gpsimd
            def _(pool):
                pool.wait_ge(s["idx_in"], 16)
                for b in range(BATCH):
                    nc.gpsimd.indirect_dma_start(
                        out=emb[:, b, :], out_offset=None, in_=io["L0_tok_E"],
                        in_offset=bass.IndirectOffsetOnAxis(ap=idx[:, b:b + 1].bitcast(U32), axis=0)).then_inc(m.embedded, 16)
                nc.gpsimd.memset(oT[:, :, :], 1.0).then_inc(s["setup_act"], 1)
                with pool.Fori(0, LAYERS) as layer:
                    for k in range(2):
                        for g in range(GROUPS):
                            pool.wait_ge(s["ln_var"], layer * 8 + (4 * k + g + 1))
                            nc.gpsimd.tensor_tensor(rstd[:, g, :], var[:, g, :], m.neg_half[:, 0:GS],
                                                    ALU.pow).then_inc(s["ln_rstd"], 1)

            @block.scalar
            def _(act):
                act.wait_ge(s["w_in"], n_w[0])
                nc.scalar.activation(bqs[:, :], bqk[:, 0:1], ACT.Copy, scale=0.25).then_inc(s["setup_act"], 1)
                act.wait_ge(s["setup_act"], 2)
                act.wait_ge(s["embT"], GROUPS)
                for g in range(GROUPS):
                    last = nc.scalar.activation(hT[:, g, :], X[g][:, :], ACT.Copy)
                    last.then_inc(s["ht_ready"], 1)
                with act.Fori(0, LAYERS) as layer:
                    for g in range(GROUPS):
                        act.wait_ge(s["qk_mm"], layer * 4 + (g + 1))
                        nc.scalar.activation(qT[:, g, :], X[g][0:DH, :], ACT.Identity, bias=bqs[:, 0:1],
                                             scale=0.25).then_inc(s["q_done"], 1)
                    for g in range(GROUPS):
                        act.wait_ge(s["mx_done"], layer * 4 + (g + 1))
                        for j in range(GS):
                            last = nc.scalar.activation(es[:, g, j, :], Y4[g][:, j, :], ACT.Exp, bias=nmx[:, g, j:j + 1],
                                                        accum_out=zs[:, g, j:j + 1])
                        last.then_inc(s["exp_done"], 1)
                    for g in range(GROUPS):
                        act.wait_ge(s["o_mm"], layer * 4 + (g + 1))
                        nc.scalar.activation(oT[0:DH, g, :], X[g][0:DH, :], ACT.Copy).then_inc(s["o_done"], 1)
                    for k in range(2):
                        dst = (h1T, hT)[k]
                        for g in range(GROUPS):
                            act.wait_ge(s["xT_mm"], layer * 8 + (4 * k + g + 1))
                            nc.scalar.activation(dst[:, g, :], X[g][:, :], ACT.Identity, bias=lngb[:, 1:2],
                                                 scale=lngb[:, 0:1]).then_inc((s["h1_ready"], s["ht_ready"])[k], 1)

            @block.vector
            def _(dve):
                dve.wait_ge(s["w_in"], n_w[0])
                nc.vector.tensor_reduce(out=wo[0:DH, :], in_=wo8[:, :, :].rearrange("p h d -> p d h"),
                                        axis=AX.X, op=ALU.add).then_inc(s["setup_dve"], 1)
                dve.wait_ge(s["setup_mm"], 1)
                nc.vector.tensor_copy(wff[:, :], X[0][:, 0:D])
                for j in range(GS):
                    last = nc.vector.tensor_copy(cff[:, j * D:(j + 1) * D], Y[0][0:1, 0:D])
                last.then_inc(s["setup_dve"], 1)
                dve.wait_ge(m.embedded, 16 * BATCH)
                for b in range(BATCH):
                    last = nc.vector.tensor_tensor(emb[:, b, :], emb[:, b, :], pe_tab[:, :], ALU.add)
                last.then_inc(s["emb_done"], 1)
                with dve.Fori(0, LAYERS) as layer:
                    for g in range(GROUPS):
                        dve.wait_ge(s["qk_mm"], layer * 4 + (g + 1))
                        nc.vector.tensor_scalar(kT[:, g, :], Y[g][0:DH, :], bqk[:, 1:2], None,
                                                ALU.add).then_inc(s["k_done"], 1)
                    for g in range(GROUPS):
                        dve.wait_ge(s["v_mm"], layer * 4 + (g + 1))
                        nc.vector.tensor_tensor(v[:, g, :, :], X[g][:, 0:GS * DH].rearrange("p (j e) -> p j e", j=GS),
                                                bv[:, :].unsqueeze(1).to_broadcast([P, GS, DH]),
                                                ALU.add).then_inc(s["v_done"], 1)
                        dve.wait_ge(s["sc_mm"], layer * 4 + (g + 1))
                        nc.vector.tensor_reduce(out=nmx[:, g, :], in_=Y4[g], axis=AX.X, op=ALU.max,
                                                negate=True).then_inc(s["mx_done"], 1)
                    for g in range(GROUPS):
                        dve.wait_ge(s["exp_done"], layer * 4 + (g + 1))
                        nc.vector.reciprocal(rz[:, g, :], zs[:, g, :]).then_inc(s["rz_done"], 1)
                        dve.wait_ge(s["rz_done"], layer * 4 + (g + 1))
                        nc.vector.tensor_tensor(vn[:, g, :, :], v[:, g, :, :],
                                                rz[:, g, :].unsqueeze(2).to_broadcast([P, GS, DH]),
                                                ALU.mult).then_inc(s["vn_done"], 1)
                    for k in range(2):
                        for g in range(GROUPS + 1):
                            if g < GROUPS:
                                dve.wait_ge((s["attn_mm"], s["ff_mm"])[k], layer * 4 + (g + 1))
                                normalise_stats(nc, dve, Y4[g], stats[:, g], mom[:, g], var[:, g, :], s,
                                                layer * 8 + (4 * k + g + 1))
                            if g > 0:
                                f = g - 1
                                dve.wait_ge(s["ln_rstd"], layer * 8 + (4 * k + f + 1))
                                for j in range(GS):
                                    last = nc.vector.tensor_scalar(xh[:, f, j, :], Y4[f][:, j, :], mom[:, f, j, 0:1],
                                                                   rstd[:, f, j:j + 1], ALU.subtract, ALU.mult)
                                last.then_inc(s["xh_done"], 1)
                for g in range(GROUPS):
                    dve.wait_ge(s["htok_mm"], g + 1)
                    nc.vector.tensor_copy(m.h[:, GS * g:GS * (g + 1), :], X4[g]).then_inc(s["htok_done"], 1)
                dve.wait_ge(s["htok_done"], GROUPS)

            @block.tensor
            def _(pe):
                pe.wait_ge(s["w_in"], n_w[0])
                for c in range(FF // P):
                    nc.tensor.matmul(X[0][:, 0:D], w1T[:, c, :], w2[:, c, :], start=(c == 0), stop=False)
                nc.tensor.matmul(X[0][:, 0:D], ident, ident, start=False, stop=True)
                for c in range(FF // P):
                    nc.tensor.matmul(Y[0][0:1, 0:D], b1c[:, c:c + 1], w2[:, c, :], start=(c == 0), stop=False)
                nc.tensor.matmul(Y[0][0:1, 0:D], m.ones_row[0:1, 0:1], b2r[:, :], start=False, stop=True).then_inc(s["setup_mm"], 1)
                pe.wait_ge(s["setup_dve"], 2)
                pe.wait_ge(s["emb_done"], 1)
                for g in range(GROUPS):
                    for j in range(GS):
                        last = nc.tensor.transpose(X4[g][:, j, :], emb[:, GS * g + j, :], ident)
                    last.then_inc(s["embT"], 1)
                with pe.Fori(0, LAYERS) as layer:
                    for g in range(GROUPS):
                        pe.wait_ge(s["ht_ready"], layer * 4 + (g + 1))
                        nc.tensor.matmul(X[g][0:DH, :], wq[:, 0, :], hT[:, g, :], start=True, stop=True)
                        nc.tensor.matmul(Y[g][0:DH, :], wq[:, 1, :], hT[:, g, :], start=True, stop=True).then_inc(s["qk_mm"], 1)
                    for g in range(GROUPS):
                        pe.wait_ge(s["q_done"], layer * 4 + (g + 1))
                        for j in range(GS):
                            last = nc.tensor.matmul(X[g][:, j * DH:(j + 1) * DH], hT[:, g, j * P:(j + 1) * P], wq[:, 2, :],
                                                    start=True, stop=True)
                        last.then_inc(s["v_mm"], 1)
                        pe.wait_ge(s["k_done"], layer * 4 + (g + 1))
                        for j in range(GS):
                            last = nc.tensor.matmul(Y4[g][:, j, :], kT[:, g, j * P:(j + 1) * P], qT[:, g, j * P:(j + 1) * P],
                                                    start=True, stop=True)
                        last.then_inc(s["sc_mm"], 1)
                    for g in range(GROUPS):
                        pe.wait_ge(s["vn_done"], layer * 4 + (g + 1))
                        for j in range(GS):
                            last = nc.tensor.matmul(X4[g][0:DH, j, :], vn[:, g, j, :], es[:, g, j, :], start=True, stop=True)
                        last.then_inc(s["o_mm"], 1)
                    for g in range(GROUPS):
                        pe.wait_ge(s["o_done"], layer * 4 + (g + 1))
                        for j in range(GS):
                            nc.tensor.matmul(Y4[g][:, j, :], oT[0:DH + 1, g, j * P:(j + 1) * P], wo[0:DH + 1, :],
                                             start=True, stop=False)
                            last = nc.tensor.matmul(Y4[g][:, j, :], hT[:, g, j * P:(j + 1) * P], ident, start=False, stop=True)
                        last.then_inc(s["attn_mm"], 1)
                    for k in range(2):
                        for g in range(GROUPS):
                            pe.wait_ge(s["xh_done"], layer * 8 + (4 * k + g + 1))
                            for j in range(GS):
                                last = nc.tensor.transpose(X4[g][:, j, :], xh[:, g, j, :], ident)
                            last.then_inc(s["xT_mm"], 1)
                        if k == 0:
                            for g in range(GROUPS):
                                pe.wait_ge(s["h1_ready"], layer * 4 + (g + 1))
                                for j in range(GS):
                                    nc.tensor.matmul(Y4[g][:, j, :], m.ones_row[0:1, 0:P], cff[:, 0:D], start=True, stop=False)
                                    last = nc.tensor.matmul(Y4[g][:, j, :], h1T[:, g, j * P:(j + 1) * P], wff[:, :],
                                                            start=False, stop=True)
                                last.then_inc(s["ff_mm"], 1)
                for g in range(GROUPS):
                    pe.wait_ge(s["ht_ready"], 4 * LAYERS + g + 1)
                    for j in range(GS):
                        last = nc.tensor.transpose(X4[g][:, j, :], hT[:, g, j * P:(j + 1) * P], ident)
                    last.then_inc(s["htok_mm"], 1)
    close_semaphores(nc, s)

def attention_input_stage(nc, io, m):
    s = open_semaphores(nc, NORM_SEMS + "w_in out_mm out_done")
    with ExitStack() as mem:
        def sb(name, shape, dt=FP32):
            return mem.enter_context(nc.sbuf_tensor(name, shape, dt))
        w = sb("ip_w", [P, D])
        b = sb("ip_b", [1, D])
        n = norm_buffers(sb, "ip")
        xT = sb("ip_xT", [P, GROUPS, GT])
        bank4 = [k[:, :].rearrange("p (j c) -> p j c", j=GS) for k in m.bank]
        with nc.Block() as block:
            @block.sync
            def _(sp):
                sp.dma_start(w[:, :], io["L0_attn_ip_w"]).then_inc(s["w_in"], 16)
                sp.dma_start(b[:, :], io["L0_attn_ip_b"]).then_inc(s["w_in"], 16)

            @block.gpsimd
            def _(pool):
                norm_pool(nc, pool, n, m, s, 0)

            @block.scalar
            def _(act):
                norm_scale(nc, act, lambda g: xT[:, g, :], lambda g: m.bank[2 * g], None, s, 0)

            @block.vector
            def _(dve):
                norm_vector(nc, dve, lambda g: m.h[:, GS * g:GS * (g + 1), :], n, s, 0)
                for g in range(GROUPS):
                    dve.wait_ge(s["out_mm"], g + 1)
                    nc.vector.tensor_copy(m.res[:, GS * g:GS * (g + 1), :], bank4[2 * g + 1]).then_inc(s["out_done"], 1)
                dve.wait_ge(s["out_done"], GROUPS)

            @block.tensor
            def _(pe):
                norm_transpose(nc, pe, lambda g: bank4[2 * g], n, m, s, 0)
                pe.wait_ge(s["w_in"], 32)
                for g in range(GROUPS):
                    pe.wait_ge(s["xT_done"], g + 1)
                    for j in range(GS):
                        nc.tensor.matmul(bank4[2 * g + 1][:, j, :], m.ones_row[0:1, 0:P], b[:, :], start=True, stop=False)
                        last = nc.tensor.matmul(bank4[2 * g + 1][:, j, :], xT[:, g, j * P:(j + 1) * P], w[:, :],
                                                start=False, stop=True)
                    last.then_inc(s["out_mm"], 1)
    close_semaphores(nc, s)


def ffn_stage(nc, io, m, tag, w, src, dst, func, extra=()):
    FF = 512
    FC = FF // P
    s = open_semaphores(nc, NORM_SEMS + "w_in extra_done up_mm up_done down_mm down_done")
    with ExitStack() as mem:
        def sb(name, shape, dt=FP32):
            return mem.enter_context(nc.sbuf_tensor(name, shape, dt))
        gb = sb(tag + "_gb", [P, 2])
        w1_sb = sb(tag + "_w1", [P, FF])
        b1_sb = sb(tag + "_b1", [P, FC])
        w2_sb = sb(tag + "_w2", [P, FC, D])
        b2_sb = sb(tag + "_b2", [1, D])
        n = norm_buffers(sb, tag)
        xT = sb(tag + "_xT", [P, GROUPS, GT])
        up = sb(tag + "_up", [P, 2, FC, GT])
        bank4 = [k[:, :].rearrange("p (j c) -> p j c", j=GS) for k in m.bank]
        with nc.Block() as block:
            @block.sync
            def _(sp):
                for dst, src in [(gb[:, 0:1], w["ln_g"]), (gb[:, 1:2], w["ln_b"]), (w1_sb[:, :], w["w1"]),
                                 (b1_sb[:, :], w["b1"]), (w2_sb[:, :, :], w["w2"]), (b2_sb[:, :], w["b2"])]:
                    sp.dma_start(dst, src).then_inc(s["w_in"], 16)

            @block.gpsimd
            def _(pool):
                norm_pool(nc, pool, n, m, s, 0)

            @block.scalar
            def _(act):
                act.wait_ge(s["w_in"], 96)
                norm_scale(nc, act, lambda g: xT[:, g, :], lambda g: m.bank[g], gb, s, 0)
                for g in range(GROUPS):
                    if g >= 2:
                        act.wait_ge(s["down_mm"], g - 1)
                    for c in range(FC):
                        act.wait_ge(s["up_mm"], FC * g + c + 1)
                        nc.scalar.activation(up[:, g % 2, c, :], m.bank[c], func,
                                             bias=b1_sb[:, c:c + 1]).then_inc(s["up_done"], 1)

            @block.vector
            def _(dve):
                norm_vector(nc, dve, lambda g: src[:, GS * g:GS * (g + 1), :], n, s, 0)
                for k, x in enumerate(extra):
                    nc.vector.tensor_tensor(dst[:, :, :], dst[:, :, :], x[:, :, :], ALU.add).then_inc(s["extra_done"], 1)
                    dve.wait_ge(s["extra_done"], k + 1)
                for g in range(GROUPS):
                    dve.wait_ge(s["down_mm"], g + 1)
                    nc.vector.tensor_tensor(dst[:, GS * g:GS * (g + 1), :], dst[:, GS * g:GS * (g + 1), :],
                                            bank4[4 + g], ALU.add).then_inc(s["down_done"], 1)
                dve.wait_ge(s["down_done"], GROUPS)

            @block.tensor
            def _(pe):
                norm_transpose(nc, pe, lambda g: bank4[g], n, m, s, 0)
                pe.wait_ge(s["w_in"], 96)
                for g in range(GROUPS + 1):
                    if g < GROUPS:
                        pe.wait_ge(s["xT_done"], GROUPS)
                        for c in range(FC):
                            if g > 0:
                                pe.wait_ge(s["up_done"], FC * (g - 1) + c + 1)
                            nc.tensor.matmul(m.bank[c], w1_sb[:, c * P:(c + 1) * P], xT[:, g, :], start=True,
                                             stop=True).then_inc(s["up_mm"], 1)
                    if g > 0:
                        f = g - 1
                        pe.wait_ge(s["up_done"], FC * g)
                        for j in range(GS):
                            nc.tensor.matmul(bank4[4 + f][:, j, :], m.ones_row[0:1, 0:P], b2_sb[:, :], start=True, stop=False)
                            for c in range(FC):
                                last = nc.tensor.matmul(bank4[4 + f][:, j, :], up[:, f % 2, c, j * P:(j + 1) * P], w2_sb[:, c, :],
                                                        start=False, stop=(c == FC - 1))
                        last.then_inc(s["down_mm"], 1)
    close_semaphores(nc, s)


def fast_weight_stage(nc, io, m, layer):
    H, DH = 8, 64
    HQ = 4
    LEVELS = 4
    FULL = LEVELS - 1
    VECTOR_LINKS = 9
    s = open_semaphores(nc, "w_in ln_stats ln_var ln_rstd xh_done xT_mm hT_done qk_mm v_mm shift_q shift_k exp_qk exp_b links qkv_done vb_done "
                            "kT_mm kT_done at_mm a_mm minus_at minus_a pt_done coff_done i_minus_at x2_done xt2_done y_mm w_done "
                            "xt_mm x_mm xt_done x_done bt_mm bt_done r_mm r_done u_mm u_done o_mm o_done out_mm out_done")
    with ExitStack() as mem:
        def sb(name, shape, dt=FP32):
            return mem.enter_context(nc.sbuf_tensor("fw%d_%s" % (layer, name), shape, dt))
        gb = sb("gb", [P, 2])
        wqkv = sb("wqkv", [P, 3, H * DH])
        wb = sb("wb", [P, H])
        wo = sb("wo", [P, H // 2, D])
        masks = sb("masks", [P, 9, P])
        stats, mom, var, rstd = sb("stats", [P, 6]), sb("mom", [P, 2]), sb("var", [P, 1]), sb("rstd", [P, 1])
        xh, hT = sb("xh", [P, D]), sb("hT", [P, P])
        mx = sb("mx", [P, 2, H])
        shifted = sb("shifted", [P, 2, H, DH])
        ez = sb("ez", [P, 2, H, DH])
        zs, rz = sb("zs", [P, 2, H]), sb("rz", [P, 2, H])
        eb, beta, rzb = sb("eb", [P, H]), sb("beta", [P, H]), sb("rzb", [P, H])
        qn, kn, kb, vb = (sb(x, [P, H, DH]) for x in ("qn", "kn", "kb", "vb"))
        qT, kT, kbT = (sb(x, [P, H // 2, P]) for x in ("qT", "kT", "kbT"))
        MT, PT = (sb(x, [P, 2, HQ, P]) for x in ("MT", "PT"))
        coff = sb("coff", [P, 2, HQ, P])
        X, W, nBT = (sb(x, [P, 2, HQ, P]) for x in ("X", "W", "nBT"))
        XTs = [sb("XT%d" % x, [P, 2, HQ, P]) for x in range(2)]
        R, U = (sb(x, [P, 2, HQ, DH]) for x in ("R", "U"))
        OT = sb("OT", [P, H // 2, P])
        misc, bq, bk, bv = m.bank[0], m.bank[1], m.bank[2], m.bank[3]
        xT_ps, beta_ps, out_ps = misc[:, 0:P], misc[:, P:P + H], misc[:, 2 * P:3 * P]
        first = [m.bank[4], m.bank[6]]
        second = [m.bank[5], m.bank[7]]
        A4 = [b[:, :].rearrange("p (j c) -> p j c", j=HQ) for b in first]
        B4 = [b[:, :].rearrange("p (j c) -> p j c", j=HQ) for b in second]
        both = [m.psum[:, 4 + 2 * Q:6 + 2 * Q, :].rearrange("p f (j c) -> p f j c", j=HQ) for Q in range(2)]
        heads = [b[:, :].rearrange("p (h e) -> p h e", h=H) for b in (bq, bk, bv)]
        pairs = [b[:, :].rearrange("p (h c) -> p h c", h=H // 2) for b in (bq, bk, bv)]
        a_ps = m.psum[:, 1:3, :].rearrange("p f (j c) -> p f j c", j=HQ)
        MINUS_SUB, MINUS_UPPER, PAIRS_T, M_OFF, M_CAUSAL, M_LEVEL = range(6)

        def mask(k):
            return masks[:, k, :].unsqueeze(1).to_broadcast([P, HQ, P])

        def mask4(k):
            return masks[:, k, :].unsqueeze(1).unsqueeze(1).to_broadcast([P, 2, 2, P])

        eye = m.ident.unsqueeze(1).to_broadcast([P, HQ, P])

        def by_parity(x, Q):
            return x[:, Q].rearrange("p (f j) c -> p f j c", f=2)

        def over_e(x):
            return x.unsqueeze(2).to_broadcast([P, H, DH])

        def tile(b):
            return m.res[:, ds(b, 1), :].rearrange("p o d -> p (o d)") if not isinstance(b, int) else m.res[:, b, :]

        with nc.Block() as block:
            @block.sync
            def _(sp):
                for dst, src in [(gb[:, 0:1], io["L0_attn_fw_ln_g"][layer]), (gb[:, 1:2], io["L0_attn_fw_ln_b"][layer]),
                                 (wqkv[:, :, :], io["fw_qkv"][layer]), (wb[:, :], io["fw_beta"][layer]), (wo[:, :, :], io["fw_out"][layer]),
                                 (masks[:, :, :], io["fw_masks"])]:
                    sp.dma_start(dst, src).then_inc(s["w_in"], 16)

            @block.gpsimd
            def _(pool):
                pool.wait_ge(s["w_in"], 96)

                def rstd_step(f):
                    pool.wait_ge(s["ln_var"], f + 1)
                    nc.gpsimd.tensor_tensor(rstd[:, :], var[:, :], m.neg_half[:, 0:1], ALU.pow).then_inc(s["ln_rstd"], 1)

                def at_eye(b, Q):
                    pool.wait_ge(s["minus_at"], 2 * b + (Q + 1))
                    nc.gpsimd.tensor_tensor(MT[:, Q], MT[:, Q], eye, ALU.add).then_inc(s["i_minus_at"], 1)

                def pairs(b, Q):
                    pool.wait_ge(s["i_minus_at"], 2 * b + (Q + 1))
                    nc.gpsimd.tensor_tensor(XTs[0][:, Q], MT[:, Q], mask(PAIRS_T), ALU.mult).then_inc(s["xt2_done"], 1)

                rstd_step(0)

                def body(b, front):
                    if front:
                        rstd_step(b + 1)
                    at_eye(b, 0)
                    at_eye(b, 1)
                    pairs(b, 0)
                    pairs(b, 1)

                with pool.Fori(0, BATCH - 1) as b:
                    body(b, True)
                body(BATCH - 1, False)

            @block.scalar
            def _(act):
                act.wait_ge(s["w_in"], 96)

                def f_hT(f):
                    act.wait_ge(s["xT_mm"], f + 1)
                    nc.scalar.activation(hT[:, :], xT_ps, ACT.Identity, bias=gb[:, 1:2], scale=gb[:, 0:1]).then_inc(s["hT_done"], 1)

                def f_exp(f):
                    act.wait_ge(s["shift_q"], f + 1)
                    nc.scalar.activation(ez[:, 0], shifted[:, 0], ACT.Exp).then_inc(s["exp_qk"], 1)
                    act.wait_ge(s["shift_k"], f + 1)
                    nc.scalar.activation(ez[:, 1], shifted[:, 1], ACT.Exp).then_inc(s["exp_qk"], 1)
                    act.wait_ge(s["v_mm"], f + 1)
                    nc.scalar.activation(eb[:, :], beta_ps, ACT.Exp, scale=-1.0).then_inc(s["exp_b"], 1)

                def f_transposed(f):
                    for n, (dst, src) in enumerate(((kbT, bq), (qT, bk), (kT, bv))):
                        act.wait_ge(s["kT_mm"], 3 * f + (n + 1))
                        nc.scalar.activation(dst[:, :, :].rearrange("p a b -> p (a b)"), src[:, :], ACT.Copy).then_inc(s["kT_done"], 1)

                f_hT(0)
                f_exp(0)
                f_transposed(0)

                def body(b, front):
                    if front:
                        f_hT(b + 1)
                    for l in range(LEVELS):
                        for Q in range(2):
                            act.wait_ge(s["xt_mm"], 2 * LEVELS * b + (2 * l + Q + 1))
                            nc.scalar.activation(XTs[(l + 1) % 2][:, Q], A4[Q], ACT.Copy).then_inc(s["xt_done"], 1)
                            if l < FULL:
                                act.wait_ge(s["x_mm"], 2 * FULL * b + (2 * l + Q + 1))
                                nc.scalar.activation(X[:, Q], B4[Q], ACT.Copy).then_inc(s["x_done"], 1)
                        if l == 1 and front:
                            f_exp(b + 1)
                    for Q in range(2):
                        act.wait_ge(s["bt_mm"], 2 * b + (Q + 1))
                        nc.scalar.activation(nBT[:, Q], B4[Q], ACT.Copy, scale=-1.0).then_inc(s["bt_done"], 1)
                    if front:
                        f_transposed(b + 1)
                    for Q in range(2):
                        act.wait_ge(s["o_mm"], 2 * b + (Q + 1))
                        nc.scalar.activation(OT[:, 2 * Q:2 * Q + 2, :], B4[Q][:, 0:2, :], ACT.Copy).then_inc(s["o_done"], 1)

                with act.Fori(0, BATCH - 1) as b:
                    body(b, True)
                body(BATCH - 1, False)

            @block.vector
            def _(dve):
                dve.wait_ge(s["w_in"], 96)

                def f_norm(f):
                    nc.vector.bn_stats(stats[:, :], tile(f)).then_inc(s["ln_stats"], 1)
                    dve.wait_ge(s["ln_stats"], 3 * f + 1)
                    nc.vector.memset(var[:, :], 0.0)
                    nc.vector.bn_aggr(mom[:, :], stats[:, :]).then_inc(s["ln_stats"], 1)
                    dve.wait_ge(s["ln_stats"], 3 * f + 2)
                    nc.vector.tensor_scalar(var[:, :], mom[:, 1:2], EPS, None, ALU.add).then_inc(s["ln_var"], 1)
                    dve.wait_ge(s["ln_rstd"], f + 1)
                    nc.vector.tensor_scalar(xh[:, :], tile(f), mom[:, 0:1], rstd[:, 0:1], ALU.subtract,
                                            ALU.mult).then_inc(s["xh_done"], 1)
                    dve.wait_ge(s["xh_done"], f + 1)
                    nc.vector.memset(var[:, :], 0.0).then_inc(s["ln_stats"], 1)

                def f_shift(f):
                    dve.wait_ge(s["qk_mm"], f + 1)
                    for n in range(2):
                        nc.vector.tensor_reduce(out=mx[:, n, :], in_=heads[n], axis=AX.X, op=ALU.max).then_inc(s["links"], 1)
                        dve.wait_ge(s["links"], VECTOR_LINKS * f + (n + 1))
                        nc.vector.tensor_tensor(shifted[:, n], heads[n], over_e(mx[:, n, :]),
                                                ALU.subtract).then_inc((s["shift_q"], s["shift_k"])[n], 1)

                def f_softmax(f):
                    for n in range(2):
                        dve.wait_ge(s["exp_qk"], 2 * f + (n + 1))
                        nc.vector.tensor_reduce(out=zs[:, n, :], in_=ez[:, n], axis=AX.X, op=ALU.add).then_inc(s["links"], 1)
                    dve.wait_ge(s["links"], VECTOR_LINKS * f + 4)
                    nc.vector.reciprocal(rz[:, :, :], zs[:, :, :]).then_inc(s["links"], 1)
                    dve.wait_ge(s["exp_b"], f + 1)
                    nc.vector.tensor_scalar(beta[:, :], eb[:, :], 1.0, None, ALU.add).then_inc(s["links"], 1)
                    dve.wait_ge(s["links"], VECTOR_LINKS * f + 6)
                    nc.vector.reciprocal(beta[:, :], beta[:, :]).then_inc(s["links"], 1)
                    dve.wait_ge(s["links"], VECTOR_LINKS * f + 7)
                    nc.vector.tensor_tensor(rzb[:, :], beta[:, :], rz[:, 1, :], ALU.mult).then_inc(s["links"], 1)
                    nc.vector.tensor_tensor(qn[:, :, :], ez[:, 0], over_e(rz[:, 0, :]), ALU.mult)
                    nc.vector.tensor_tensor(kn[:, :, :], ez[:, 1], over_e(rz[:, 1, :]), ALU.mult)
                    dve.wait_ge(s["links"], VECTOR_LINKS * f + 8)
                    nc.vector.tensor_tensor(kb[:, :, :], ez[:, 1], over_e(rzb[:, :]), ALU.mult).then_inc(s["qkv_done"], 1)

                def f_value(f):
                    dve.wait_ge(s["v_mm"], f + 1)
                    nc.vector.tensor_tensor(vb[:, :, :], heads[2], over_e(beta[:, :]), ALU.mult).then_inc(s["vb_done"], 1)
                    dve.wait_ge(s["vb_done"], f + 1)
                    nc.vector.memset(mx[:, 0, :], 0.0).then_inc(s["links"], 1)

                f_norm(0)
                f_shift(0)
                f_softmax(0)
                f_value(0)

                def add_out(b):
                    dve.wait_ge(s["out_mm"], b)
                    nc.vector.tensor_tensor(tile(b - 1), out_ps, tile(b - 1), ALU.add).then_inc(s["out_done"], 1)

                def body(b, front, back):
                    def minus_at(Q):
                        dve.wait_ge(s["at_mm"], 2 * b + (Q + 1))
                        nc.vector.tensor_tensor(by_parity(MT, Q), both[Q][:, :, 0:2], mask4(MINUS_UPPER), ALU.mult).then_inc(s["minus_at"], 1)

                    def causal(Q):
                        nc.vector.tensor_tensor(by_parity(PT, Q), both[Q][:, :, 2:4], mask4(M_CAUSAL), ALU.mult).then_inc(s["pt_done"], 1)

                    def minus_a(Q):
                        nc.vector.tensor_tensor(by_parity(X, Q), a_ps[:, :, 2 * Q:2 * Q + 2], mask4(MINUS_SUB), ALU.mult).then_inc(s["minus_a"], 1)

                    def a_eye(Q):
                        dve.wait_ge(s["minus_a"], 2 * b + (Q + 1))
                        nc.vector.tensor_tensor(X[:, Q], X[:, Q], eye, ALU.add).then_inc(s["x2_done"], 1)

                    if front:
                        f_norm(b + 1)
                    dve.wait_ge(s["a_mm"], b + 1)
                    minus_a(0)
                    a_eye(0)
                    minus_a(1)
                    minus_at(0)
                    causal(0)
                    if back:
                        add_out(b)
                    minus_at(1)
                    causal(1)
                    a_eye(1)
                    for l in range(LEVELS):
                        for Q in range(2):
                            dve.wait_ge(s["y_mm"], 2 * LEVELS * b + (2 * l + Q + 1))
                            nc.vector.tensor_tensor(W[:, Q], B4[Q], mask(M_LEVEL + l), ALU.mult).then_inc(s["w_done"], 1)
                        if l == 0:
                            for Q in range(2):
                                nc.vector.tensor_tensor(by_parity(coff, Q), a_ps[:, :, 2 * Q:2 * Q + 2], mask4(M_OFF), ALU.mult).then_inc(s["coff_done"], 1)
                        if l == 1 and front:
                            f_shift(b + 1)
                        if l == 2 and front:
                            f_softmax(b + 1)
                    for Q in range(2):
                        dve.wait_ge(s["r_mm"], 2 * b + (Q + 1))
                        nc.vector.tensor_copy(R[:, Q], first[Q][:, 0:HQ * DH].rearrange("p (h e) -> p h e", h=HQ)).then_inc(s["r_done"], 1)
                    if front:
                        f_value(b + 1)
                    for k in range(3):
                        for Q in range(2):
                            at = HQ * DH * ((k + 1) % 2)
                            dve.wait_ge(s["u_mm"], 6 * b + (2 * k + Q + 1))
                            nc.vector.tensor_tensor(U[:, Q], first[Q][:, at:at + HQ * DH].rearrange("p (h e) -> p h e", h=HQ), R[:, Q],
                                                    ALU.add).then_inc(s["u_done"], 1)

                body(0, True, False)
                with dve.Fori(1, BATCH - 1) as b:
                    body(b, True, True)
                body(BATCH - 1, False, True)
                add_out(BATCH)
                dve.wait_ge(s["out_done"], BATCH)

            @block.tensor
            def _(pe):
                pe.wait_ge(s["w_in"], 96)

                def f_xT(f):
                    pe.wait_ge(s["xh_done"], f + 1)
                    nc.tensor.transpose(xT_ps, xh[:, :], m.ident).then_inc(s["xT_mm"], 1)

                def f_qk(f):
                    pe.wait_ge(s["hT_done"], f + 1)
                    for n, bank in enumerate((bq, bk)):
                        last = nc.tensor.matmul(bank[:, :], hT[:, :], wqkv[:, n, :], start=True, stop=True)
                    last.then_inc(s["qk_mm"], 1)

                def f_v(f):
                    pe.wait_ge(s["hT_done"], f + 1)
                    nc.tensor.matmul(beta_ps, hT[:, :], wb[:, :], start=True, stop=True)
                    nc.tensor.matmul(bv[:, :], hT[:, :], wqkv[:, 2, :], start=True, stop=True).then_inc(s["v_mm"], 1)

                def f_transposes(f):
                    pe.wait_ge(s["qkv_done"], f + 1)
                    for n, (src, dst) in enumerate(((kb, pairs[0]), (qn, pairs[1]), (kn, pairs[2]))):
                        if n == 2:
                            pe.wait_ge(s["vb_done"], f + 1)
                        for h in range(H // 2):
                            last = nc.tensor.transpose(dst[:, h, :], src[:, 2 * h:2 * h + 2, :].rearrange("p h e -> p (h e)"), m.ident)
                        last.then_inc(s["kT_mm"], 1)

                f_xT(0)
                f_qk(0)
                f_v(0)
                f_transposes(0)

                def output(b):
                    pe.wait_ge(s["o_done"], 2 * b)
                    for h in range(H // 2):
                        last = nc.tensor.matmul(out_ps, OT[:, h, :], wo[:, h, :], start=(h == 0), stop=(h == H // 2 - 1))
                    last.then_inc(s["out_mm"], 1)

                def body(b, front, back):
                    pe.wait_ge(s["kT_done"], 3 * b + 3)

                    def scores(Q, dst, at, left, right, sem):
                        for h in range(HQ):
                            lo, pr = DH * (h // 2), 2 * Q + h % 2
                            last = nc.tensor.matmul(dst[:, h // 2, at + h % 2, :], left[lo:lo + DH, pr, :], right[lo:lo + DH, pr, :],
                                                    start=True, stop=True)
                        if sem is not None:
                            last.then_inc(sem, 1)

                    scores(0, a_ps, 0, kbT, kT, None)
                    scores(1, a_ps, 2, kbT, kT, s["a_mm"])
                    if back:
                        pe.wait_ge(s["o_done"], 2 * b)
                    scores(0, both[0], 0, kT, kbT, None)
                    scores(0, both[0], 2, kT, qT, s["at_mm"])
                    if back:
                        pe.wait_ge(s["exp_b"], b + 1)
                        output(b)
                    scores(1, both[1], 0, kT, kbT, None)
                    scores(1, both[1], 2, kT, qT, s["at_mm"])
                    if front:
                        if back:
                            pe.wait_ge(s["out_done"], b)
                        f_xT(b + 1)
                    for l in range(LEVELS):
                        for Q in range(2):
                            if l == 0:
                                pe.wait_ge(s["i_minus_at"], 2 * b + (Q + 1))
                                pe.wait_ge(s["x2_done"], 2 * b + (Q + 1))
                                pe.wait_ge(s["pt_done"], 2 * b + (Q + 1))
                            else:
                                pe.wait_ge(s["x_done"], 2 * FULL * b + (2 * (l - 1) + Q + 1))
                            for h in range(HQ):
                                last = nc.tensor.matmul(B4[Q][:, h, :], MT[:, Q, h, :], X[:, Q, h, :], start=True, stop=True)
                            last.then_inc(s["y_mm"], 1)
                            if l == 0 and Q == 0 and front:
                                f_v(b + 1)
                        for Q in range(2):
                            pe.wait_ge(s["w_done"], 2 * LEVELS * b + (2 * l + Q + 1))
                            if l == 0:
                                pe.wait_ge(s["xt2_done"], 2 * b + (Q + 1))
                            else:
                                pe.wait_ge(s["xt_done"], 2 * LEVELS * b + (2 * (l - 1) + Q + 1))
                            for h in range(HQ):
                                last = nc.tensor.matmul(A4[Q][:, h, :], W[:, Q, h, :], XTs[l % 2][:, Q, h, :], start=True, stop=True)
                            last.then_inc(s["xt_mm"], 1)
                            if l < FULL:
                                for h in range(HQ):
                                    last = nc.tensor.matmul(B4[Q][:, h, :], XTs[l % 2][:, Q, h, :], W[:, Q, h, :], start=True, stop=True)
                                last.then_inc(s["x_mm"], 1)
                        if l == 0 and front:
                            pe.wait_ge(s["coff_done"], 2 * b + 2)
                            f_qk(b + 1)
                    for Q in range(2):
                        pe.wait_ge(s["xt_done"], 2 * LEVELS * b + (2 * FULL + Q + 1))
                        for h in range(HQ):
                            last = nc.tensor.matmul(B4[Q][:, h, :], coff[:, Q, h, :], XTs[0][:, Q, h, :], start=True, stop=True)
                        last.then_inc(s["bt_mm"], 1)
                        for h in range(HQ):
                            last = nc.tensor.matmul(first[Q][:, h * DH:(h + 1) * DH], XTs[0][:, Q, h, :], vb[:, HQ * Q + 2 * (h % 2) + h // 2, :], start=True, stop=True)
                        last.then_inc(s["r_mm"], 1)
                    for k in range(3):
                        for Q in range(2):
                            if k == 0:
                                pe.wait_ge(s["bt_done"], 2 * b + (Q + 1))
                                pe.wait_ge(s["r_done"], 2 * b + (Q + 1))
                            else:
                                pe.wait_ge(s["u_done"], 6 * b + (2 * (k - 1) + Q + 1))
                            at = HQ * DH * ((k + 1) % 2)
                            for h in range(HQ):
                                last = nc.tensor.matmul(first[Q][:, at + h * DH:at + (h + 1) * DH], nBT[:, Q, h, :],
                                                        (R if k == 0 else U)[:, Q, h, :], start=True, stop=True)
                            last.then_inc(s["u_mm"], 1)
                        if k == 0 and front:
                            f_transposes(b + 1)
                    for Q in range(2):
                        pe.wait_ge(s["u_done"], 6 * b + (4 + Q + 1))
                        for h in range(HQ):
                            lo = DH * (h // 2)
                            last = nc.tensor.matmul(B4[Q][lo:lo + DH, h % 2, :], U[:, Q, h, :], PT[:, Q, h, :], start=True, stop=True)
                        last.then_inc(s["o_mm"], 1)

                body(0, True, False)
                with pe.Fori(1, BATCH - 1) as b:
                    body(b, True, True)
                body(BATCH - 1, False, True)
                output(BATCH)
    close_semaphores(nc, s)


def attention_stage(nc, io, m):
    with nc.sbuf_tensor("res", [P, BATCH, D], FP32) as res:
        m.res = res
        attention_input_stage(nc, io, m)
        fast_weight_stage(nc, io, m, 0)
        ffn_stage(nc, io, m, "af", dict(ln_g=io["L0_attn_ff_ln_g"], ln_b=io["L0_attn_ff_ln_b"], w1=io["L0_attn_ff_w1"], b1=io["L0_attn_ff_b1"],
                                                   w2=io["L0_attn_ff_w2"], b2=io["L0_attn_ff_b2"]), res, res, ACT.Relu)
        fast_weight_stage(nc, io, m, 1)
        add_stage(nc, m, res)


def add_stage(nc, m, res):
    s = open_semaphores(nc, "added")
    with nc.Block() as block:
        @block.vector
        def _(dve):
            nc.vector.tensor_tensor(m.h[:, :, :], m.h[:, :, :], res[:, :, :], ALU.add).then_inc(s["added"], 1)
            dve.wait_ge(s["added"], 1)
    close_semaphores(nc, s)


DIN, NSTATE, NTAPS, DTR = 256, 16, 4, 32
HALVES = DIN // P


def recurrent_input_stage(nc, io, m):
    s = open_semaphores(nc, NORM_SEMS)
    with ExitStack() as mem:
        def sb(name, shape, dt=FP32):
            return mem.enter_context(nc.sbuf_tensor(name, shape, dt))
        n = norm_buffers(sb, "ri")
        bank4 = [k.rearrange("p (j c) -> p j c", j=GS) for k in m.bank]
        with nc.Block() as block:
            @block.gpsimd
            def _(pool):
                norm_pool(nc, pool, n, m, s, 0)

            @block.scalar
            def _(act):
                norm_scale(nc, act, lambda g: m.xT[:, g, :], lambda g: m.bank[g], None, s, 0)
                act.wait_ge(s["xT_done"], GROUPS)

            @block.vector
            def _(dve):
                norm_vector(nc, dve, lambda g: m.h[:, GS * g:GS * (g + 1), :], n, s, 0)

            @block.tensor
            def _(pe):
                norm_transpose(nc, pe, lambda g: bank4[g], n, m, s, 0)
    close_semaphores(nc, s)


GATES, HD = 4, 64
CELL = 2
STEPS = 64


FRONT_LOADS, BACK_LOADS = 16 * 7, 16 * 4


def load_front(sp, io, m, z, layer):
    for dst, a in [(z["w"][:, :], io["L1_attn_in_proj_w"][layer]), (z["cw"][:, :, :], io["L1_attn_conv_w"][layer]),
                   (z["cb"][:, :], io["L1_attn_conv_b"][layer]), (z["xw"][:, :, :], io["L1_attn_x_proj_w"][layer]),
                   (z["dw"][:, :], io["L1_attn_dt_proj_w"][layer]), (z["db"][:, :], io["L1_attn_dt_proj_b"][layer]),
                   (z["a_log"][:, :, :], io["L1_attn_A_log"][layer])]:
        sp.dma_start(dst, a).then_inc(m.front_loaded, 16)


def load_back(sp, io, m, z, layer):
    for dst, a in [(z["dparam"][:, :], io["L1_attn_D_param"][layer]), (z["wo"][:, :, :], io["L1_attn_out_proj_w"][layer]),
                   (z["gb"][:, 0:1], io["L1_attn_ln_g"][layer]), (z["gb"][:, 1:2], io["L1_attn_ln_b"][layer])]:
        sp.dma_start(dst, a).then_inc(m.back_loaded, 16)


def mamba_input_stage(nc, io, m, z, layer, src):
    s = open_semaphores(nc, "padded in_mm in_done taps conv_done u_done")
    with ExitStack() as mem:
        def sb(name, shape, dt=FP32):
            return mem.enter_context(nc.sbuf_tensor("mi%d_%s" % (layer, name), shape, dt))
        w, cw, cb = z["w"], z["cw"], z["cb"]
        xpad = sb("xpad", [P, HALVES, BATCH, P + NTAPS - 1])
        conv = sb("conv", [P, HALVES, BATCH, P])
        with nc.Block() as block:
            @block.sync
            def _(sp):
                load_back(sp, io, m, z, layer)

            @block.gpsimd
            def _(pool):
                nc.gpsimd.memset(xpad[:, :, :, 0:NTAPS - 1], 0.0).then_inc(s["padded"], 1)

            @block.tensor
            def _(pe):
                pe.wait_ge(m.front_loaded, FRONT_LOADS * (layer + 1))
                for g in range(GROUPS):
                    for c in range(2 * HALVES):
                        if g >= 2:
                            pe.wait_ge(s["in_done"], 4 * (g - 2) + c + 1)
                        nc.tensor.matmul(m.bank[4 * (g % 2) + c], w[:, c * P:(c + 1) * P], src[:, g, :], start=True,
                                         stop=True).then_inc(s["in_mm"], 1)

            @block.scalar
            def _(act):
                for g in range(GROUPS):
                    for c in range(2 * HALVES):
                        act.wait_ge(s["in_mm"], 4 * g + c + 1)
                        bank = m.bank[4 * (g % 2) + c]
                        if c < HALVES:
                            nc.scalar.activation(xpad[:, c, GS * g:GS * (g + 1), NTAPS - 1:], bank.rearrange("p (j c) -> p j c", j=GS),
                                                 ACT.Copy).then_inc(s["in_done"], 1)
                        else:
                            nc.scalar.activation(z["gate"][:, c - HALVES, g * GT:(g + 1) * GT], bank, ACT.Silu).then_inc(s["in_done"], 1)
                for g in range(GROUPS):
                    act.wait_ge(s["conv_done"], g + 1)
                    nc.scalar.activation(z["u"][:, :, g * GT:(g + 1) * GT],
                                         conv[:, :, GS * g:GS * (g + 1), :].rearrange("p f j c -> p f (j c)"), ACT.Silu).then_inc(s["u_done"], 1)
                act.wait_ge(s["u_done"], GROUPS)

            @block.vector
            def _(dve):
                dve.wait_ge(m.front_loaded, FRONT_LOADS * (layer + 1))
                dve.wait_ge(s["padded"], 1)
                for g in range(GROUPS):
                    seqs = slice(GS * g, GS * (g + 1))
                    dve.wait_ge(s["in_done"], 4 * g + HALVES)
                    for k in range(NTAPS):
                        if k > 0:
                            dve.wait_ge(s["taps"], (NTAPS - 1) * g + k)
                        for f in range(HALVES):
                            tap = xpad[:, f, seqs, k:k + P]
                            if k == 0:
                                last = nc.vector.tensor_scalar(conv[:, f, seqs, :], tap, cw[:, f, 0:1], cb[:, f:f + 1], ALU.mult, ALU.add)
                            else:
                                last = nc.vector.scalar_tensor_tensor(out=conv[:, f, seqs, :], in0=tap, scalar=cw[:, f, k:k + 1],
                                                                      in1=conv[:, f, seqs, :], op0=ALU.mult, op1=ALU.add)
                        last.then_inc(s["conv_done"] if k == NTAPS - 1 else s["taps"], 1)
    close_semaphores(nc, s)


def mamba_step_size_stage(nc, io, m, z, layer):
    s = open_semaphores(nc, "dbl_mm dtin_done hi_done rest_done mid_done split_done dt_mm x_done abs_done exp_done ln_done "
                            "w_done d_done t_done dt_done a_exp dtu_done")
    with ExitStack() as mem:
        def sb(name, shape, dt=FP32):
            return mem.enter_context(nc.sbuf_tensor("ms%d_%s" % (layer, name), shape, dt))
        xw, dw, db = z["xw"], z["dw"], z["db"]
        dtin = sb("dtin", [DTR, GROUPS, GT])
        rest = sb("rest", [32, GROUPS, GT])
        e, w = z["y"], z["dtu"]
        ln = sb("ln", [P, HALVES, BATCH * P])
        with nc.Block() as block:
            @block.tensor
            def _(pe):
                pe.wait_ge(m.front_loaded, FRONT_LOADS * (layer + 1))
                for g in range(GROUPS):
                    for f in range(HALVES):
                        last = nc.tensor.matmul(m.bank[g][0:DTR + 2 * NSTATE, :], xw[:, f, :], z["u"][:, f, g * GT:(g + 1) * GT],
                                                start=(f == 0), stop=(f == HALVES - 1))
                    last.then_inc(s["dbl_mm"], 1)
                for f in range(HALVES):
                    for g in range(GROUPS):
                        if f == 0:
                            pe.wait_ge(s["dtin_done"], g + 1)
                        else:
                            pe.wait_ge(s["x_done"], g + 1)
                        nc.tensor.matmul(m.bank[4 + g], dw[:, f * P:(f + 1) * P], dtin[:, g, :], start=True, stop=True).then_inc(s["dt_mm"], 1)

            @block.scalar
            def _(act):
                act.wait_ge(m.front_loaded, FRONT_LOADS * (layer + 1))
                nc.scalar.activation(z["a"][:, :, :], z["a_log"][:, :, :], ACT.Exp).then_inc(s["a_exp"], 1)
                for g in range(GROUPS):
                    act.wait_ge(s["dbl_mm"], g + 1)
                    nc.scalar.activation(dtin[:, g, :], m.bank[g][0:DTR, :], ACT.Copy).then_inc(s["dtin_done"], 1)
                for f in range(HALVES):
                    for g in range(GROUPS):
                        act.wait_ge(s["dt_mm"], GROUPS * f + g + 1)
                        nc.scalar.activation(z["dt"][:, f, g * GT:(g + 1) * GT], m.bank[4 + g], ACT.Identity,
                                             bias=db[:, f:f + 1]).then_inc(s["x_done"], 1)
                for f in range(HALVES):
                    act.wait_ge(s["x_done"], GROUPS * (f + 1))
                    nc.scalar.activation(e[:, f, :], z["dt"][:, f, :], ACT.Abs).then_inc(s["abs_done"], 1)
                    act.wait_ge(s["abs_done"], f + 1)
                    nc.scalar.activation(e[:, f, :], e[:, f, :], ACT.Exp, scale=-1.0).then_inc(s["exp_done"], 1)
                    act.wait_ge(s["exp_done"], f + 1)
                    nc.scalar.activation(ln[:, f, :], e[:, f, :], ACT.Ln, bias=m.ones_col[:, 0:1]).then_inc(s["ln_done"], 1)

            @block.vector
            def _(dve):
                dve.wait_ge(s["a_exp"], 1)
                nc.vector.tensor_scalar(z["a"][:, :, :], z["a"][:, :, :], -1.0, None, ALU.mult).then_inc(s["a_exp"], 1)
                dve.wait_ge(s["a_exp"], 2)
                for g in range(GROUPS):
                    dve.wait_ge(s["dbl_mm"], g + 1)
                    nc.vector.tensor_copy(z["bc"][32:64, g, :], m.bank[g][32:64, :]).then_inc(s["hi_done"], 1)
                    dve.wait_ge(s["hi_done"], g + 1)
                    nc.vector.tensor_tensor(rest[:, g, :], m.bank[g][32:64, :], z["bc"][32:64, g, :], ALU.subtract).then_inc(s["rest_done"], 1)
                    dve.wait_ge(s["rest_done"], g + 1)
                    nc.vector.tensor_copy(z["bc"][0:32, g, :], rest[:, g, :]).then_inc(s["mid_done"], 1)
                    dve.wait_ge(s["mid_done"], g + 1)
                    nc.vector.tensor_tensor(z["bc"][64:96, g, :], rest[:, g, :], z["bc"][0:32, g, :], ALU.subtract).then_inc(s["split_done"], 1)
                dve.wait_ge(s["split_done"], GROUPS)
                for f in range(HALVES):
                    dve.wait_ge(s["exp_done"], f + 1)
                    nc.vector.tensor_scalar(w[:, f, :], e[:, f, :], 1.0, -1.0, ALU.add, ALU.add).then_inc(s["w_done"], 1)
                    dve.wait_ge(s["w_done"], f + 1)
                    dve.wait_ge(s["ln_done"], f + 1)
                    nc.vector.tensor_tensor(e[:, f, :], e[:, f, :], w[:, f, :], ALU.subtract)
                    nc.vector.scalar_tensor_tensor(out=ln[:, f, :], in0=w[:, f, :], scalar=0.0, in1=ln[:, f, :], op0=ALU.is_gt,
                                                   op1=ALU.mult).then_inc(s["d_done"], 1)
                    dve.wait_ge(s["d_done"], f + 1)
                    nc.vector.tensor_tensor(w[:, f, :], ln[:, f, :], e[:, f, :], ALU.add).then_inc(s["t_done"], 1)
                    dve.wait_ge(s["t_done"], f + 1)
                    nc.vector.scalar_tensor_tensor(out=z["dt"][:, f, :], in0=z["dt"][:, f, :], scalar=0.0, in1=w[:, f, :], op0=ALU.max,
                                                   op1=ALU.add).then_inc(s["dt_done"], 1)
                dve.wait_ge(s["dt_done"], HALVES)

            @block.gpsimd
            def _(pool):
                for f in range(HALVES):
                    pool.wait_ge(s["dt_done"], f + 1)
                    nc.gpsimd.tensor_tensor(z["dtu"][:, f, :], z["dt"][:, f, :], z["u"][:, f, :], ALU.mult).then_inc(s["dtu_done"], 1)
                pool.wait_ge(s["dtu_done"], HALVES)
    close_semaphores(nc, s)


def mamba_scan_stage(nc, io, m, z, r, layer):
    lstm = layer < 2
    first_step = layer * STEPS
    CHUNKS = 2
    CS = BATCH // CHUNKS
    CT = CS * P
    SCAN_CREDIT, HC_CREDIT, Y_CREDIT, DBU_CREDIT, COPY_CREDIT = 2, 4, 2, 2, 1
    s = open_semaphores(nc, "zeroed b_mm c_mm c_copied decay_done dbu_done scan_done hc_done y_mm y_done "
                            "step_mm gates_done in_part cell_done tanh_done hidden_done")
    with ExitStack() as mem:
        def sb(name, shape, dt=FP32):
            return mem.enter_context(nc.sbuf_tensor("mc%d_%s" % (layer, name), shape, dt))
        dparam = z["dparam"]
        zeros = sb("zeros", [P, 512], BF16)
        decay = sb("decay", [P, HALVES, CS, P])
        dbu = sb("dbu", [P, HALVES, CT])
        states = sb("states", [P, HALVES, CT])
        hc = sb("hc", [P, HALVES, CT])
        c_sb = sb("c_sb", [P, 2, CT])
        b_ps = m.psum[:, 0:2, :].rearrange("p a b -> p (a b)")
        c_ps, step_ps = m.bank[2], m.bank[3][:, 0:GATES * BATCH]
        y_ps = [m.psum[:, 4 + 2 * f:6 + 2 * f, :].rearrange("p a b -> p (a b)") for f in range(HALVES)]
        dt4 = z["dt"][:, :, :].rearrange("p f (b t) -> p f b t", b=BATCH)
        bc = z["bc"][:, :, :].rearrange("p g t -> p (g t)")
        gates, hs, cell = r["gates"], r["hs"], r["cell"][:, :]
        part_f, part_i = r["part_f"][:, :], r["part_i"][:, :]
        with nc.Block() as block:
            @block.sync
            def _(sp):
                if layer < 2:
                    load_front(sp, io, m, z, layer + 1)

            @block.gpsimd
            def _(pool):
                nc.gpsimd.memset(zeros[:, :], 0.0)
                nc.gpsimd.memset(decay[:, :, :, 0:1], 0.0).then_inc(s["zeroed"], 1)
                pool.sem_inc(s["hc_done"], HC_CREDIT)
                with pool.Fori(0, CHUNKS) as c, pool.Fori(0, NSTATE // 2) as i:
                    for u in range(2):
                        step = c * NSTATE + i * 2 + u
                        for f in range(HALVES):
                            half = c * (2 * NSTATE) + i * 4 + (2 * u + f)
                            pool.wait_ge(s["c_copied"], step * 2 + (COPY_CREDIT + 2))
                            pool.wait_ge(s["y_mm"], half + (Y_CREDIT - 1))
                            pool.wait_ge(s["scan_done"], half + (SCAN_CREDIT + 1))
                            nc.gpsimd.tensor_tensor(hc[:, f, :], states[:, f, :], c_sb[:, u, :], ALU.mult).then_inc(s["hc_done"], 1)

            @block.scalar
            def _(act):
                act.wait_ge(s["zeroed"], 1)
                act.sem_inc(s["c_copied"], COPY_CREDIT)

                def copy_c(step, u, k):
                    act.wait_ge(s["c_mm"], step * 2 + (k + 1))
                    act.wait_ge(s["hc_done"], step * 2 + (HC_CREDIT - 2))
                    nc.scalar.activation(c_sb[:, u, k * 512:(k + 1) * 512], c_ps, ACT.Copy).then_inc(s["c_copied"], 1)

                def body(c, n, u, last):
                    step = c * NSTATE + n
                    for f in range(HALVES):
                        half = c * (2 * NSTATE) + (n * 2 + f)
                        act.wait_ge(s["scan_done"], half + (SCAN_CREDIT - 1))
                        if lstm:
                            act.wait_ge(s["step_mm"], half + 1)
                            nc.scalar.activation(r["gates"][:, :, :].rearrange("p q b -> p (q b)"), step_ps, ACT.Tanh).then_inc(s["gates_done"], 1)
                        else:
                            nc.scalar.activation(decay[:, f, 0, 0:1], hs[:, 0, 0:1], ACT.Copy)
                        nc.scalar.activation(decay[:, f, :, 1:P], dt4[:, f, ds(c * CS, CS), 1:P], ACT.Exp,
                                             scale=z["a"][:, f, n:n + 1] if isinstance(n, int) else z["a"][:, f, ds(n, 1)]).then_inc(s["decay_done"], 1)
                        if lstm:
                            act.wait_ge(s["cell_done"], half + 1)
                            nc.scalar.activation(r["tanh_cell"][:, :], r["cell"][:, :], ACT.Tanh, scale=0.5).then_inc(s["tanh_done"], 1)
                        if lstm and not last:
                            copy_c(step + 1, 1 - u, f)
                    if not lstm and not last:
                        for k in range(2):
                            copy_c(step + 1, 1 - u, k)

                with act.Fori(0, CHUNKS) as c:
                    for k in range(2):
                        copy_c(c * NSTATE, 0, k)
                    body(c, 0, 0, False)
                    with act.Fori(0, NSTATE // 2 - 1) as i:
                        body(c, i * 2 + 1, 1, False)
                        body(c, i * 2 + 2, 0, False)
                    body(c, NSTATE - 1, 1, True)

            @block.vector
            def _(dve):
                dve.wait_ge(m.back_loaded, BACK_LOADS * (layer + 1))
                dve.sem_inc(s["dbu_done"], DBU_CREDIT)
                dve.sem_inc(s["scan_done"], SCAN_CREDIT)
                dve.sem_inc(s["y_done"], HALVES)
                with dve.Fori(0, CHUNKS) as c:
                    with dve.Fori(0, NSTATE // 2) as i:
                        for u in range(2):
                            step = c * NSTATE + i * 2 + u
                            for f in range(HALVES):
                                half = c * (2 * NSTATE) + i * 4 + (2 * u + f)
                                if lstm:
                                    dve.wait_ge(s["gates_done"], half + 2)
                                    nc.vector.scalar_tensor_tensor(out=part_f, in0=gates[:, 1, :], scalar=1.0, in1=cell, op0=ALU.add, op1=ALU.mult)
                                    nc.vector.scalar_tensor_tensor(out=part_i, in0=gates[:, 0, :], scalar=1.0, in1=gates[:, CELL, :], op0=ALU.add,
                                                                   op1=ALU.mult).then_inc(s["in_part"], 1)
                                    dve.wait_ge(s["in_part"], half + 1)
                                    nc.vector.scalar_tensor_tensor(out=cell, in0=part_f, scalar=0.5, in1=part_i, op0=ALU.mult,
                                                                   op1=ALU.add).then_inc(s["cell_done"], 1)
                                dve.wait_ge(s["b_mm"], step + 1)
                                nc.vector.tensor_tensor(dbu[:, f, :], b_ps, z["dtu"][:, f, ds(c * CT, CT)],
                                                        ALU.mult).then_inc(s["dbu_done"], 1)
                                if lstm:
                                    dve.wait_ge(s["tanh_done"], half + 1)
                                    nc.vector.scalar_tensor_tensor(out=hs[:, ds(half + (first_step + 1), 1), :].rearrange("p o b -> p (o b)"),
                                                                   in0=gates[:, 3, :], scalar=1.0, in1=r["tanh_cell"][:, :], op0=ALU.add,
                                                                   op1=ALU.mult).then_inc(s["hidden_done"], 1)
                                dve.wait_ge(s["decay_done"], half + 1)
                                dve.wait_ge(s["hc_done"], half + (HC_CREDIT - 1))
                                dve.wait_ge(s["dbu_done"], half + (DBU_CREDIT + 1))
                                nc.vector.tensor_tensor_scan(out=states[:, f, :], data0=decay[:, f, :, :].rearrange("p b t -> p (b t)"),
                                                             data1=dbu[:, f, :], initial=0.0, op0=ALU.mult,
                                                             op1=ALU.add).then_inc(s["scan_done"], 1)
                    dve.wait_ge(s["y_mm"], c * (2 * NSTATE) + (2 * NSTATE + Y_CREDIT))
                    for f in range(HALVES):
                        nc.vector.scalar_tensor_tensor(out=z["y"][:, f, ds(c * CT, CT)], in0=z["u"][:, f, ds(c * CT, CT)],
                                                       scalar=dparam[:, f:f + 1], in1=y_ps[f], op0=ALU.mult,
                                                       op1=ALU.add).then_inc(s["y_done"], 1)
                dve.wait_ge(s["y_done"], HALVES + HALVES * CHUNKS)

            @block.tensor
            def _(pe):
                pe.wait_ge(s["zeroed"], 1)
                pe.sem_inc(s["y_mm"], Y_CREDIT)

                pe.sem_inc(s["hidden_done"], 1)
                pe.sem_inc(s["gates_done"], 1)

                def broadcast_b(c, step, n):
                    pe.wait_ge(s["dbu_done"], step * 2 + DBU_CREDIT)
                    for k in range(2):
                        last = nc.tensor.matmul(b_ps[:, k * 512:(k + 1) * 512], m.select[:, ds(n, 1), :].rearrange("p o c -> p (o c)"),
                                                bc[0:96, ds(c * CT + k * 512, 512)], start=True, stop=True)
                    last.then_inc(s["b_mm"], 1)

                def broadcast_c(c, step, n, k):
                    pe.wait_ge(s["c_copied"], step * 2 + (k + COPY_CREDIT))
                    nc.tensor.matmul(c_ps, m.select[:, ds(n + NSTATE, 1), :].rearrange("p o c -> p (o c)"),
                                     bc[0:96, ds(c * CT + k * 512, 512)], start=True, stop=True).then_inc(s["c_mm"], 1)

                def accumulate(half, f):
                    pe.wait_ge(s["hc_done"], half + (HC_CREDIT + 1))
                    for k in range(2):
                        last = nc.tensor.matmul(y_ps[f][:, k * 512:(k + 1) * 512], m.ident, hc[:, f, k * 512:(k + 1) * 512],
                                                start=False, stop=False, skip_group_check=True)
                    last.then_inc(s["y_mm"], 1)

                def lstm_step(half):
                    pe.wait_ge(s["gates_done"], half + 1)
                    nc.tensor.matmul(step_ps, m.ident, r["pre"][:, ds(half + first_step, 1), :, :].rearrange("p o q b -> p (o q b)"),
                                     start=True, stop=False, skip_group_check=True)
                    pe.wait_ge(s["hidden_done"], half + 1)
                    for q in range(GATES):
                        last = nc.tensor.matmul(step_ps[:, q * BATCH:(q + 1) * BATCH], r["whh"][:, q, :],
                                                hs[:, ds(half + first_step, 1), :].rearrange("p o b -> p (o b)"),
                                                start=False, stop=(q == GATES - 1), skip_group_check=True)
                    last.then_inc(s["step_mm"], 1)

                def body(c, n, first, last):
                    step = c * NSTATE + n
                    for f in range(HALVES):
                        half = c * (2 * NSTATE) + (n * 2 + f)
                        if lstm:
                            lstm_step(half)
                        if f == 0:
                            broadcast_b(c, step, n)
                        if not last and (lstm or f == 0):
                            broadcast_c(c, step + 1, n + 1, f)
                        if not first:
                            accumulate(half - 2, f)
                        if not last and not lstm and f == 1:
                            broadcast_c(c, step + 1, n + 1, f)

                with pe.Fori(0, CHUNKS) as c:
                    pe.wait_ge(s["y_done"], c * HALVES + HALVES)
                    for k in range(2 * HALVES):
                        nc.tensor.matmul(m.bank[4 + k], zeros[:, 0:P], zeros[:, :], start=True, stop=False, skip_group_check=True)
                    for k in range(2):
                        broadcast_c(c, c * NSTATE, c * 0, k)
                    body(c, c * 0, True, False)
                    with pe.Fori(0, NSTATE // 2 - 1) as i:
                        body(c, i * 2 + 1, False, False)
                        body(c, i * 2 + 2, False, False)
                    body(c, c * 0 + (NSTATE - 1), False, True)
                    for f in range(HALVES):
                        accumulate(c * (2 * NSTATE) + (2 * NSTATE - 2 + f), f)
    close_semaphores(nc, s)


def mamba_output_stage(nc, io, m, z, layer, src):
    s = open_semaphores(nc, NORM_SEMS + "gated out_mm")
    with ExitStack() as mem:
        def sb(name, shape, dt=FP32):
            return mem.enter_context(nc.sbuf_tensor("mo%d_%s" % (layer, name), shape, dt))
        w, gb = z["wo"], z["gb"]
        n = norm_buffers(sb, "mo%d" % layer)
        bank4 = [k.rearrange("p (j c) -> p j c", j=GS) for k in m.bank]
        with nc.Block() as block:
            @block.gpsimd
            def _(pool):
                norm_pool(nc, pool, n, m, s, 0)

            @block.scalar
            def _(act):
                act.wait_ge(m.back_loaded, BACK_LOADS * (layer + 1))
                norm_scale(nc, act, lambda g: m.mT[:, g, :], lambda g: m.bank[2 * g], gb, s, 0)
                act.wait_ge(s["xT_done"], GROUPS)

            @block.vector
            def _(dve):
                for g in range(GROUPS):
                    cols = slice(g * GT, (g + 1) * GT)
                    nc.vector.tensor_tensor(z["y"][:, :, cols], z["y"][:, :, cols], z["gate"][:, :, cols], ALU.mult).then_inc(s["gated"], 1)
                dve.wait_ge(s["out_mm"], GROUPS)
                norm_vector(nc, dve, lambda g: bank4[2 * g + 1], n, s, 0)

            @block.tensor
            def _(pe):
                pe.wait_ge(m.back_loaded, BACK_LOADS * (layer + 1))
                for g in range(GROUPS):
                    pe.wait_ge(s["gated"], g + 1)
                    for j in range(GS):
                        cols = slice(g * GT + j * P, g * GT + (j + 1) * P)
                        for f in range(HALVES):
                            nc.tensor.matmul(bank4[2 * g + 1][:, j, :], z["y"][:, f, cols], w[:, f, :], start=(f == 0), stop=False)
                        last = nc.tensor.matmul(bank4[2 * g + 1][:, j, :], src[:, g, j * P:(j + 1) * P], m.ident, start=False, stop=True)
                    last.then_inc(s["out_mm"], 1)
                norm_transpose(nc, pe, lambda g: bank4[2 * g], n, m, s, 0)
    close_semaphores(nc, s)


def lstm_input_stage(nc, io, m, r):
    s = open_semaphores(nc, "w_in scaled bias_done g_mm g_done")
    with ExitStack() as mem:
        def sb(name, shape, dt=FP32):
            return mem.enter_context(nc.sbuf_tensor("ls_" + name, shape, dt))
        wih = sb("wih", [P, 2, GATES * HD])
        bias = sb("bias", [P, 2, GATES])
        bsum = sb("bsum", [P, GATES])
        pre, whh = r["pre"], r["whh"]
        with nc.Block() as block:
            @block.sync
            def _(sp):
                for dst, a in [(wih[:, :, :], io["lstm_w_ih"]), (whh[:, :, :], io["lstm_w_hh"]), (bias[:, :, :], io["lstm_bias"])]:
                    sp.dma_start(dst, a).then_inc(s["w_in"], 16)

            @block.gpsimd
            def _(pool):
                nc.gpsimd.memset(r["hs"][:, 0:1, :], 0.0)
                nc.gpsimd.memset(r["cell"][:, :], 0.0)

            @block.scalar
            def _(act):
                act.wait_ge(s["bias_done"], 2)
                for g in range(GROUPS):
                    for q in range(GATES):
                        act.wait_ge(s["g_mm"], GATES * g + q + 1)
                        bank = m.bank[q][:, :].rearrange("p (b t) -> p b t", b=GS)
                        for d in range(2):
                            rows = slice(HD * d, HD * (d + 1))
                            dst = pre[rows, :, q, GS * g:GS * (g + 1)].rearrange("p t b -> p b t")
                            if d == 1:
                                dst = dst[:, :, ::-1]
                            last = nc.scalar.activation(dst, bank[rows], ACT.Identity, bias=bsum[rows, q:q + 1],
                                                        scale=1.0 if q == CELL else 0.5)
                        last.then_inc(s["g_done"], 1)
                act.wait_ge(s["g_done"], GATES * GROUPS)

            @block.vector
            def _(dve):
                dve.wait_ge(s["w_in"], 48)
                for q in range(GATES):
                    last = nc.vector.tensor_scalar(whh[:, q, :], whh[:, q, :], 0.5 if q == CELL else 0.25, None, ALU.mult)
                last.then_inc(s["scaled"], 1)
                nc.vector.tensor_tensor(bsum[:, :], bias[:, 0, :], bias[:, 1, :], ALU.add).then_inc(s["bias_done"], 1)
                dve.wait_ge(s["bias_done"], 1)
                for q in range(GATES):
                    last = nc.vector.tensor_scalar(bsum[:, q:q + 1], bsum[:, q:q + 1], 1.0 if q == CELL else 0.5, None, ALU.mult)
                last.then_inc(s["bias_done"], 1)
                dve.wait_ge(s["scaled"], 1)

            @block.tensor
            def _(pe):
                pe.wait_ge(s["w_in"], 48)
                for g in range(GROUPS):
                    for q in range(GATES):
                        if g > 0:
                            pe.wait_ge(s["g_done"], GATES * (g - 1) + q + 1)
                        for d in range(2):
                            last = nc.tensor.matmul(m.bank[q][HD * d:HD * (d + 1), :], wih[:, d, q * HD:(q + 1) * HD], m.xT[:, g, :],
                                                    start=True, stop=True)
                        last.then_inc(s["g_mm"], 1)
    close_semaphores(nc, s)


def lstm_output_stage(nc, m, r):
    s = open_semaphores(nc, "out_done")
    with nc.Block() as block:
        @block.vector
        def _(dve):
            by_seq = m.lstmT[:, :].rearrange("p (b t) -> p b t", b=BATCH)
            nc.vector.tensor_scalar(by_seq[0:HD], r["hs"][0:HD, 1:P + 1, :].rearrange("p t b -> p b t"), 0.5, None, ALU.mult)
            nc.vector.tensor_scalar(by_seq[HD:P, :, ::-1], r["hs"][HD:P, 1:P + 1, :].rearrange("p t b -> p b t"), 0.5, None,
                                    ALU.mult).then_inc(s["out_done"], 1)
            dve.wait_ge(s["out_done"], 1)
    close_semaphores(nc, s)


def fusion_stage(nc, io, m):
    s = open_semaphores(nc, "w_in out_mm added")
    with ExitStack() as mem:
        w = mem.enter_context(nc.sbuf_tensor("fu_w", [P, 2, D], FP32))
        b = mem.enter_context(nc.sbuf_tensor("fu_b", [1, D], FP32))
        bank4 = [k.rearrange("p (j c) -> p j c", j=GS) for k in m.bank]
        with nc.Block() as block:
            @block.sync
            def _(sp):
                sp.dma_start(w[:, :, :], io["L1_attn_fusion_w"]).then_inc(s["w_in"], 16)
                sp.dma_start(b[:, :], io["L1_attn_fusion_b"]).then_inc(s["w_in"], 16)

            @block.vector
            def _(dve):
                for g in range(GROUPS):
                    dve.wait_ge(s["out_mm"], g + 1)
                    seqs = slice(GS * g, GS * (g + 1))
                    nc.vector.tensor_tensor(m.h[:, seqs, :], m.h[:, seqs, :], bank4[g], ALU.add).then_inc(s["added"], 1)
                dve.wait_ge(s["added"], GROUPS)

            @block.tensor
            def _(pe):
                pe.wait_ge(s["w_in"], 32)
                for g in range(GROUPS):
                    for j in range(GS):
                        cols = slice(j * P, (j + 1) * P)
                        nc.tensor.matmul(bank4[g][:, j, :], m.ones_row[0:1, 0:P], b[:, :], start=True, stop=False)
                        nc.tensor.matmul(bank4[g][:, j, :], m.mT[:, g, cols], w[:, 0, :], start=False, stop=False)
                        last = nc.tensor.matmul(bank4[g][:, j, :], m.lstmT[:, g * GT + j * P:g * GT + (j + 1) * P], w[:, 1, :],
                                                start=False, stop=True)
                    last.then_inc(s["out_mm"], 1)
    close_semaphores(nc, s)


def recurrent_stage(nc, io, m):
    with ExitStack() as mem:
        def sb(name, shape, dt=FP32):
            return mem.enter_context(nc.sbuf_tensor(name, shape, dt))
        m.xT = sb("xT", [P, GROUPS, GT])
        m.mT = m.xT
        m.lstmT = m.zeros
        recurrent_input_stage(nc, io, m)
        r = dict(pre=sb("ls_pre", [P, P, GATES, BATCH]), hs=sb("ls_hs", [P, P + 1, BATCH]), whh=sb("ls_whh", [P, GATES, P]),
                 gates=sb("ls_gates", [P, GATES, BATCH]), cell=sb("ls_cell", [P, BATCH]), tanh_cell=sb("ls_tanh", [P, BATCH]),
                 part_f=sb("ls_part_f", [P, BATCH]), part_i=sb("ls_part_i", [P, BATCH]))
        lstm_input_stage(nc, io, m, r)
        with ExitStack() as inner:
            def sbi(name, shape, dt=FP32):
                return inner.enter_context(nc.sbuf_tensor(name, shape, dt))
            m.select = sbi("select", [96, 2 * NSTATE, P], BF16)
            z = dict(u=sbi("u", [P, HALVES, BATCH * P]), gate=sbi("gate", [P, HALVES, BATCH * P]),
                                dt=sbi("dt", [P, HALVES, BATCH * P]), dtu=sbi("dtu", [P, HALVES, BATCH * P]),
                                y=sbi("y", [P, HALVES, BATCH * P]), a=sbi("a", [P, HALVES, NSTATE]),
                                bc=sbi("bc", [96, GROUPS, GT], BF16), w=sbi("mw", [P, 2 * DIN]), cw=sbi("mcw", [P, HALVES, NTAPS]),
                     cb=sbi("mcb", [P, HALVES]), xw=sbi("mxw", [P, HALVES, DTR + 2 * NSTATE]), dw=sbi("mdw", [DTR, DIN]),
                     db=sbi("mdb", [P, HALVES]), a_log=sbi("ma_log", [P, HALVES, NSTATE]), dparam=sbi("mdparam", [P, HALVES]),
                     wo=sbi("mwo", [P, HALVES, D]), gb=sbi("mgb", [P, 2]))
            selector_stage(nc, io, m, z)
            for layer in range(3):
                src = m.xT if layer == 0 else m.mT
                mamba_input_stage(nc, io, m, z, layer, src)
                mamba_step_size_stage(nc, io, m, z, layer)
                mamba_scan_stage(nc, io, m, z, r, layer)
                mamba_output_stage(nc, io, m, z, layer, src)
        lstm_output_stage(nc, m, r)
        fusion_stage(nc, io, m)


def selector_stage(nc, io, m, z):
    s = open_semaphores(nc, "w_in made")
    with nc.sbuf_tensor("which", [96, 2 * NSTATE], FP32) as which:
        with nc.Block() as block:
            @block.sync
            def _(sp):
                sp.dma_start(which[:, :], io["selector"]).then_inc(s["w_in"], 16)
                load_front(sp, io, m, z, 0)

            @block.vector
            def _(dve):
                dve.wait_ge(s["w_in"], 16)
                nc.vector.tensor_copy(m.select[:, :, :], which[:, :].unsqueeze(2).to_broadcast([96, 2 * NSTATE, P])).then_inc(s["made"], 1)
                dve.wait_ge(s["made"], 1)
    close_semaphores(nc, s)



SLOT_TILE = 256


def routing_buffers(sb, tag, experts):
    n = BATCH
    return dict(
        E=experts, scores=sb(tag + "_scores", [P, n, experts]), top=sb(tag + "_top", [P, n, 8]),
        index=sb(tag + "_index", [P, n, 8], U32), indexf=sb(tag + "_indexf", [P, 2, n]),
        chosen=[sb(tag + "_chosen%d" % k, [P, n, experts]) for k in range(2)], both=sb(tag + "_both", [P, n, experts]),
        before=sb(tag + "_before", [P, n + 1, experts]), place=sb(tag + "_place", [P, n, experts]),
        product=sb(tag + "_product", [P, n, experts]), pos=sb(tag + "_pos", [P, 2, n]),
        iota=sb(tag + "_iota", [P, experts]), earlier=sb(tag + "_earlier", [P, P]), ones=sb(tag + "_ones", [P, P]))


def choose_two(nc, dve, r, s):
    n, E = BATCH, r["E"]
    for b in range(n):
        last = nc.vector.max(out=r["top"][:, b, :], in_=r["scores"][:, b, :])
    last.then_inc(s["top_done"], 1)
    dve.wait_ge(s["top_done"], 1)
    for b in range(n):
        last = nc.vector.max_index(r["index"][:, b, :], r["top"][:, b, :], r["scores"][:, b, :])
    last.then_inc(s["index_done"], 1)
    dve.wait_ge(s["index_done"], 1)
    nc.vector.tensor_copy(r["indexf"][:, :, :], r["index"][:, :, 0:2].rearrange("p n k -> p k n")).then_inc(s["indexf_done"], 1)
    dve.wait_ge(s["indexf_done"], 1)
    for k in range(2):
        last = nc.vector.tensor_tensor(r["chosen"][k][:, :, :], r["iota"][:, :].unsqueeze(1).to_broadcast([P, n, E]),
                                       r["indexf"][:, k, :].unsqueeze(2).to_broadcast([P, n, E]), ALU.is_equal)
    last.then_inc(s["chosen_done"], 1)
    nc.vector.memset(r["before"][:, 0, :], 0.0).then_inc(s["before_done"], 1)
    dve.wait_ge(s["chosen_done"], 1)
    nc.vector.tensor_tensor(r["both"][:, :, :], r["chosen"][0][:, :, :], r["chosen"][1][:, :, :], ALU.add).then_inc(s["both_done"], 1)
    dve.wait_ge(s["both_done"], 1)
    for b in range(n):
        dve.wait_ge(s["before_done"], b + 1)
        nc.vector.tensor_tensor(r["before"][:, b + 1, :], r["before"][:, b, :], r["both"][:, b, :], ALU.add).then_inc(s["before_done"], 1)


def count_earlier(nc, pe, r, dst, s):
    pe.wait_ge(s["before_done"], BATCH + 1)
    for b in range(BATCH):
        nc.tensor.matmul(dst[:, b, :], r["earlier"][:, :], r["both"][:, b, :], start=True, stop=False, skip_group_check=True)
        last = nc.tensor.matmul(dst[:, b, :], r["ones"][:, :], r["before"][:, b, :], start=False, stop=True, skip_group_check=True)
    last.then_inc(s["count_mm"], 1)


def pick(nc, dve, r, table, s, base):
    for k in range(2):
        if k > 0:
            dve.wait_ge(s["picked"], base + k)
        nc.vector.tensor_tensor(r["product"][:, :, :], r["chosen"][k][:, :, :], table, ALU.mult).then_inc(s["product_done"], 1)
        dve.wait_ge(s["product_done"], base + k + 1)
        nc.vector.tensor_reduce(out=r["pos"][:, k, :], in_=r["product"][:, :, :], axis=AX.X, op=ALU.add).then_inc(s["picked"], 1)
    dve.wait_ge(s["picked"], base + 2)


ROUTE_SEMS = ("top_done index_done indexf_done chosen_done before_done both_done count_mm product_done picked ")


def scatter_rows(nc, pool, rows_of, slots, buffer, last_slot, scattered):
    for b in range(BATCH):
        for k in range(2):
            nc.gpsimd.indirect_dma_start(out=buffer, out_offset=bass.IndirectOffsetOnAxis(ap=slots[:, k, b:b + 1], axis=0),
                                         in_=rows_of(b), in_offset=None, bounds_check=last_slot,
                                         oob_is_err=False).then_inc(scattered, 16)


def combine_stage(nc, io, m, tag, buffer, slots, weights, dst, gathered):
    s = open_semaphores(nc, "first_done second_done")
    with ExitStack() as mem:
        ys = mem.enter_context(nc.sbuf_tensor(tag + "_y", [P, 2, BATCH, D], FP32))
        with nc.Block() as block:
            @block.gpsimd
            def _(pool):
                for k in range(2):
                    for b in range(BATCH):
                        nc.gpsimd.indirect_dma_start(out=ys[:, k, b, :], out_offset=None, in_=buffer,
                                                     in_offset=bass.IndirectOffsetOnAxis(ap=slots[:, k, b:b + 1], axis=0)).then_inc(gathered[k], 16)

            @block.vector
            def _(dve):
                for k in range(2):
                    dve.wait_ge(gathered[k], 16 * BATCH)
                    if k > 0:
                        dve.wait_ge(s["first_done"], 1)
                    for b in range(BATCH):
                        last = nc.vector.scalar_tensor_tensor(out=dst[:, b, :], in0=ys[:, k, b, :], scalar=weights[:, k, b:b + 1],
                                                              in1=dst[:, b, :], op0=ALU.mult, op1=ALU.add)
                    last.then_inc((s["first_done"], s["second_done"])[k], 1)
                dve.wait_ge(s["second_done"], 1)
    close_semaphores(nc, s)


E1, FF1, SHARED1 = 16, 512, 256
SETS = 8
SET_SEMS = "".join("in%d stored%d " % (k, k) for k in range(SETS))
TILES1 = 2 * BATCH * P // SLOT_TILE + E1
TEMPERATURE = 0.7


def mixture1_norm_stage(nc, io, m, x):
    s = open_semaphores(nc, NORM_SEMS + "w_in")
    with ExitStack() as mem:
        def sb(name, shape, dt=FP32):
            return mem.enter_context(nc.sbuf_tensor(name, shape, dt))
        n0, n1 = norm_buffers(sb, "n0"), norm_buffers(sb, "n1")
        n0["xh"] = x["x1"][:, :, :].rearrange("p (g j) d -> p g j d", g=GROUPS)
        n1["xh"] = x["xh"][:, :, :].rearrange("p (g j) d -> p g j d", g=GROUPS)
        bank4 = [k.rearrange("p (j c) -> p j c", j=GS) for k in m.bank]
        with nc.Block() as block:
            @block.sync
            def _(sp):
                sp.dma_start(x["gb"][:, 0:1], io["L0_ffn_ln_in_g"]).then_inc(s["w_in"], 16)
                sp.dma_start(x["gb"][:, 1:2], io["L0_ffn_ln_in_b"]).then_inc(s["w_in"], 16)

            @block.gpsimd
            def _(pool):
                norm_pool(nc, pool, n0, m, s, 0)
                norm_pool(nc, pool, n1, m, s, 1)

            @block.scalar
            def _(act):
                act.wait_ge(s["w_in"], 32)
                for g in range(GROUPS):
                    act.wait_ge(s["xT_mm"], g + 1)
                    nc.scalar.activation(x["hT"][:, g, :], m.bank[g], ACT.Identity, bias=x["gb"][:, 1:2], scale=x["gb"][:, 0:1]).then_inc(s["xT_done"], 1)
                act.wait_ge(s["xT_done"], GROUPS)

            @block.vector
            def _(dve):
                norm_vector(nc, dve, lambda g: m.h[:, GS * g:GS * (g + 1), :], n0, s, 0)
                dve.wait_ge(s["xh_done"], GROUPS)
                norm_vector(nc, dve, lambda g: n0["xh"][:, g], n1, s, 1)
                dve.wait_ge(s["xh_done"], 2 * GROUPS)

            @block.tensor
            def _(pe):
                for g in range(GROUPS):
                    pe.wait_ge(s["xh_done"], GROUPS + g + 1)
                    for j in range(GS):
                        last = nc.tensor.transpose(bank4[g][:, j, :], n1["xh"][:, g, j, :], m.ident)
                    last.then_inc(s["xT_mm"], 1)
    close_semaphores(nc, s)


def mixture1_route_stage(nc, io, m, x):
    s = open_semaphores(nc, ROUTE_SEMS + "w_in logit_mm max_done shift_done exp_done sum_done rz_done gate_done tiles_mm tiles_done ends_done "
                            "base_done place_done slot_done te_done weights_done comb_done combT_mm combT_done bias_mm bias_done up_mm up_done down_mm down_done")
    with ExitStack() as mem:
        def sb(name, shape, dt=FP32):
            return mem.enter_context(nc.sbuf_tensor(name, shape, dt))
        r = routing_buffers(sb, "r1", E1)
        w = sb("r1_w", [P, E1])
        b = sb("r1_b", [1, E1])
        eb2 = sb("r1_eb2", [E1, D])
        sw1 = sb("r1_sw1", [P, SHARED1])
        sb1 = sb("r1_sb1", [P, SHARED1 // P])
        sw2 = sb("r1_sw2", [P, SHARED1 // P, D])
        sb2 = sb("r1_sb2", [1, D])
        mx, zs = sb("r1_mx", [P, BATCH]), sb("r1_zs", [P, BATCH])
        shifted = sb("r1_shifted", [P, BATCH, E1])
        counts = sb("r1_counts", [P, E1])
        tiles_i = sb("r1_tiles_i", [P, E1], mybir.dt.int32)
        tiles, ends, base = sb("r1_tiles", [P, E1]), sb("r1_ends", [P, E1]), sb("r1_base", [P, E1])
        iota_t = sb("r1_iota_t", [1, TILES1])
        past = sb("r1_past", [1, TILES1, E1])
        tef = sb("r1_tef", [1, TILES1])
        comb = sb("r1_comb", [P, BATCH, E1])
        combT = sb("r1_combT", [E1, GROUPS, GT])
        up = sb("r1_up", [P, GROUPS, SHARED1 // P, GT])
        bank4 = [k.rearrange("p (j c) -> p j c", j=GS) for k in m.bank]
        small = m.bank[0][:, 0:BATCH * E1].rearrange("p (b e) -> p b e", b=BATCH)
        FC = SHARED1 // P

        def over_e(a):
            return a.unsqueeze(2).to_broadcast([P, BATCH, E1])

        def over_b(a):
            return a.unsqueeze(1).to_broadcast([P, BATCH, E1])

        with nc.Block() as block:
            @block.sync
            def _(sp):
                for dst, src in [(w[:, :], io["L0_ffn_router_w"]), (b[:, :], io["L0_ffn_router_b"]), (eb2[:, :], io["L0_ffn_eb2"]),
                                 (sw1[:, :], io["L0_ffn_sw1"]), (sb1[:, :], io["L0_ffn_sb1"]), (sw2[:, :, :], io["L0_ffn_sw2"]),
                                 (sb2[:, :], io["L0_ffn_sb2"]), (r["iota"][:, :], io["iota"][:, 0:E1]), (iota_t[:, :], io["iota"][0:1, 0:TILES1]),
                                 (r["earlier"][:, :], io["earlier"])]:
                    sp.dma_start(dst, src).then_inc(s["w_in"], 16)

            @block.gpsimd
            def _(pool):
                nc.gpsimd.memset(r["ones"][:, :], 1.0).then_inc(s["w_in"], 16)
                pool.wait_ge(s["slot_done"], 1)
                pool.wait_ge(m.slots_zeroed, m.slots_zeroed_count)
                scatter_rows(nc, pool, lambda b: x["xh"][:, b, :], x["slots"], io["slots1_x"], TILES1 * SLOT_TILE - 1, m.scattered1)

            @block.scalar
            def _(act):
                act.wait_ge(s["w_in"], 176)
                act.wait_ge(s["shift_done"], 1)
                nc.scalar.activation(r["scores"][:, :, :], shifted[:, :, :], ACT.Exp, scale=1.0 / TEMPERATURE).then_inc(s["exp_done"], 1)
                for g in range(GROUPS):
                    for c in range(FC):
                        act.wait_ge(s["up_mm"], FC * g + c + 1)
                        nc.scalar.activation(up[:, g, c, :], m.bank[2 + c], ACT.Silu, bias=sb1[:, c:c + 1]).then_inc(s["up_done"], 1)

            @block.vector
            def _(dve):
                dve.wait_ge(s["w_in"], 176)
                dve.wait_ge(s["logit_mm"], 1)
                nc.vector.tensor_reduce(out=mx[:, :], in_=small, axis=AX.X, op=ALU.max).then_inc(s["max_done"], 1)
                dve.wait_ge(s["max_done"], 1)
                nc.vector.tensor_tensor(shifted[:, :, :], small, over_e(mx[:, :]), ALU.subtract).then_inc(s["shift_done"], 1)
                dve.wait_ge(s["exp_done"], 1)
                nc.vector.tensor_reduce(out=zs[:, :], in_=r["scores"][:, :, :], axis=AX.X, op=ALU.add).then_inc(s["sum_done"], 1)
                dve.wait_ge(s["sum_done"], 1)
                nc.vector.reciprocal(zs[:, :], zs[:, :]).then_inc(s["rz_done"], 1)
                dve.wait_ge(s["rz_done"], 1)
                nc.vector.tensor_tensor(r["scores"][:, :, :], r["scores"][:, :, :], over_e(zs[:, :]), ALU.mult).then_inc(s["gate_done"], 1)
                dve.wait_ge(s["gate_done"], 1)
                choose_two(nc, dve, r, s)
                nc.vector.tensor_copy(x["weights"][:, :, :], r["top"][:, :, 0:2].rearrange("p n k -> p k n")).then_inc(s["weights_done"], 1)
                nc.vector.tensor_tensor(comb[:, :, :], r["scores"][:, :, :], r["both"][:, :, :], ALU.mult).then_inc(s["comb_done"], 1)
                dve.wait_ge(s["tiles_mm"], 1)
                nc.vector.tensor_scalar(counts[:, :], m.bank[1][:, 0:E1], float(SLOT_TILE - 1), None, ALU.add).then_inc(s["tiles_done"], 1)
                dve.wait_ge(s["tiles_done"], 1)
                nc.vector.tensor_copy(tiles_i[:, :], counts[:, :]).then_inc(s["tiles_done"], 1)
                dve.wait_ge(s["tiles_done"], 2)
                nc.vector.tensor_scalar(tiles_i[:, :], tiles_i[:, :], SLOT_TILE.bit_length() - 1, None,
                                        ALU.logical_shift_right).then_inc(s["tiles_done"], 1)
                dve.wait_ge(s["tiles_done"], 3)
                nc.vector.tensor_copy(tiles[:, :], tiles_i[:, :]).then_inc(s["tiles_done"], 1)
                dve.wait_ge(s["tiles_done"], 4)
                nc.vector.tensor_tensor_scan(out=ends[:, :], data0=r["ones"][:, 0:E1], data1=tiles[:, :], initial=0.0, op0=ALU.mult,
                                             op1=ALU.add).then_inc(s["ends_done"], 1)
                dve.wait_ge(s["ends_done"], 1)
                nc.vector.tensor_tensor(base[:, :], ends[:, :], tiles[:, :], ALU.subtract).then_inc(s["base_done"], 1)
                dve.wait_ge(s["base_done"], 1)
                nc.vector.tensor_scalar(base[:, :], base[:, :], float(SLOT_TILE), None, ALU.mult).then_inc(s["base_done"], 1)
                dve.wait_ge(s["base_done"], 2)
                dve.wait_ge(s["count_mm"], 1)
                nc.vector.tensor_tensor(r["place"][:, :, :], small, over_b(base[:, :]), ALU.add).then_inc(s["place_done"], 1)
                dve.wait_ge(s["place_done"], 1)
                pick(nc, dve, r, r["place"][:, :, :], s, 0)
                nc.vector.tensor_copy(x["slots"][:, :, :], r["pos"][:, :, :]).then_inc(s["slot_done"], 1)
                nc.vector.tensor_tensor(past[:, :, :], ends[0:1, :].unsqueeze(1).to_broadcast([1, TILES1, E1]),
                                        iota_t[:, :].unsqueeze(2).to_broadcast([1, TILES1, E1]), ALU.is_le).then_inc(s["te_done"], 1)
                dve.wait_ge(s["te_done"], 1)
                nc.vector.tensor_reduce(out=tef[:, :], in_=past[:, :, :], axis=AX.X, op=ALU.add).then_inc(s["te_done"], 1)
                dve.wait_ge(s["te_done"], 2)
                nc.vector.tensor_scalar(x["tile_expert"][:, :], tef[:, :], float(E1 - 1), None, ALU.min).then_inc(s["te_done"], 1)
                for g in range(GROUPS):
                    dve.wait_ge(s["combT_mm"], g + 1)
                    nc.vector.tensor_copy(combT[:, g, :], m.bank[4 + g % 2][0:E1, :]).then_inc(s["combT_done"], 1)
                    dve.wait_ge(s["bias_mm"], g + 1)
                    nc.vector.tensor_copy(x["moe"][:, GS * g:GS * (g + 1), :], bank4[6]).then_inc(s["bias_done"], 1)
                    dve.wait_ge(s["bias_done"], g + 1)
                    dve.wait_ge(s["down_mm"], g + 1)
                    nc.vector.scalar_tensor_tensor(out=x["moe"][:, GS * g:GS * (g + 1), :], in0=bank4[7], scalar=0.25,
                                                   in1=x["moe"][:, GS * g:GS * (g + 1), :], op0=ALU.mult, op1=ALU.add).then_inc(s["down_done"], 1)
                dve.wait_ge(s["down_done"], GROUPS)
                dve.wait_ge(s["te_done"], 3)
                dve.wait_ge(s["slot_done"], 1)
                dve.wait_ge(s["weights_done"], 1)

            @block.tensor
            def _(pe):
                pe.wait_ge(s["w_in"], 176)
                for t in range(BATCH):
                    nc.tensor.matmul(small[:, t, :], m.ones_row[0:1, 0:P], b[:, :], start=True, stop=False, skip_group_check=True)
                    last = nc.tensor.matmul(small[:, t, :], x["hT"][:, t // GS, t % GS * P:(t % GS + 1) * P], w[:, :], start=False, stop=True,
                                            skip_group_check=True)
                last.then_inc(s["logit_mm"], 1)
                for g in range(GROUPS):
                    for c in range(FC):
                        if g > 0:
                            pe.wait_ge(s["up_done"], FC * (g - 1) + c + 1)
                        nc.tensor.matmul(m.bank[2 + c], sw1[:, c * P:(c + 1) * P], x["hT"][:, g, :], start=True, stop=True).then_inc(s["up_mm"], 1)
                count_earlier(nc, pe, r, small, s)
                nc.tensor.matmul(m.bank[1][:, 0:E1], r["ones"][:, :], r["before"][:, BATCH, :], start=True, stop=True).then_inc(s["tiles_mm"], 1)
                pe.wait_ge(s["comb_done"], 1)
                for g in range(GROUPS):
                    if g >= 2:
                        pe.wait_ge(s["combT_done"], g - 1)
                    for j in range(GS):
                        last = nc.tensor.transpose(bank4[4 + g % 2][0:E1, j, :], comb[:, GS * g + j, :], m.ident)
                    last.then_inc(s["combT_mm"], 1)
                    pe.wait_ge(s["combT_done"], g + 1)
                    if g > 0:
                        pe.wait_ge(s["down_done"], g)
                    for j in range(GS):
                        last = nc.tensor.matmul(bank4[6][:, j, :], combT[:, g, j * P:(j + 1) * P], eb2[:, :], start=True, stop=True)
                    last.then_inc(s["bias_mm"], 1)
                    pe.wait_ge(s["up_done"], FC * (g + 1))
                    for j in range(GS):
                        nc.tensor.matmul(bank4[7][:, j, :], m.ones_row[0:1, 0:P], sb2[:, :], start=True, stop=False)
                        for c in range(FC):
                            last = nc.tensor.matmul(bank4[7][:, j, :], up[:, g, c, j * P:(j + 1) * P], sw2[:, c, :], start=False,
                                                    stop=(c == FC - 1))
                    last.then_inc(s["down_mm"], 1)
    close_semaphores(nc, s)


def mixture1_expert_stage(nc, io, m, x):
    FC = FF1 // P
    LOADS = 4
    HT = SLOT_TILE // P
    DOWN_CREDIT = 2
    s = open_semaphores(nc, SET_SEMS + "xT_mm xT_done up_mm up_done down_mm down_done")
    loaded, stored = [s["in%d" % k] for k in range(SETS)], [s["stored%d" % k] for k in range(SETS)]
    with ExitStack() as mem:
        def sb(name, shape, dt=FP32):
            return mem.enter_context(nc.sbuf_tensor(name, shape, dt))
        xs = sb("e1_x", [P, SETS, HT, D])
        w1 = sb("e1_w1", [P, SETS, FF1])
        b1 = sb("e1_b1", [P, SETS, FC])
        w2 = sb("e1_w2", [P, SETS, FC, D])
        xT = sb("e1_xT", [P, SETS, SLOT_TILE])
        up = sb("e1_up", [P, 2, FC, SLOT_TILE])
        ys = sb("e1_y", [P, SETS, HT, D])
        rows_in = io["slots1_x"].rearrange("(t j p) d -> t p j d", j=HT, p=P)
        rows_out = io["slots1_y"].rearrange("(t j p) d -> t p j d", j=HT, p=P)
        xT_ps = [m.bank[u][:, 0:SLOT_TILE].rearrange("p (j c) -> p j c", j=HT) for u in range(2)]
        up_ps = [m.bank[2 + c][:, 0:SLOT_TILE] for c in range(FC)]
        down_ps = [m.bank[6 + u][:, 0:SLOT_TILE].rearrange("p (j c) -> p j c", j=HT) for u in range(2)]
        with nc.Block() as block:
            @block.sync
            def _(sp):
                def load(t, k):
                    e = sp.value_load(x["tile_expert"][0:1, ds(t, 1)], min_val=0, max_val=E1 - 1)
                    sp.dma_start(xs[:, k], rows_in[ds(t, 1)].rearrange("o p j d -> p (o j) d")).then_inc(loaded[k], 16)
                    sp.dma_start(w1[:, k], io["L0_ffn_ew1"][ds(e, 1)].rearrange("o p f -> p (o f)")).then_inc(loaded[k], 16)
                    sp.dma_start(b1[:, k], io["L0_ffn_eb1"][ds(e, 1)].rearrange("o p f -> p (o f)")).then_inc(loaded[k], 16)
                    sp.dma_start(w2[:, k], io["L0_ffn_ew2"][ds(e, 1)].rearrange("o p c d -> p (o c) d")).then_inc(loaded[k], 16)

                def store(t, k):
                    sp.wait_ge(s["down_done"], t + (DOWN_CREDIT + 1))
                    sp.dma_start(rows_out[ds(t, 1)].rearrange("o p j d -> p (o j) d"), ys[:, k]).then_inc(stored[k], 16)

                sp.wait_ge(m.scattered1, 16 * 2 * BATCH)
                for k in range(SETS):
                    sp.sem_inc(stored[k], 16)
                    load(k, k)
                with sp.Fori(0, TILES1 // SETS - 1) as i:
                    for k in range(SETS):
                        sp.wait_ge(s["down_mm"], i * SETS + (k + 1))
                        load(i * SETS + (k + SETS), k)
                        store(i * SETS + k, k)
                for k in range(SETS):
                    store(TILES1 - SETS + k, k)
                for k in range(SETS):
                    sp.wait_ge(stored[k], 16 * (TILES1 // SETS + 1))

            @block.scalar
            def _(act):
                def act_up(t, u):
                    for c in range(FC):
                        act.wait_ge(s["up_mm"], t * FC + (c + 1))
                        nc.scalar.activation(up[:, u % 2, c, :], up_ps[c], ACT.Silu, bias=b1[:, u, c:c + 1]).then_inc(s["up_done"], 1)

                with act.Fori(0, TILES1 // SETS) as i:
                    for u in range(SETS):
                        act_up(i * SETS + u, u)

            @block.vector
            def _(dve):
                def turn(t, k):
                    dve.wait_ge(s["xT_mm"], t + 1)
                    nc.vector.tensor_scalar(xT[:, k, :].rearrange("p (j c) -> p j c", j=HT), xT_ps[k % 2], x["gb"][:, 0:1], x["gb"][:, 1:2],
                                            ALU.mult, ALU.add).then_inc(s["xT_done"], 1)

                def result(t, i, k):
                    dve.wait_ge(stored[k], i * 16 + 16)
                    dve.wait_ge(s["down_mm"], t + 1)
                    nc.vector.tensor_copy(ys[:, k], down_ps[k % 2]).then_inc(s["down_done"], 1)

                dve.sem_inc(s["down_done"], DOWN_CREDIT)
                turn(0, 0)
                turn(1, 1)
                turn(2, 2)
                with dve.Fori(0, TILES1 // SETS - 1) as i:
                    for u in range(SETS):
                        turn(i * SETS + (u + 3), (u + 3) % SETS)
                        result(i * SETS + u, i, u)
                for u in range(SETS):
                    if u + 3 < SETS:
                        turn(TILES1 - SETS + u + 3, u + 3)
                    result(TILES1 - SETS + u, TILES1 // SETS - 1, u)

            @block.tensor
            def _(pe):
                pe.sem_inc(s["up_done"], FC)

                def turn(t, i, k):
                    pe.wait_ge(loaded[k], i * (16 * LOADS) + 16 * LOADS)
                    for j in range(HT):
                        last = nc.tensor.transpose(xT_ps[k % 2][:, j, :], xs[:, k, j, :], m.ident)
                    last.then_inc(s["xT_mm"], 1)

                def expand(t, k):
                    pe.wait_ge(s["xT_done"], t + 1)
                    for c in range(FC):
                        pe.wait_ge(s["up_done"], t * FC + (c + 1))
                        nc.tensor.matmul(up_ps[c], w1[:, k, c * P:(c + 1) * P], xT[:, k, :], start=True, stop=True).then_inc(s["up_mm"], 1)

                def contract(t, k):
                    pe.wait_ge(s["up_done"], t * FC + 2 * FC)
                    pe.wait_ge(s["down_done"], t + 1)
                    for j in range(HT):
                        for c in range(FC):
                            last = nc.tensor.matmul(down_ps[k % 2][:, j, :], up[:, k % 2, c, j * P:(j + 1) * P], w2[:, k, c, :], start=(c == 0),
                                                    stop=(c == FC - 1))
                    last.then_inc(s["down_mm"], 1)

                turn(0, 0, 0)
                turn(1, 0, 1)
                expand(0, 0)
                with pe.Fori(0, TILES1 // SETS - 1) as i:
                    for u in range(SETS):
                        turn(i * SETS + (u + 2), i + (u + 2) // SETS, (u + 2) % SETS)
                        expand(i * SETS + (u + 1), (u + 1) % SETS)
                        contract(i * SETS + u, u)
                for u in range(SETS):
                    t = TILES1 - SETS + u
                    if t + 2 < TILES1:
                        turn(t + 2, TILES1 // SETS - 1, u + 2)
                    if t + 1 < TILES1:
                        expand(t + 1, u + 1)
                    contract(t, u)
    close_semaphores(nc, s)


def mixture1_stage(nc, io, m):
    with ExitStack() as mem:
        def sb(name, shape, dt=FP32):
            return mem.enter_context(nc.sbuf_tensor(name, shape, dt))
        x = dict(x1=sb("x1", [P, BATCH, D]), xh=sb("x1h", [P, BATCH, D]), hT=sb("x1T", [P, GROUPS, GT]), gb=sb("x1_gb", [P, 2]),
                            slots=sb("slots1", [P, 2, BATCH], U32), weights=sb("weights1", [P, 2, BATCH]),
                            tile_expert=sb("tile_expert", [1, TILES1], mybir.dt.int32), moe=sb("moe1", [P, BATCH, D]))
        mixture1_norm_stage(nc, io, m, x)
        mixture1_route_stage(nc, io, m, x)
        mixture1_expert_stage(nc, io, m, x)
        combine_stage(nc, io, m, "c1", io["slots1_y"], x["slots"], x["weights"], x["moe"], m.gathered1)
        ffn_stage(nc, io, m, "f1", dict(ln_g=io["L0_ffn_ff_ln_g"], ln_b=io["L0_ffn_ff_ln_b"], w1=io["L0_ffn_ff_w1"], b1=io["L0_ffn_ff_b1"],
                                                   w2=io["L0_ffn_ff_w2"], b2=io["L0_ffn_ff_b2"]), x["moe"], m.h, ACT.Silu, (x["x1"], x["moe"]))


E2, H2 = 64, 64
CAP = SLOT_TILE


def mixture2_route_stage(nc, io, m, x):
    s = open_semaphores(nc, NORM_SEMS + ROUTE_SEMS + "w_in logit_mm scores_done sum_done eps_done rz_done norm_done over_done capped_done "
                            "valid_done slot_base slot_done shift_done weight_done up_mm silu_done gated_done down_mm down_done")
    with ExitStack() as mem:
        def sb(name, shape, dt=FP32):
            return mem.enter_context(nc.sbuf_tensor(name, shape, dt))
        n = norm_buffers(sb, "n2")
        n["xh"] = x["xh"][:, :, :].rearrange("p (g j) d -> p g j d", g=GROUPS)
        r = routing_buffers(sb, "r2", E2)
        hT = sb("r2_hT", [P, GROUPS, GT])
        w = sb("r2_w", [P, E2])
        sw1, sw3, sw2 = sb("r2_sw1", [P, P]), sb("r2_sw3", [P, P]), sb("r2_sw2", [P, D])
        zs = sb("r2_zs", [P, BATCH])
        top = sb("r2_tops", [P, 2, BATCH])
        capped, over, valid, slotf = (sb("r2_" + k, [P, 2, BATCH]) for k in ("capped", "over", "valid", "slotf"))
        act1, gated = sb("r2_act1", [P, 2, GT]), sb("r2_gated", [P, 2, GT])
        bank4 = [k.rearrange("p (j c) -> p j c", j=GS) for k in m.bank]
        wide = m.psum[:, 0:2, :].rearrange("p a (b e) -> p (a b) e", e=E2)
        with nc.Block() as block:
            @block.sync
            def _(sp):
                for dst, src in [(w[:, :], io["L1_ffn_gate_w"]), (sw1[:, :], io["L1_ffn_sw1"]), (sw3[:, :], io["L1_ffn_sw3"]), (sw2[:, :], io["L1_ffn_sw2"]),
                                 (r["iota"][:, :], io["iota"][:, 0:E2]), (r["earlier"][:, :], io["earlier"])]:
                    sp.dma_start(dst, src).then_inc(s["w_in"], 16)

            @block.gpsimd
            def _(pool):
                nc.gpsimd.memset(r["ones"][:, :], 1.0).then_inc(s["w_in"], 16)
                norm_pool(nc, pool, n, m, s, 0)
                pool.wait_ge(s["slot_done"], 2)
                scatter_rows(nc, pool, lambda b: x["xh"][:, b, :], x["targets"], io["slots2_x"], E2 * CAP - 1, m.scattered2)

            @block.scalar
            def _(act):
                act.wait_ge(s["w_in"], 112)
                norm_scale(nc, act, lambda g: hT[:, g, :], lambda g: m.bank[4 + g], None, s, 0)
                act.wait_ge(s["logit_mm"], 1)
                nc.scalar.activation(r["scores"][:, :, :], wide, ACT.Sigmoid).then_inc(s["scores_done"], 1)
                for g in range(GROUPS):
                    act.wait_ge(s["up_mm"], g + 1)
                    if g >= 2:
                        act.wait_ge(s["gated_done"], g - 1)
                    nc.scalar.activation(act1[:, g % 2, :], m.bank[2], ACT.Silu).then_inc(s["silu_done"], 1)

            @block.vector
            def _(dve):
                dve.wait_ge(s["w_in"], 112)
                norm_vector(nc, dve, lambda g: m.h[:, GS * g:GS * (g + 1), :], n, s, 0)
                dve.wait_ge(s["xh_done"], GROUPS)
                dve.wait_ge(s["scores_done"], 1)
                choose_two(nc, dve, r, s)
                nc.vector.tensor_copy(top[:, :, :], r["top"][:, :, 0:2].rearrange("p n k -> p k n")).then_inc(s["norm_done"], 1)
                dve.wait_ge(s["norm_done"], 1)
                nc.vector.tensor_tensor(zs[:, :], top[:, 0, :], top[:, 1, :], ALU.add).then_inc(s["sum_done"], 1)
                dve.wait_ge(s["sum_done"], 1)
                nc.vector.tensor_scalar(zs[:, :], zs[:, :], 1e-20, None, ALU.add).then_inc(s["eps_done"], 1)
                dve.wait_ge(s["eps_done"], 1)
                nc.vector.reciprocal(zs[:, :], zs[:, :]).then_inc(s["rz_done"], 1)
                dve.wait_ge(s["rz_done"], 1)
                nc.vector.tensor_tensor(top[:, :, :], top[:, :, :], zs[:, :].unsqueeze(1).to_broadcast([P, 2, BATCH]),
                                        ALU.mult).then_inc(s["norm_done"], 1)
                dve.wait_ge(s["count_mm"], 1)
                pick(nc, dve, r, wide, s, 0)
                nc.vector.tensor_scalar(valid[:, :, :], r["pos"][:, :, :], float(CAP), 2.5, ALU.is_lt, ALU.mult).then_inc(s["valid_done"], 1)
                nc.vector.tensor_scalar(over[:, :, :], r["pos"][:, :, :], float(CAP), float(2 * E2 * CAP), ALU.is_ge, ALU.mult).then_inc(s["over_done"], 1)
                nc.vector.tensor_scalar(capped[:, :, :], r["pos"][:, :, :], float(CAP - 1), None, ALU.min).then_inc(s["capped_done"], 1)
                dve.wait_ge(s["capped_done"], 1)
                dve.wait_ge(s["norm_done"], 2)
                nc.vector.tensor_tensor(x["weights"][:, :, :], top[:, :, :], valid[:, :, :], ALU.mult).then_inc(s["weight_done"], 1)
                nc.vector.scalar_tensor_tensor(out=slotf[:, :, :], in0=r["indexf"][:, :, :], scalar=float(CAP), in1=capped[:, :, :], op0=ALU.mult,
                                               op1=ALU.add).then_inc(s["slot_base"], 1)
                dve.wait_ge(s["slot_base"], 1)
                nc.vector.tensor_copy(x["slots"][:, :, :], slotf[:, :, :]).then_inc(s["slot_done"], 1)
                nc.vector.tensor_tensor(over[:, :, :], over[:, :, :], slotf[:, :, :], ALU.add).then_inc(s["shift_done"], 1)
                dve.wait_ge(s["shift_done"], 1)
                nc.vector.tensor_copy(x["targets"][:, :, :], over[:, :, :]).then_inc(s["slot_done"], 1)
                for g in range(GROUPS):
                    dve.wait_ge(s["silu_done"], g + 1)
                    if g >= 2:
                        dve.wait_ge(s["down_mm"], g - 1)
                    nc.vector.tensor_tensor(gated[:, g % 2, :], act1[:, g % 2, :], m.bank[3], ALU.mult).then_inc(s["gated_done"], 1)
                for g in range(GROUPS):
                    dve.wait_ge(s["down_mm"], g + 1)
                    nc.vector.tensor_tensor(m.h[:, GS * g:GS * (g + 1), :], m.h[:, GS * g:GS * (g + 1), :], bank4[4 + g],
                                            ALU.add).then_inc(s["down_done"], 1)
                dve.wait_ge(s["down_done"], GROUPS)
                dve.wait_ge(s["slot_done"], 2)
                dve.wait_ge(s["weight_done"], 1)

            @block.tensor
            def _(pe):
                pe.wait_ge(s["w_in"], 112)
                norm_transpose(nc, pe, lambda g: bank4[4 + g], n, m, s, 0)
                for t in range(BATCH):
                    pe.wait_ge(s["xT_done"], t // GS + 1)
                    last = nc.tensor.matmul(wide[:, t, :], hT[:, t // GS, t % GS * P:(t % GS + 1) * P], w[:, :], start=True, stop=True)
                last.then_inc(s["logit_mm"], 1)
                pe.wait_ge(s["scores_done"], 1)
                count_earlier(nc, pe, r, wide, s)
                for g in range(GROUPS):
                    if g > 0:
                        pe.wait_ge(s["gated_done"], g)
                    nc.tensor.matmul(m.bank[2], sw1[:, :], hT[:, g, :], start=True, stop=True)
                    nc.tensor.matmul(m.bank[3], sw3[:, :], hT[:, g, :], start=True, stop=True).then_inc(s["up_mm"], 1)
                    if g > 0:
                        for j in range(GS):
                            last = nc.tensor.matmul(bank4[4 + g - 1][:, j, :], gated[:, (g - 1) % 2, j * P:(j + 1) * P], sw2[:, :], start=True,
                                                    stop=True)
                        last.then_inc(s["down_mm"], 1)
                pe.wait_ge(s["gated_done"], GROUPS)
                for j in range(GS):
                    last = nc.tensor.matmul(bank4[4 + GROUPS - 1][:, j, :], gated[:, (GROUPS - 1) % 2, j * P:(j + 1) * P], sw2[:, :], start=True,
                                            stop=True)
                last.then_inc(s["down_mm"], 1)
    close_semaphores(nc, s)


def mixture2_expert_stage(nc, io, m, x):
    LOADS = 2
    DOWN_CREDIT = 2
    HT = SLOT_TILE // P
    s = open_semaphores(nc, SET_SEMS + "xT_mm xT_done up_mm silu_done gated_done down_mm down_done")
    loaded, stored = [s["in%d" % k] for k in range(SETS)], [s["stored%d" % k] for k in range(SETS)]
    with ExitStack() as mem:
        def sb(name, shape, dt=FP32):
            return mem.enter_context(nc.sbuf_tensor(name, shape, dt))
        xs = sb("e2_x", [P, SETS, HT, D])
        ws = sb("e2_w", [P, SETS, 2 * H2 + D])
        xT = sb("e2_xT", [P, SETS, SLOT_TILE])
        act1 = sb("e2_act1", [H2, 2, SLOT_TILE])
        gated = sb("e2_gated", [H2, 2, SLOT_TILE])
        ys = sb("e2_y", [P, SETS, HT, D])
        rows_in = io["slots2_x"].rearrange("(t j p) d -> t p j d", j=HT, p=P)
        rows_out = io["slots2_y"].rearrange("(t j p) d -> t p j d", j=HT, p=P)
        xT_ps = [m.bank[u][:, 0:SLOT_TILE].rearrange("p (j c) -> p j c", j=HT) for u in range(2)]
        up_ps = [m.bank[2 + u][0:H2, :].rearrange("p (k c) -> p k c", k=2) for u in range(2)]
        down_ps = [m.bank[4 + u][:, 0:SLOT_TILE].rearrange("p (j c) -> p j c", j=HT) for u in range(2)]
        with nc.Block() as block:
            @block.sync
            def _(sp):
                def load(e, k):
                    sp.dma_start(xs[:, k], rows_in[ds(e, 1)].rearrange("o p j d -> p (o j) d")).then_inc(loaded[k], 16)
                    sp.dma_start(ws[:, k], io["L1_ffn_w132"][ds(e, 1)].rearrange("o p f -> p (o f)")).then_inc(loaded[k], 16)

                def store(e, k):
                    sp.wait_ge(s["down_done"], e + (DOWN_CREDIT + 1))
                    sp.dma_start(rows_out[ds(e, 1)].rearrange("o p j d -> p (o j) d"), ys[:, k]).then_inc(stored[k], 16)

                sp.wait_ge(m.scattered2, 16 * 2 * BATCH)
                for k in range(SETS):
                    sp.sem_inc(stored[k], 16)
                    load(k, k)
                with sp.Fori(0, E2 // SETS - 1) as i:
                    for k in range(SETS):
                        sp.wait_ge(s["down_mm"], i * SETS + (k + 1))
                        load(i * SETS + (k + SETS), k)
                        store(i * SETS + k, k)
                for k in range(SETS):
                    store(E2 - SETS + k, k)
                for k in range(SETS):
                    sp.wait_ge(stored[k], 16 * (E2 // SETS + 1))

            @block.scalar
            def _(act):
                with act.Fori(0, E2 // 2) as i:
                    for u in range(2):
                        act.wait_ge(s["up_mm"], i * 2 + (u + 1))
                        nc.scalar.activation(act1[:, u, :], up_ps[u][:, 0, :], ACT.Silu).then_inc(s["silu_done"], 1)

            @block.vector
            def _(dve):
                def turn(e, k):
                    dve.wait_ge(s["xT_mm"], e + 1)
                    nc.vector.tensor_copy(xT[:, k, :].rearrange("p (j c) -> p j c", j=HT), xT_ps[k % 2]).then_inc(s["xT_done"], 1)

                def gate(e, k):
                    dve.wait_ge(s["silu_done"], e + 1)
                    nc.vector.tensor_tensor(gated[:, k % 2, :], act1[:, k % 2, :], up_ps[k % 2][:, 1, :], ALU.mult).then_inc(s["gated_done"], 1)

                def result(e, i, k):
                    dve.wait_ge(stored[k], i * 16 + 16)
                    dve.wait_ge(s["down_mm"], e + 1)
                    nc.vector.tensor_copy(ys[:, k], down_ps[k % 2]).then_inc(s["down_done"], 1)

                dve.sem_inc(s["down_done"], DOWN_CREDIT)
                turn(0, 0)
                turn(1, 1)
                turn(2, 2)
                gate(0, 0)
                with dve.Fori(0, E2 // SETS - 1) as i:
                    for u in range(SETS):
                        turn(i * SETS + (u + 3), (u + 3) % SETS)
                        gate(i * SETS + (u + 1), (u + 1) % SETS)
                        result(i * SETS + u, i, u)
                for u in range(SETS):
                    if u + 3 < SETS:
                        turn(E2 - SETS + u + 3, u + 3)
                    if u < SETS - 1:
                        gate(E2 - SETS + u + 1, u + 1)
                    result(E2 - SETS + u, E2 // SETS - 1, u)

            @block.tensor
            def _(pe):
                def turn(i, k):
                    pe.wait_ge(loaded[k], i * (16 * LOADS) + 16 * LOADS)
                    for j in range(HT):
                        last = nc.tensor.transpose(xT_ps[k % 2][:, j, :], xs[:, k, j, :], m.ident)
                    last.then_inc(s["xT_mm"], 1)

                def expand(e, k):
                    pe.wait_ge(s["xT_done"], e + 1)
                    for n in range(2):
                        last = nc.tensor.matmul(up_ps[k % 2][:, n, :], ws[:, k, n * H2:(n + 1) * H2], xT[:, k, :], start=True, stop=True)
                    last.then_inc(s["up_mm"], 1)

                def contract(e, k):
                    pe.wait_ge(s["gated_done"], e + 1)
                    pe.wait_ge(s["down_done"], e + 1)
                    for j in range(HT):
                        last = nc.tensor.matmul(down_ps[k % 2][:, j, :], gated[:, k % 2, j * P:(j + 1) * P], ws[0:H2, k, 2 * H2:], start=True, stop=True)
                    last.then_inc(s["down_mm"], 1)

                turn(0, 0)
                turn(0, 1)
                expand(0, 0)
                with pe.Fori(0, E2 // SETS - 1) as i:
                    for u in range(SETS):
                        turn(i + (u + 2) // SETS, (u + 2) % SETS)
                        expand(i * SETS + (u + 1), (u + 1) % SETS)
                        contract(i * SETS + u, u)
                for u in range(SETS):
                    if u + 2 < SETS:
                        turn(E2 // SETS - 1, u + 2)
                    if u + 1 < SETS:
                        expand(E2 - SETS + u + 1, u + 1)
                    contract(E2 - SETS + u, u)
    close_semaphores(nc, s)


def mixture2_stage(nc, io, m):
    with ExitStack() as mem:
        def sb(name, shape, dt=FP32):
            return mem.enter_context(nc.sbuf_tensor(name, shape, dt))
        x = dict(xh=sb("x2h", [P, BATCH, D]), slots=sb("slots2", [P, 2, BATCH], U32), targets=sb("targets2", [P, 2, BATCH], U32),
                            weights=sb("weights2", [P, 2, BATCH]))
        mixture2_route_stage(nc, io, m, x)
        mixture2_expert_stage(nc, io, m, x)
        combine_stage(nc, io, m, "c2", io["slots2_y"], x["slots"], x["weights"], m.h, m.gathered2)


def clear_slots_stage(nc, io, m):
    m.slots_zeroed = nc.alloc_semaphore("slots_zeroed")
    s = open_semaphores(nc, "zeros_made")
    zeros = m.zeros
    with nc.Block() as block:
        @block.gpsimd
        def _(pool):
            nc.gpsimd.memset(zeros[:, :], 0.0).then_inc(s["zeros_made"], 1)

        @block.sync
        def _(sp):
            sp.wait_ge(s["zeros_made"], 1)
            count = 0
            per = zeros.shape[1] // D * P
            for buffer in (io["slots1_x"], io["slots2_x"]):
                for k in range(buffer.shape[0] // per):
                    sp.dma_start(buffer[k * per:(k + 1) * per, :].rearrange("(p r) d -> p (r d)", p=P), zeros[:, :]).then_inc(m.slots_zeroed, 16)
                    count += 16
            m.slots_zeroed_count = count
    close_semaphores(nc, s)



def setup_stage(nc, io, m):
    s = open_semaphores(nc, "zero_done const_done")
    with nc.Block() as block:
        @block.gpsimd
        def _(pool):
            nc.gpsimd.memset(m.ident_t[:, :], 0.0).then_inc(s["zero_done"], 1)
            nc.gpsimd.memset(m.ones_row[:, :], 1.0)
            nc.gpsimd.memset(m.ones_col[:, :], 1.0)
            nc.gpsimd.memset(m.neg_half[:, :], -0.5)
            pool.wait_ge(s["zero_done"], 1)
            nc.gpsimd.affine_select(out=m.ident_t[:, :], in_=m.ident_t[:, :], compare_op=ALU.not_equal, fill=1.0,
                                    base=0, pattern=[[-1, P]], channel_multiplier=1).then_inc(s["const_done"], 1)
            pool.wait_ge(s["const_done"], 1)
    close_semaphores(nc, s)


def store_stage(nc, io, m):
    s = open_semaphores(nc, "stored")
    with nc.Block() as block:
        @block.sync
        def _(sp):
            sp.dma_start(io["out"].rearrange("b t d -> t b d"), m.h[:, :, :]).then_inc(s["stored"], 16)
            sp.wait_ge(s["stored"], 16)
    close_semaphores(nc, s)


def program(nc, io):
    with ExitStack() as mem:
        m = Model()
        m.psum = mem.enter_context(nc.psum_tensor("psum", [P, 8, 512], FP32))
        m.bank = [m.psum[:, i, :] for i in range(8)]
        m.ident_t = mem.enter_context(nc.sbuf_tensor("ident", [P, P], FP32))
        m.ident = m.ident_t[:, :]
        m.ones_row = mem.enter_context(nc.sbuf_tensor("ones_row", [1, 512], FP32))
        m.ones_col = mem.enter_context(nc.sbuf_tensor("ones_col", [P, 1], FP32))
        m.neg_half = mem.enter_context(nc.sbuf_tensor("neg_half", [P, 64], FP32))
        m.h = mem.enter_context(nc.sbuf_tensor("h", [P, BATCH, D], FP32))
        m.zeros = mem.enter_context(nc.sbuf_tensor("zeros", [P, 16 * D], FP32))
        m.front_loaded, m.back_loaded = nc.alloc_semaphore("front_loaded"), nc.alloc_semaphore("back_loaded")
        m.embedded = nc.alloc_semaphore("embedded")
        m.scattered1, m.gathered1 = nc.alloc_semaphore("scattered1"), [nc.alloc_semaphore("gathered1_%d" % k) for k in range(2)]
        m.scattered2, m.gathered2 = nc.alloc_semaphore("scattered2"), [nc.alloc_semaphore("gathered2_%d" % k) for k in range(2)]
        setup_stage(nc, io, m)
        clear_slots_stage(nc, io, m)
        for stage in (token_stage, attention_stage, mixture1_stage, recurrent_stage, mixture2_stage):
            stage(nc, io, m)
        store_stage(nc, io, m)


def column(a):
    a = np.asarray(a)
    return a.reshape(-1, 1) if a.size <= P else a.reshape(-1, P).T


def rows(a):
    a = np.asarray(a)
    return a.reshape(-1, P, a.shape[-1]).transpose(1, 0, 2)


def layouts(i):
    o = {}
    pos = np.arange(P, dtype=np.float32)[:, None]
    div = np.exp(np.arange(0, D, 2, dtype=np.float32) * np.float32(-np.log(10000.0) / D))
    pe = np.zeros((P, D), np.float32)
    pe[:, 0::2] = np.sin(pos * div)
    pe[:, 1::2] = np.cos(pos * div)
    o["pe_table"] = pe
    o["x_t"] = i["x"].T
    for n in ("E", "Wq", "Wk", "Wv"):
        o["L0_tok_" + n] = i["L0_tok_" + n]
    o["L0_tok_bq"] = column(i["L0_tok_bq"])
    o["L0_tok_bk"] = column(i["L0_tok_bk"])
    o["L0_tok_bv"] = np.broadcast_to(i["L0_tok_bv"], (P, 16))
    o["L0_tok_Wo"] = i["L0_tok_Wo"].reshape(8, 16, D).transpose(1, 0, 2)
    o["L0_tok_bo"] = i["L0_tok_bo"].reshape(1, D)
    o["L0_tok_ln_g"] = column(i["L0_tok_ln_g"])
    o["L0_tok_ln_b"] = column(i["L0_tok_ln_b"])
    o["L0_tok_W1"] = rows(i["L0_tok_W1"].T)
    o["L0_tok_W2"] = rows(i["L0_tok_W2"])
    o["L0_tok_b1"] = column(i["L0_tok_b1"])
    o["L0_tok_b2"] = i["L0_tok_b2"].reshape(1, D)
    o["L0_attn_ip_w"] = i["L0_attn_ip_w"].T
    for n in ("ip_b", "ff_b2"):
        o["L0_attn_" + n] = i["L0_attn_" + n].reshape(1, D)
    for n in ("ff_ln_g", "ff_ln_b", "ff_b1"):
        o["L0_attn_" + n] = column(i["L0_attn_" + n])
    o["L0_attn_ff_w1"] = i["L0_attn_ff_w1"].T
    o["L0_attn_ff_w2"] = rows(i["L0_attn_ff_w2"].T)
    o["L0_attn_fw_ln_g"] = i["L0_attn_fw_ln_g"][:, :, None]
    o["L0_attn_fw_ln_b"] = i["L0_attn_fw_ln_b"][:, :, None]
    slow = i["L0_attn_fw_slow_w"].reshape(2, 8, 193, D)
    o["fw_qkv"] = np.stack([slow[:, :, 64 * n:64 * n + 64].reshape(2, 512, D) for n in range(3)], 1).transpose(0, 3, 1, 2)
    o["fw_beta"] = slow[:, :, 192].transpose(0, 2, 1)
    o["fw_out"] = i["L0_attn_fw_out_w"].transpose(0, 2, 1).reshape(2, 4, P, D).transpose(0, 2, 1, 3)
    o["fw_masks"] = fast_weight_masks()
    for n in ("in_proj_w", "x_proj_w", "dt_proj_w", "out_proj_w"):
        o["L1_attn_" + n] = i["L1_attn_" + n].transpose(0, 2, 1)
    o["L1_attn_x_proj_w"] = o["L1_attn_x_proj_w"].reshape(3, 2, P, 64).transpose(0, 2, 1, 3)
    o["L1_attn_out_proj_w"] = o["L1_attn_out_proj_w"].reshape(3, 2, P, D).transpose(0, 2, 1, 3)
    o["L1_attn_conv_w"] = i["L1_attn_conv_w"].reshape(3, 2, P, 4).transpose(0, 2, 1, 3)
    o["L1_attn_A_log"] = i["L1_attn_A_log"].reshape(3, 2, P, 16).transpose(0, 2, 1, 3)
    for n in ("conv_b", "dt_proj_b", "D_param"):
        o["L1_attn_" + n] = i["L1_attn_" + n].reshape(3, 2, P).transpose(0, 2, 1)
    for n in ("ln_g", "ln_b"):
        o["L1_attn_" + n] = i["L1_attn_" + n][:, :, None]
    o["lstm_w_ih"] = i["L1_attn_lstm_w_ih"].transpose(2, 0, 1)
    whh = np.zeros((P, 4, P), np.float32)
    for d in range(2):
        whh[64 * d:64 * d + 64, :, 64 * d:64 * d + 64] = i["L1_attn_lstm_w_hh"][d].reshape(4, 64, 64).transpose(2, 0, 1)
    o["lstm_w_hh"] = whh
    o["lstm_bias"] = np.stack([i["L1_attn_lstm_b_ih"], i["L1_attn_lstm_b_hh"]]).reshape(2, 2, 4, 64).transpose(1, 3, 0, 2).reshape(P, 2, 4)
    o["L1_attn_fusion_w"] = rows(i["L1_attn_fusion_w"].T)
    o["L1_attn_fusion_b"] = i["L1_attn_fusion_b"].reshape(1, D)
    for n in ("ln_in_g", "ln_in_b", "sb1", "ff_ln_g", "ff_ln_b", "ff_b1"):
        o["L0_ffn_" + n] = column(i["L0_ffn_" + n])
    for n in ("router_w", "ew1", "eb2", "sw1", "ff_w1"):
        o["L0_ffn_" + n] = i["L0_ffn_" + n]
    for n in ("router_b", "sb2", "ff_b2"):
        o["L0_ffn_" + n] = i["L0_ffn_" + n].reshape(1, -1)
    for n in ("sw2", "ff_w2"):
        o["L0_ffn_" + n] = rows(i["L0_ffn_" + n])
    o["L0_ffn_eb1"] = i["L0_ffn_eb1"].reshape(16, 4, P).transpose(0, 2, 1)
    o["L0_ffn_ew2"] = i["L0_ffn_ew2"].reshape(16, 4, P, D).transpose(0, 2, 1, 3)
    o["L1_ffn_gate_w"] = i["L1_ffn_gate_w"].T
    w132 = np.zeros((E2, P, 2 * H2 + D), np.float32)
    w132[:, :, 0:H2], w132[:, :, H2:2 * H2], w132[:, 0:H2, 2 * H2:] = i["L1_ffn_w1"], i["L1_ffn_w3"], i["L1_ffn_w2"]
    o["L1_ffn_w132"] = w132
    for n in ("sw1", "sw3", "sw2"):
        o["L1_ffn_" + n] = i["L1_ffn_" + n]
    o["iota"] = np.broadcast_to(np.arange(64, dtype=np.float32), (P, 64))
    o["earlier"] = (np.arange(P)[:, None] < np.arange(P)[None, :]).astype(np.float32)
    o["selector"] = (np.arange(96)[:, None] % 32 == np.arange(32)[None, :]).astype(np.float32)
    return o


def fast_weight_masks():
    t, u = np.arange(P)[:, None], np.arange(P)[None, :]

    def level(l):
        z = 1 << l
        return (t // (2 * z) == u // (2 * z)) & (t // z % 2 == 1) & (u // z % 2 == 0)
    below = [-1 * level(0), -1 * (t < u), level(0).T | (t == u), t // 32 > u // 32, t <= u]
    return np.stack(below + [level(l) | (t == u) for l in range(1, 5)], 1).astype(np.float32)


def kernel(**inputs):
    import concourse.bacc as bacc
    from concourse.bass_utils import run_bass_kernel_spmd

    nc = bacc.Bacc("TRN2", target_bir_lowering=False, num_devices=1)
    arrays, aps = {}, {}
    for name, a in layouts({k: np.asarray(v) for k, v in inputs.items()}).items():
        a = np.ascontiguousarray(a)
        arrays["in_" + name] = a
        aps[name] = nc.dram_tensor("in_" + name, a.shape, mybir.dt.from_np(a.dtype), kind="ExternalInput").ap()
    aps["out"] = nc.dram_tensor("out_0_dram", (BATCH, P, D), FP32, kind="ExternalOutput").ap()
    for name, rows_of in (("slots1_x", TILES1 * SLOT_TILE), ("slots1_y", TILES1 * SLOT_TILE), ("slots2_x", E2 * CAP), ("slots2_y", E2 * CAP)):
        aps[name] = nc.dram_tensor(name, (rows_of, D), FP32, kind="Internal").ap()
    program(nc, aps)
    r = run_bass_kernel_spmd(nc, [arrays], core_ids=[0])
    return r.results[0]["out_0_dram"]
```
